# Optimizing a Trainium2 kernel written in Bass

```python
import numpy as np
import jax
import jax.numpy as jnp

def _softmax(x, axis=-1):
    return jax.nn.softmax(x, axis=axis)

def _gelu(x):
    return jax.nn.gelu(x, approximate=True)

def _silu(x):
    return jax.nn.silu(x)

def _sigmoid(x):
    return jax.nn.sigmoid(x)

def _layernorm(x, axis=-1, eps=1e-05):
    m = jnp.mean(x, axis=axis, keepdims=True)
    v = jnp.var(x, axis=axis, keepdims=True)
    return (x - m) / jnp.sqrt(v + eps)

def _scatter_add(tgt, idx, src, axis=0):
    return tgt.at[idx].add(src)

def _segment_sum(src, seg, n):
    return jax.ops.segment_sum(src, seg, n)
kernel_name = 'mk_adj_ffn_d2_adj_r2_b8756c'

def setup_inputs(seed: int=0):
    np.random.seed(seed)
    _w = jnp.asarray

    def _rec_inputs():
        import jax
        import jax.numpy as jnp
        _gk = jax.random.key(seed)
        x = -0.0003929 + 0.9999 * jax.random.normal(jax.random.fold_in(_gk, 1), (16, 512, 128), jnp.float32)
        _a = jax.random.bernoulli(jax.random.fold_in(_gk, 2), 0.03125, (512, 512))
        _a = jnp.logical_or(_a, jnp.swapaxes(_a, -1, -2))
        _a = jnp.logical_or(_a, jnp.eye(512, dtype=bool))
        _af = _a.astype(jnp.float32)
        _af = _af * jax.random.uniform(jax.random.fold_in(_gk, 3), (512, 512), jnp.float32, 0.05, 0.999963)
        adj = _af
        return (x, adj)
    x, adj = _rec_inputs()

    def _L0_gnn_setup():
        import jax, jax.numpy as jnp
        import numpy as np
        BT, N, D, HEADS, E = (512, 64, 128, 4, 256)
        LRELU_SLOPE = 0.2
        EPS = 1e-08
        key = jax.random.key(seed)
        ks = jax.random.split(key, 8)
        d = D
        return {'H': jax.random.normal(ks[0], (BT, N, d), jnp.float32), 'W_lin': jax.random.normal(ks[1], (d, d), jnp.float32) / np.sqrt(d).astype(np.float32), 'W_val': jax.random.normal(ks[2], (d, d), jnp.float32) / np.sqrt(d).astype(np.float32), 'a': jax.random.normal(ks[3], (HEADS, d // HEADS), jnp.float32), 'W_out': jax.random.normal(ks[4], (d, d), jnp.float32) / np.sqrt(d).astype(np.float32), 'A0': jax.random.uniform(ks[5], (N, N), jnp.float32), 'src': jax.random.randint(ks[6], (E,), 0, N, jnp.int32), 'dst': jax.random.randint(ks[7], (E,), 0, N, jnp.int32)}
    _L0_gnn_all = _L0_gnn_setup()
    _L0_gnn_in = {k: v for k, v in _L0_gnn_all.items() if k in ('W_lin', 'W_val', 'a', 'W_out', 'src', 'dst')}
    del _L0_gnn_all

    def _L0_ffn_setup():
        import jax, jax.numpy as jnp
        import numpy as np
        N_EXPERTS = 8
        TOP_K = 2
        key = jax.random.key(seed)
        ks = jax.random.split(key, 5)
        B, T, C, E, H = (8, 1024, 128, 8, 341)
        scale = 1.0 / np.sqrt(C)
        return {'x': jax.random.normal(ks[0], (B, T, C), dtype=jnp.float32), 'router_w': jax.random.normal(ks[1], (E, C), dtype=jnp.float32) * scale, 'w1': jax.random.normal(ks[2], (E, H, C), dtype=jnp.float32) * scale, 'w2': jax.random.normal(ks[3], (E, C, H), dtype=jnp.float32) * (1.0 / np.sqrt(H)), 'w3': jax.random.normal(ks[4], (E, H, C), dtype=jnp.float32) * scale}
    _L0_ffn_all = _L0_ffn_setup()
    _L0_ffn_in = {k: v for k, v in _L0_ffn_all.items() if k in ('router_w', 'w1', 'w2', 'w3')}
    del _L0_ffn_all

    def _L1_gnn_setup():
        import jax, jax.numpy as jnp
        import numpy as np
        B, N, D, H = (4, 2048, 128, 128)
        key = jax.random.key(seed)
        ks = jax.random.split(key, 10)
        base_features = jax.random.normal(ks[0], (B, N, D), dtype=jnp.float32)
        pc = (jax.random.uniform(ks[1], (N, N)) < 8.0 / N).astype(jnp.float32)
        pc = pc * (1.0 - jnp.eye(N, dtype=jnp.float32))
        neighbor_mask = jnp.clip(pc + pc.T + jnp.eye(N, dtype=jnp.float32), 0.0, 1.0)
        s = 1.0 / np.sqrt(D)
        Wq = jax.random.normal(ks[2], (D, H), dtype=jnp.float32) * s
        Wk = jax.random.normal(ks[3], (D, H), dtype=jnp.float32) * s
        Wv = jax.random.normal(ks[4], (D, H), dtype=jnp.float32) * s
        Wo = jax.random.normal(ks[5], (H, D), dtype=jnp.float32) * (1.0 / np.sqrt(H))
        bq = jnp.zeros((H,), jnp.float32)
        bk = jnp.zeros((H,), jnp.float32)
        bv = jnp.zeros((H,), jnp.float32)
        bo = jnp.zeros((D,), jnp.float32)
        alpha = jnp.asarray(2.0, jnp.float32)
        gamma = jnp.asarray(0.3, jnp.float32)
        return dict(base_features=base_features, neighbor_mask=neighbor_mask, parent_child_mask=pc, Wq=Wq, bq=bq, Wk=Wk, bk=bk, Wv=Wv, bv=bv, Wo=Wo, bo=bo, alpha=alpha, gamma=gamma)
    _L1_gnn_all = _L1_gnn_setup()
    _L1_gnn_in = {k: v for k, v in _L1_gnn_all.items() if k in ('Wq', 'bq', 'Wk', 'bk', 'Wv', 'bv', 'Wo', 'bo', 'alpha', 'gamma')}
    del _L1_gnn_all

    def _L1_ffn_setup():
        import jax, jax.numpy as jnp
        import numpy as np
        B, N, D = (16, 2048, 128)
        NUM_EXPERTS, TOP_K, HEADS = (4, 2, 4)
        N_EDGES = 524288
        LN_EPS = 1e-05

        def _layernorm(x, g, b):
            mu = x.mean(-1, keepdims=True)
            var = ((x - mu) ** 2).mean(-1, keepdims=True)
            return (x - mu) * jax.lax.rsqrt(var + LN_EPS) * g + b

        def _forward(x, edge_index, W_gat, att_src, att_dst, b_gat, ln_gamma, ln_beta, W1, b1, W2, b2):
            Bc, Nc, Dc = x.shape
            M = Bc * Nc
            x_flat = x.reshape(M, Dc)
            h = (x_flat @ W_gat).reshape(M, HEADS, NUM_EXPERTS)
            loops = jnp.arange(M, dtype=edge_index.dtype)
            src = jnp.concatenate([edge_index[0], loops])
            dst = jnp.concatenate([edge_index[1], loops])
            a_src = (h * att_src).sum(-1)
            a_dst = (h * att_dst).sum(-1)
            e = jax.nn.leaky_relu(a_src[src] + a_dst[dst], negative_slope=0.2)
            e_max = jax.ops.segment_max(e, dst, num_segments=M)
            ee = jnp.exp(e - e_max[dst])
            denom = jax.ops.segment_sum(ee, dst, num_segments=M)
            alpha = ee / (denom[dst] + 1e-16)
            msg = h[src] * alpha[:, :, None]
            agg = jax.ops.segment_sum(msg, dst, num_segments=M).reshape(M, HEADS * NUM_EXPERTS) + b_gat
            scores = _layernorm(agg, ln_gamma, ln_beta).reshape(M, HEADS, NUM_EXPERTS).mean(1)
            scores = scores.reshape(Bc, Nc, NUM_EXPERTS)
            topk_s, topk_i = jax.lax.top_k(scores, TOP_K)
            w = jax.nn.softmax(topk_s, axis=-1)
            out = jnp.zeros_like(x)
            for ei in range(NUM_EXPERTS):
                g = jnp.where(topk_i == ei, w, 0.0).sum(-1)
                hh = jax.nn.gelu(x @ W1[ei] + b1[ei], approximate=False)
                out = out + g[..., None] * (hh @ W2[ei] + b2[ei])
            return out
        key = jax.random.key(seed)
        ks = jax.random.split(key, 8)
        s = 0.05
        return {'x': jax.random.normal(ks[0], (B, N, D), jnp.float32), 'W_gat': jax.random.normal(ks[1], (D, HEADS * NUM_EXPERTS), jnp.float32) * s, 'att_src': jax.random.normal(ks[2], (HEADS, NUM_EXPERTS), jnp.float32) * s, 'att_dst': jax.random.normal(ks[3], (HEADS, NUM_EXPERTS), jnp.float32) * s, 'b_gat': jnp.zeros((HEADS * NUM_EXPERTS,), jnp.float32), 'ln_gamma': jnp.ones((HEADS * NUM_EXPERTS,), jnp.float32), 'ln_beta': jnp.zeros((HEADS * NUM_EXPERTS,), jnp.float32), 'W1': jax.random.normal(ks[4], (NUM_EXPERTS, D, 2 * D), jnp.float32) * s, 'b1': jnp.zeros((NUM_EXPERTS, 2 * D), jnp.float32), 'W2': jax.random.normal(ks[5], (NUM_EXPERTS, 2 * D, D), jnp.float32) * s, 'b2': jnp.zeros((NUM_EXPERTS, D), jnp.float32), 'edge_index': jax.random.randint(ks[6], (2, N_EDGES), 0, B * N, jnp.int32)}
    _L1_ffn_all = _L1_ffn_setup()
    _L1_ffn_in = {k: v for k, v in _L1_ffn_all.items() if k in ('W_gat', 'att_src', 'att_dst', 'b_gat', 'ln_gamma', 'ln_beta', 'W1', 'b1', 'W2', 'b2', 'edge_index')}
    del _L1_ffn_all
    return {'x': x, 'adj': adj, 'L0_gnn_W_lin': _L0_gnn_in['W_lin'], 'L0_gnn_W_val': _L0_gnn_in['W_val'], 'L0_gnn_a': _L0_gnn_in['a'], 'L0_gnn_W_out': _L0_gnn_in['W_out'], 'L0_gnn_src': _L0_gnn_in['src'], 'L0_gnn_dst': _L0_gnn_in['dst'], 'L0_ffn_router_w': _L0_ffn_in['router_w'], 'L0_ffn_w1': _L0_ffn_in['w1'], 'L0_ffn_w2': _L0_ffn_in['w2'], 'L0_ffn_w3': _L0_ffn_in['w3'], 'L1_gnn_Wq': _L1_gnn_in['Wq'], 'L1_gnn_bq': _L1_gnn_in['bq'], 'L1_gnn_Wk': _L1_gnn_in['Wk'], 'L1_gnn_bk': _L1_gnn_in['bk'], 'L1_gnn_Wv': _L1_gnn_in['Wv'], 'L1_gnn_bv': _L1_gnn_in['bv'], 'L1_gnn_Wo': _L1_gnn_in['Wo'], 'L1_gnn_bo': _L1_gnn_in['bo'], 'L1_gnn_alpha': _L1_gnn_in['alpha'], 'L1_gnn_gamma': _L1_gnn_in['gamma'], 'L1_ffn_W_gat': _L1_ffn_in['W_gat'], 'L1_ffn_att_src': _L1_ffn_in['att_src'], 'L1_ffn_att_dst': _L1_ffn_in['att_dst'], 'L1_ffn_b_gat': _L1_ffn_in['b_gat'], 'L1_ffn_ln_gamma': _L1_ffn_in['ln_gamma'], 'L1_ffn_ln_beta': _L1_ffn_in['ln_beta'], 'L1_ffn_W1': _L1_ffn_in['W1'], 'L1_ffn_b1': _L1_ffn_in['b1'], 'L1_ffn_W2': _L1_ffn_in['W2'], 'L1_ffn_b2': _L1_ffn_in['b2'], 'L1_ffn_edge_index': _L1_ffn_in['edge_index']}

def reference(x, adj, L0_gnn_W_lin, L0_gnn_W_val, L0_gnn_a, L0_gnn_W_out, L0_gnn_src, L0_gnn_dst, L0_ffn_router_w, L0_ffn_w1, L0_ffn_w2, L0_ffn_w3, L1_gnn_Wq, L1_gnn_bq, L1_gnn_Wk, L1_gnn_bk, L1_gnn_Wv, L1_gnn_bv, L1_gnn_Wo, L1_gnn_bo, L1_gnn_alpha, L1_gnn_gamma, L1_ffn_W_gat, L1_ffn_att_src, L1_ffn_att_dst, L1_ffn_b_gat, L1_ffn_ln_gamma, L1_ffn_ln_beta, L1_ffn_W1, L1_ffn_b1, L1_ffn_W2, L1_ffn_b2, L1_ffn_edge_index):
    import jax
    import jax.numpy as jnp

    def _L0_gnn_ref(H, W_lin, W_val, a, W_out, A0, src, dst):
        import jax, jax.numpy as jnp
        import numpy as np
        BT, N, D, HEADS, E = (512, 64, 128, 4, 256)
        LRELU_SLOPE = 0.2
        EPS = 1e-08
        bt, n, d = H.shape
        h, dh = a.shape
        Xq = (H @ W_lin.T).reshape(bt, n, h, dh)
        Xv = (H @ W_val.T).reshape(bt, n, h, dh)
        Qs = Xq[:, src]
        Kt = Xq[:, dst]
        e = jnp.einsum('behd,hd->beh', jax.nn.leaky_relu(Qs + Kt, LRELU_SLOPE), a)
        e = e + jnp.log(A0[src, dst] + EPS)[None, :, None]
        e_t = e.transpose(1, 0, 2)
        m = jax.ops.segment_max(e_t, src, num_segments=n)
        ex = jnp.exp(e_t - m[src])
        denom = jax.ops.segment_sum(ex, src, num_segments=n)
        attn = ex / denom[src]
        Vt = Xv[:, dst].transpose(1, 0, 2, 3)
        Y = jax.ops.segment_sum(attn[..., None] * Vt, src, num_segments=n)
        Y = Y.transpose(1, 0, 2, 3).reshape(bt, n, d)
        return Y @ W_out.T

    def _L0_ffn_ref(x, router_w, w1, w2, w3):
        import jax, jax.numpy as jnp
        import numpy as np
        N_EXPERTS = 8
        TOP_K = 2
        B, T, C = x.shape
        flat = x.reshape(-1, C)
        logits = flat @ router_w.T
        probs = jax.nn.softmax(logits, axis=-1)
        topk_probs, topk_idx = jax.lax.top_k(probs, TOP_K)
        topk_probs = topk_probs / (jnp.sum(topk_probs, axis=-1, keepdims=True) + 1e-09)
        onehot = jax.nn.one_hot(topk_idx, N_EXPERTS, dtype=flat.dtype)
        gates = jnp.einsum('nk,nke->ne', topk_probs, onehot)
        h1 = jnp.einsum('nc,ehc->neh', flat, w1)
        h3 = jnp.einsum('nc,ehc->neh', flat, w3)
        h = jax.nn.silu(h1) * h3
        y = jnp.einsum('neh,ech->nec', h, w2)
        out = jnp.einsum('ne,nec->nc', gates, y)
        return out.reshape(B, T, C)

    def _L1_gnn_ref(base_features, neighbor_mask, parent_child_mask, Wq, bq, Wk, bk, Wv, bv, Wo, bo, alpha, gamma):
        import jax, jax.numpy as jnp
        import numpy as np
        B, N, D, H = (4, 2048, 128, 128)
        x = base_features
        Q = x @ Wq + bq
        K = x @ Wk + bk
        V = x @ Wv + bv
        scale = 1.0 / jnp.sqrt(jnp.asarray(K.shape[-1], x.dtype))
        scores = jnp.einsum('bnh,bmh->bnm', Q, K) * scale
        scores = scores + parent_child_mask[None] * alpha
        scores = jnp.where(neighbor_mask[None] == 0, jnp.asarray(-1000000000.0, x.dtype), scores)
        attn = jax.nn.softmax(scores, axis=-1)
        attn_out = jnp.einsum('bnm,bmh->bnh', attn, V)
        refined = attn_out @ Wo + bo + x
        child_sum = jnp.einsum('nm,bmd->bnd', parent_child_mask, refined)
        is_parent = (parent_child_mask.sum(axis=1) > 0).astype(x.dtype)
        delta = gamma * (child_sum - refined)
        return refined + delta * is_parent[None, :, None]

    def _L1_ffn_ref(x, W_gat, att_src, att_dst, b_gat, ln_gamma, ln_beta, W1, b1, W2, b2, edge_index):
        import jax, jax.numpy as jnp
        import numpy as np
        B, N, D = (16, 2048, 128)
        NUM_EXPERTS, TOP_K, HEADS = (4, 2, 4)
        N_EDGES = 524288
        LN_EPS = 1e-05

        def _layernorm(x, g, b):
            mu = x.mean(-1, keepdims=True)
            var = ((x - mu) ** 2).mean(-1, keepdims=True)
            return (x - mu) * jax.lax.rsqrt(var + LN_EPS) * g + b

        def _forward(x, edge_index, W_gat, att_src, att_dst, b_gat, ln_gamma, ln_beta, W1, b1, W2, b2):
            Bc, Nc, Dc = x.shape
            M = Bc * Nc
            x_flat = x.reshape(M, Dc)
            h = (x_flat @ W_gat).reshape(M, HEADS, NUM_EXPERTS)
            loops = jnp.arange(M, dtype=edge_index.dtype)
            src = jnp.concatenate([edge_index[0], loops])
            dst = jnp.concatenate([edge_index[1], loops])
            a_src = (h * att_src).sum(-1)
            a_dst = (h * att_dst).sum(-1)
            e = jax.nn.leaky_relu(a_src[src] + a_dst[dst], negative_slope=0.2)
            e_max = jax.ops.segment_max(e, dst, num_segments=M)
            ee = jnp.exp(e - e_max[dst])
            denom = jax.ops.segment_sum(ee, dst, num_segments=M)
            alpha = ee / (denom[dst] + 1e-16)
            msg = h[src] * alpha[:, :, None]
            agg = jax.ops.segment_sum(msg, dst, num_segments=M).reshape(M, HEADS * NUM_EXPERTS) + b_gat
            scores = _layernorm(agg, ln_gamma, ln_beta).reshape(M, HEADS, NUM_EXPERTS).mean(1)
            scores = scores.reshape(Bc, Nc, NUM_EXPERTS)
            topk_s, topk_i = jax.lax.top_k(scores, TOP_K)
            w = jax.nn.softmax(topk_s, axis=-1)
            out = jnp.zeros_like(x)
            for ei in range(NUM_EXPERTS):
                g = jnp.where(topk_i == ei, w, 0.0).sum(-1)
                hh = jax.nn.gelu(x @ W1[ei] + b1[ei], approximate=False)
                out = out + g[..., None] * (hh @ W2[ei] + b2[ei])
            return out
        return _forward(x, edge_index, W_gat, att_src, att_dst, b_gat, ln_gamma, ln_beta, W1, b1, W2, b2)
    x = x + _L0_gnn_ref(_layernorm(x, axis=-1), L0_gnn_W_lin, L0_gnn_W_val, L0_gnn_a, L0_gnn_W_out, adj, L0_gnn_src, L0_gnn_dst)
    x = x + _L0_ffn_ref(_layernorm(x, axis=-1), L0_ffn_router_w, L0_ffn_w1, L0_ffn_w2, L0_ffn_w3)
    x = x + _L1_gnn_ref(_layernorm(x, axis=-1), adj, adj, L1_gnn_Wq, L1_gnn_bq, L1_gnn_Wk, L1_gnn_bk, L1_gnn_Wv, L1_gnn_bv, L1_gnn_Wo, L1_gnn_bo, L1_gnn_alpha, L1_gnn_gamma)
    x = x + _L1_ffn_ref(_layernorm(x, axis=-1), L1_ffn_W_gat, L1_ffn_att_src, L1_ffn_att_dst, L1_ffn_b_gat, L1_ffn_ln_gamma, L1_ffn_ln_beta, L1_ffn_W1, L1_ffn_b1, L1_ffn_W2, L1_ffn_b2, L1_ffn_edge_index)
    return x

_drawn_inputs = setup_inputs


def setup_inputs(seed=0):
    import zlib

    import numpy as np

    out = dict(_drawn_inputs(seed))
    spreads = {'L1_gnn_bq': (0.0, 0.282),
     'L1_gnn_bk': (0.0, 2.0),
     'L1_gnn_bv': (0.0, 0.1),
     'L1_gnn_bo': (0.0, 0.1),
     'L1_ffn_b_gat': (0.0, 0.8),
     'L1_ffn_ln_gamma': (1.0, 0.6),
     'L1_ffn_ln_beta': (0.0, 2.0),
     'L1_ffn_b1': (0.0, 0.577),
     'L1_ffn_b2': (0.0, 0.28)}
    factors = {'L1_ffn_att_src': 64.0, 'L1_ffn_att_dst': 64.0}
    for name, (base, spread) in spreads.items():
        noise = np.random.default_rng([zlib.crc32(name.encode()), seed]).standard_normal(out[name].shape)
        drawn = base * np.exp(spread * noise) if base else spread * noise
        out[name] = jnp.asarray(drawn.astype(out[name].dtype))
    for name, factor in factors.items():
        out[name] = (out[name] * factor).astype(out[name].dtype)
    return out
```

```python
from contextlib import ExitStack

import numpy as np

import concourse.bass as bass
from concourse import mybir

ALU = mybir.AluOpType
ACT = mybir.ActivationFunctionType
AX = mybir.AxisListType.X
F32 = mybir.dt.float32
BF16 = mybir.dt.bfloat16
I32 = mybir.dt.int32
P = 128
BATCH, NODES, C = 16, 512, 128
TOKENS = BATCH * NODES
TILES = TOKENS // P
GT = NODES // P
GROUPS = BATCH
PAIRS = GROUPS // 2
LN_EPS = 1e-5
SRC_NODES = TOKENS


class Steps:

    def __init__(self, eng, sem, base=0):
        self.eng, self.sem, self.base, self.n = eng, sem, base, 0

    def mark(self, ins):
        self.n += 1
        ins.then_inc(self.sem, 1)

    def done(self, ins):
        self.n += 1
        ins.then_inc(self.sem, 1)
        self.eng.wait_ge(self.sem, self.base + self.n)


def credit(eng, *counts):
    for sems, n in counts:
        for sem in sems:
            eng.sem_inc(sem, n)


def spread(ap, n):
    return ap.unsqueeze(2).to_broadcast([*ap.shape, n])


class Space:

    def __init__(self, nc, ctx, stage):
        self.nc, self.ctx, self.stage = nc, ctx, stage
        self.taken = []
        ctx.callback(self.release)

    def release(self):
        if self.taken:
            self.nc.clear_and_free_semaphores(self.taken)
            self.nc.all_engine_barrier()

    def sb(self, name, shape, dt=F32):
        return self.ctx.enter_context(self.nc.sbuf_tensor(f"{self.stage}_{name}", shape, dt))

    def ps(self, name, shape, dt=F32):
        return self.ctx.enter_context(self.nc.psum_tensor(f"{self.stage}_{name}", shape, dt))

    def sem(self, name):
        self.taken.append(self.nc.alloc_semaphore(f"{self.stage}_{name}"))
        return self.taken[-1]

    def sems(self, name, n=2):
        return [self.sem(f"{name}{i}") for i in range(n)]


def constants(nc, ctx):
    sp = Space(nc, ctx, "const")
    ident = sp.sb("ident", [P, P])
    ident16 = sp.sb("ident16", [P, P], BF16)
    minus_half = sp.sb("minus_half", [P, GT])
    ones = sp.sb("ones", [P, P])
    cleared, drawn = sp.sem("cleared"), sp.sem("drawn")
    with nc.Block() as block:
        @block.gpsimd
        def _(pool):
            pool.memset(ident[:], 0.0).then_inc(cleared, 1)
            pool.memset(minus_half[:], -0.5)
            pool.memset(ones[:], 1.0)
            pool.wait_ge(cleared, 1)
            pool.affine_select(out=ident[:], in_=ident[:], compare_op=ALU.not_equal, fill=1.0, base=0,
                               pattern=[[-1, P]], channel_multiplier=1).then_inc(drawn, 1)
            pool.wait_ge(drawn, 1)
            pool.tensor_copy(ident16[:], ident[:])
    return {"ident": ident, "ident16": ident16, "minus_half": minus_half, "ones": ones}


def normalise(nc, stage, k, X, xnT, w_small, small, width):
    with ExitStack() as ctx:
        sp = Space(nc, ctx, stage)
        total, mean = sp.sb("total", [P, 2, GT]), sp.sb("mean", [P, 2, GT])
        centred, squares = sp.sb("centred", [P, 2, GT, C]), sp.sb("squares", [P, 2, GT, C])
        sqsum, var, rstd = (sp.sb(n, [P, 2, GT]) for n in ("sqsum", "var", "rstd"))
        xn, xT = sp.sb("xn", [P, 2, GT, C]), sp.sb("xT", [P, 2, NODES])
        psT = sp.ps("psT", [P, 2, 512])
        psS = sp.ps("psS", [P, 2, 512])
        s_link = sp.sem("link")
        s_centred, s_squared, s_var, s_rstd = (sp.sems(n) for n in ("s_centred", "s_squared", "s_var", "s_rstd"))
        s_normed, s_turned, s_xT, s_small, s_kept = (
            sp.sems(n) for n in ("s_normed", "s_turned", "s_xT", "s_small", "s_kept"))
        with nc.Block() as block:
            @block.sync
            def _(eng):
                credit(eng, ((s_link,), 6), (s_centred + s_squared + s_var + s_rstd, 1),
                       (s_normed + s_turned + s_xT + s_small + s_kept, 1))

            @block.vector
            def _(dve):
                with dve.Fori(1, PAIRS + 1) as j:
                    link = Steps(dve, s_link, j * 6)
                    for u in range(2):
                        x4 = X[:, bass.ds((2 * (j - 1) + u) * GT, GT), :]
                        link.done(nc.vector.tensor_reduce(total[:, u], x4, AX, ALU.add))
                        link.done(nc.vector.tensor_scalar(mean[:, u], total[:, u], 1.0 / C, None, ALU.mult))
                        nc.vector.tensor_tensor(centred[:, u], x4, spread(mean[:, u], C),
                                                ALU.subtract).then_inc(s_centred[u], 1)
                    for u in range(2):
                        dve.wait_ge(s_squared[u], j + 1)
                        link.done(nc.vector.tensor_reduce(sqsum[:, u], squares[:, u], AX, ALU.add))
                        nc.vector.tensor_scalar(var[:, u], sqsum[:, u], 1.0 / C, LN_EPS, ALU.mult,
                                                ALU.add).then_inc(s_var[u], 1)
                    for u in range(2):
                        dve.wait_ge(s_rstd[u], j + 1)
                        dve.wait_ge(s_turned[u], j)
                        nc.vector.tensor_tensor(xn[:, u], centred[:, u], spread(rstd[:, u], C),
                                                ALU.mult).then_inc(s_normed[u], 1)

            @block.gpsimd
            def _(pool):
                with pool.Fori(1, PAIRS + 1) as j:
                    for u in range(2):
                        pool.wait_ge(s_centred[u], j + 1)
                        pool.tensor_tensor(squares[:, u], centred[:, u], centred[:, u],
                                           ALU.mult).then_inc(s_squared[u], 1)
                    for u in range(2):
                        pool.wait_ge(s_var[u], j + 1)
                        pool.tensor_tensor(rstd[:, u], var[:, u], k["minus_half"][:],
                                           ALU.pow).then_inc(s_rstd[u], 1)

            @block.tensor
            def _(pe):
                with pe.Fori(1, PAIRS + 1) as j:
                    for u in range(2):
                        pe.wait_ge(s_normed[u], j + 1)
                        pe.wait_ge(s_xT[u], j)
                        for t in range(GT):
                            last = nc.tensor.transpose(psT[:, u, t * P:(t + 1) * P], xn[:, u, t, :], k["ident"][:])
                        last.then_inc(s_turned[u], 1)
                    for u in range(2):
                        if w_small is None:
                            continue
                        pe.wait_ge(s_xT[u], j + 1)
                        pe.wait_ge(s_kept[u], j)
                        for t in range(GT):
                            last = nc.tensor.matmul(psS[:, u, t * width:(t + 1) * width], xT[:, u, t * P:(t + 1) * P],
                                                    w_small, start=True, stop=True)
                        last.then_inc(s_small[u], 1)

            @block.scalar
            def _(act):
                with act.Fori(1, PAIRS + 1) as j:
                    for u in range(2):
                        g = 2 * (j - 1) + u
                        act.wait_ge(s_turned[u], j + 1)
                        if w_small is not None:
                            act.wait_ge(s_small[u], j)
                            nc.scalar.copy(xT[:, u, :], psT[:, u, :])
                        nc.scalar.copy(xnT[:, bass.ds(g * NODES, NODES)], psT[:, u, :]).then_inc(s_xT[u], 1)
                    for u in range(2):
                        if w_small is None:
                            continue
                        g = 2 * (j - 1) + u
                        act.wait_ge(s_small[u], j + 1)
                        nc.scalar.copy(small[:, bass.ds(g * GT, GT), :],
                                       psS[:, u, 0:GT * width].rearrange("p (t w) -> p t w", t=GT)).then_inc(s_kept[u], 1)


def top_two(dve, link, sp, logits, rank, d, both, m, n):
    eq, one = sp.sb("eq", [P, TILES, n]), sp.sb("one", [P, TILES, n])
    place = sp.sb("place", [P, TILES])
    rank_b = rank.unsqueeze(1).to_broadcast([P, TILES, n])
    link.done(dve.tensor_reduce(m[:], logits, AX, ALU.max))
    link.done(dve.tensor_tensor(d[:], logits, spread(m[:], n), ALU.subtract))
    link.done(dve.scalar_tensor_tensor(eq[:], d[:], 0.0, rank_b, ALU.is_equal, ALU.mult))
    link.done(dve.tensor_reduce(place[:], eq[:], AX, ALU.max))
    link.done(dve.tensor_tensor(both[:], rank_b, spread(place[:], n), ALU.is_equal))
    link.done(dve.scalar_tensor_tensor(one[:], both[:], -1e30, d[:], ALU.mult, ALU.add))
    link.done(dve.tensor_reduce(m[:], one[:], AX, ALU.max))
    link.done(dve.tensor_tensor(eq[:], one[:], spread(m[:], n), ALU.is_equal))
    link.done(dve.tensor_tensor(eq[:], eq[:], rank_b, ALU.mult))
    link.done(dve.tensor_reduce(place[:], eq[:], AX, ALU.max))
    link.done(dve.tensor_tensor(eq[:], rank_b, spread(place[:], n), ALU.is_equal))
    link.done(dve.tensor_tensor(both[:], both[:], eq[:], ALU.add))


def gates_of(nc, stage, logits, n, eps, gate_parts):
    with ExitStack() as ctx:
        sp = Space(nc, ctx, stage)
        rank_i, rank = sp.sb("rank_i", [P, n], I32), sp.sb("rank", [P, n])
        d, both, e, g, rest = (sp.sb(x, [P, TILES, n]) for x in ("d", "both", "e", "g", "rest"))
        m, s = sp.sb("m", [P, TILES]), sp.sb("s", [P, TILES])
        s_rank, s_link, s_d, s_e = (sp.sem(x) for x in ("s_rank", "s_link", "s_d", "s_e"))
        with nc.Block() as block:
            @block.gpsimd
            def _(pool):
                pool.iota(rank_i[:], [[-1, n]], base=n, channel_multiplier=0).then_inc(s_rank, 1)

            @block.scalar
            def _(act):
                act.wait_ge(s_d, 1)
                nc.scalar.activation(e[:], d[:], ACT.Exp).then_inc(s_e, 1)

            @block.vector
            def _(dve):
                link = Steps(dve, s_link)
                dve.wait_ge(s_rank, 1)
                link.done(nc.vector.tensor_copy(rank[:], rank_i[:]))
                top_two(nc.vector, link, sp, logits, rank[:], d, both, m, n)
                nc.vector.tensor_copy(s[:], m[:]).then_inc(s_d, 1)
                dve.wait_ge(s_e, 1)
                dve.wait_ge(s_d, 1)
                link.done(nc.vector.tensor_reduce(s[:], e[:], AX, ALU.add))
                link.done(nc.vector.reciprocal(m[:], s[:]))
                link.done(nc.vector.tensor_tensor(g[:], e[:], spread(m[:], n), ALU.mult))
                link.done(nc.vector.tensor_tensor(g[:], g[:], both[:], ALU.mult))
                link.done(nc.vector.tensor_reduce(s[:], g[:], AX, ALU.add))
                link.done(nc.vector.tensor_scalar(s[:], s[:], eps, None, ALU.add))
                link.done(nc.vector.reciprocal(m[:], s[:]))
                link.done(nc.vector.tensor_tensor(g[:], g[:], spread(m[:], n), ALU.mult))
                link.done(nc.vector.tensor_copy(gate_parts[:, :, 0, :], g[:]))
                link.done(nc.vector.tensor_tensor(rest[:], g[:], gate_parts[:, :, 0, :], ALU.subtract))
                link.done(nc.vector.tensor_copy(gate_parts[:, :, 1, :], rest[:]))
                link.done(nc.vector.tensor_tensor(g[:], rest[:], gate_parts[:, :, 1, :], ALU.subtract))
                nc.vector.tensor_copy(gate_parts[:, :, 2, :], g[:])


def experts(nc, stage, k, X, xnT, gate_parts, n, cuts, first, second, load, act_func, b2=None):
    w1, w3 = first
    hidden = sum(c for _, c in cuts)
    K = n * len(cuts)
    with ExitStack() as ctx:
        sp = Space(nc, ctx, stage)
        picks = sp.sb("picks", [3 * n, n, P], BF16)
        picks_f = sp.sb("picks_f", [3 * n, n, P])
        gate_now = sp.sb("gate_now", [P, 2, GT, 3 * n], BF16)
        gT = sp.sb("gT", [3 * n, 2, NODES], BF16)
        S, T, H = (sp.sb(x, [P, 2, NODES]) for x in ("S", "T", "H"))
        yT = sp.sb("yT", [P, 2, NODES])
        ps1 = sp.ps("ps1", [P, 2, 512])
        ps3 = sp.ps("ps3", [P, 2, 512]) if w3 is not None else None
        psG = sp.ps("psG", [P, 2, 512])
        acc = sp.ps("acc", [P, 512])
        psX = sp.ps("psX", [P, 512])
        psX16 = psX[:, 0:256].bitcast(BF16)
        (s_load, s_picks0, s_picks, s_up, s_S, s_gate, s_T, s_H, s_down) = (
            sp.sem(x) for x in ("s_load", "s_picks0", "s_picks", "s_up", "s_S", "s_gate", "s_T", "s_H", "s_down"))
        if w3 is None:
            s_H = s_T
        s_now, s_gturn, s_gT, s_acc, s_y, s_yturn, s_added = (
            sp.sems(x) for x in ("s_now", "s_gturn", "s_gT", "s_acc", "s_y", "s_yturn", "s_added"))
        with nc.Block() as block:
            @block.sync
            def _(sp_eng):
                own_H = (s_H,) if w3 is not None else ()
                credit(sp_eng, ((s_up, s_S, s_T, s_down) + own_H, 2 * K), ((s_gate,), 2 * n),
                       (s_now + s_gturn + s_gT + s_acc + s_y + s_yturn + s_added, 1))
                loads = load(sp_eng, s_load)
                sp_eng.wait_ge(s_load, loads)

            @block.gpsimd
            def _(pool):
                pool.memset(picks_f[:], 0.0).then_inc(s_picks0, 1)
                for part in range(3):
                    pool.wait_ge(s_picks0, part + 1)
                    pool.affine_select(out=picks_f[:], in_=picks_f[:], compare_op=ALU.not_equal, fill=1.0,
                                       base=-part * n, pattern=[[-1, n], [0, P]],
                                       channel_multiplier=1).then_inc(s_picks0, 1)
                pool.wait_ge(s_picks0, 4)
                pool.tensor_copy(picks[:], picks_f[:]).then_inc(s_picks, 1)
                with pool.Fori(1, PAIRS + 1) as j:
                    for u in range(2):
                        g = 2 * (j - 1) + u
                        pool.wait_ge(s_gturn[u], j)
                        pool.tensor_copy(gate_now[:, u], gate_parts[:, bass.ds(g * GT, GT), :, :]
                                         .rearrange("p t a e -> p t (a e)")).then_inc(s_now[u], 1)

            @block.tensor
            def _(pe):
                pe.wait_ge(s_load, load.total)
                pe.wait_ge(s_picks, 1)
                with pe.Fori(1, PAIRS + 1) as j:
                    for u in range(2):
                        g = 2 * (j - 1) + u
                        xg = xnT[:, bass.ds(g * NODES, NODES)]
                        at = lambda per, i: j * (2 * per) + max(u * per + i, 0)
                        pe.wait_ge(s_now[u], j + 1)
                        pe.wait_ge(s_added[1 - u], j + u)
                        for t in range(GT):
                            last = nc.tensor.transpose(psX16[0:3 * n, t * P:(t + 1) * P], gate_now[:, u, t, :],
                                                       k["ident16"][:])
                        last.then_inc(s_gturn[u], 1)
                        pe.wait_ge(s_gT[u], j + 1)

                        def up(i):
                            e, (c0, rows) = i // len(cuts), cuts[i % len(cuts)]
                            if i % len(cuts) == 0:
                                pe.wait_ge(s_T, at(K, i - len(cuts)))
                                nc.tensor.matmul(psG[:, e % 2, :], picks[:, e, :], gT[:, u, :], start=True,
                                                 stop=True).then_inc(s_gate, 1)
                            col = e * hidden + c0
                            pe.wait_ge(s_S, at(K, i - 1))
                            last = nc.tensor.matmul(ps1[0:rows, i % 2, :], w1[:, col:col + rows], xg, start=True, stop=True)
                            if w3 is not None:
                                pe.wait_ge(s_H, at(K, i - 1))
                                last = nc.tensor.matmul(ps3[0:rows, i % 2, :], w3[:, col:col + rows], xg, start=True,
                                                        stop=True)
                            last.then_inc(s_up, 1)

                        def down(i):
                            rows = cuts[i % len(cuts)][1]
                            pe.wait_ge(s_H, at(K, i + 1))
                            if i == 0:
                                pe.wait_ge(s_y[1 - u], j + u)
                            last = nc.tensor.matmul(acc[:], second[0:rows, i, :], H[0:rows, i % 2, :],
                                                    start=(i == 0), stop=(i == K - 1 and b2 is None))
                            if i == K - 1 and b2 is not None:
                                for q in range(3):
                                    last = nc.tensor.matmul(acc[:], b2[:, q, :], gT[:, u, :], start=False, stop=(q == 2))
                            last.then_inc(s_down, 1)

                        for i in range(K):
                            up(i)
                            if i:
                                down(i - 1)
                        down(K - 1)
                        pe.wait_ge(s_y[u], j + 1)
                        for t in range(GT):
                            last = nc.tensor.transpose(psX[:, t * P:(t + 1) * P], yT[:, u, t * P:(t + 1) * P],
                                                       k["ident"][:])
                        last.then_inc(s_yturn[u], 1)

            @block.scalar
            def _(act):
                with act.Fori(1, PAIRS + 1) as j:
                    for u in range(2):
                        at = lambda per, i: j * (2 * per) + max(u * per + i, 0)
                        act.wait_ge(s_gturn[u], j + 1)
                        nc.scalar.copy(gT[:, u, :], psX16[0:3 * n, :]).then_inc(s_gT[u], 1)
                        for i in range(K):
                            e, rows = i // len(cuts), cuts[i % len(cuts)][1]
                            act.wait_ge(s_up, at(K, i + 1))
                            act.wait_ge(s_T, at(K, i - 1))
                            b = act_func[1](i)
                            kw = {"bias": b} if b is not None else {}
                            nc.scalar.activation(S[0:rows, i % 2, :], ps1[0:rows, i % 2, :], act_func[0],
                                                 **kw).then_inc(s_S, 1)
                        act.wait_ge(s_down, at(K, K))
                        nc.scalar.copy(yT[:, u, :], acc[:]).then_inc(s_y[u], 1)

            @block.vector
            def _(dve):
                with dve.Fori(1, PAIRS + 1) as j:
                    for u in range(2):
                        g = 2 * (j - 1) + u
                        at = lambda per, i: j * (2 * per) + max(u * per + i, 0)
                        for i in range(K):
                            e, rows = i // len(cuts), cuts[i % len(cuts)][1]
                            dve.wait_ge(s_gate, at(n, e + 1))
                            dve.wait_ge(s_S, at(K, i + 1))
                            dve.wait_ge(s_down, at(K, i - 1))
                            out = T if w3 is not None else H
                            ins = nc.vector.tensor_tensor(out[0:rows, i % 2, :], S[0:rows, i % 2, :],
                                                          psG[0:rows, e % 2, :], ALU.mult)
                            ins.then_inc(s_T, 1)
                            if w3 is not None:
                                dve.wait_ge(s_T, at(K, i + 1))
                                nc.vector.tensor_tensor(H[0:rows, i % 2, :], T[0:rows, i % 2, :],
                                                        ps3[0:rows, i % 2, :], ALU.mult).then_inc(s_H, 1)
                        dve.wait_ge(s_yturn[u], j + 1)
                        x4 = X[:, bass.ds(g * GT, GT), :]
                        nc.vector.tensor_tensor(x4, x4, psX[:].rearrange("p (t c) -> p t c", t=GT),
                                                ALU.add).then_inc(s_added[u], 1)


class Loads:

    def __init__(self, pairs):
        self.pairs = pairs
        self.total = 16 * len(pairs)

    def __call__(self, eng, sem):
        for dst, src in self.pairs:
            eng.dma_start(dst, src).then_inc(sem, 16)
        return self.total


def load_now(nc, name, pairs):
    with ExitStack() as ctx:
        sem = Space(nc, ctx, name).sem("loaded")
        block = ctx.enter_context(nc.Block())

        @block.sync
        def _(sp_eng):
            for dst, src in pairs:
                sp_eng.dma_start(dst, src).then_inc(sem, 16)
            sp_eng.wait_ge(sem, 16 * len(pairs))


def moe_stage(nc, k, X, xnT, A):
    E, hid = 8, 341
    cuts = [(0, 128), (128, 128), (256, hid - 256)]
    with ExitStack() as ctx:
        sp = Space(nc, ctx, "moe")
        router = sp.sb("router", [P, E])
        logits = sp.sb("logits", [P, TILES, E])
        parts = sp.sb("parts", [P, TILES, 3, E], BF16)
        w1, w3 = sp.sb("w1", [P, E * hid]), sp.sb("w3", [P, E * hid])
        w2 = sp.sb("w2", [P, E * len(cuts), C])
        load_now(nc, "moe_first", [(router[:], A["router_wT"])])
        normalise(nc, "moe_ln", k, X, xnT, router[:], logits, E)
        gates_of(nc, "moe_gate", logits[:], E, 1e-9, parts)
        w2v = w2[:].rearrange("p (e c) d -> p e c d", c=len(cuts))
        pairs = [(w1[:], A["w1T"]), (w3[:], A["w3T"])]
        for c, (c0, r) in enumerate(cuts):
            pairs.append((w2v[0:r, :, c, :], A["w2T"][:, c0:c0 + r, :].rearrange("e h d -> h e d")))
        experts(nc, "moe_mix", k, X, xnT, parts, E, cuts, (w1, w3), w2, Loads(pairs), (ACT.Silu, lambda i: None))


def edge_attention_stage(nc, k, X, A):
    EDGES, HEADS, DH = 256, 4, 32
    EC = EDGES // P
    with ExitStack() as ctx:
        sp = Space(nc, ctx, "edge")
        W_linT, W_valT, W_outT = (sp.sb(n, [C, C]) for n in ("W_linT", "W_valT", "W_outT"))
        a_blocks = sp.sb("a_blocks", [C, HEADS])
        a_wide = sp.sb("a_wide", [C, HEADS, P])
        src_col_i, dst_col_i = sp.sb("src_col_i", [P, EC], I32), sp.sb("dst_col_i", [P, EC], I32)
        src_row_i, dst_row_i = sp.sb("src_row_i", [P, EDGES], I32), sp.sb("dst_row_i", [P, EDGES], I32)
        src_col, dst_col = sp.sb("src_col", [P, EC]), sp.sb("dst_col", [P, EC])
        src_row, dst_row = sp.sb("src_row", [P, EDGES]), sp.sb("dst_row", [P, EDGES])
        node_i, node = sp.sb("node_i", [P, GT], I32), sp.sb("node", [P, GT])
        nodes_i, nodes = sp.sb("nodes_i", [P, NODES], I32), sp.sb("nodes", [P, NODES])
        pick = sp.sb("pick", [P, GT, 2 * EDGES])
        place = sp.sb("place", [P, EC, NODES])
        same = sp.sb("same", [P, EC, EDGES])
        place_idx, place_idx_i = sp.sb("place_idx", [P, EC]), sp.sb("place_idx_i", [P, EC], I32)
        A0, logA = sp.sb("A0", [P, EC]), sp.sb("logA", [P, EC])
        diag = sp.sb("diag", [P, EC, P])
        away = sp.sb("away", [P, EC, EDGES])
        bias = sp.sb("bias", [P, EC, EDGES])
        psR = sp.ps("psR", [P, 512])
        s_load, s_iota, s_zero, s_link, s_idx, s_A0, s_Aeps, s_log, s_diag, s_row = (
            sp.sem(n) for n in ("s_load", "s_iota", "s_zero", "s_link", "s_idx", "s_A0", "s_Aeps", "s_log",
                                "s_diag", "s_row"))
        with nc.Block() as block:
            @block.sync
            def _(eng):
                n = 0
                for dst, src in ((W_linT, A["W_linT"]), (W_valT, A["W_valT"]), (W_outT, A["W_outT"]),
                                 (src_col_i, A["src"].rearrange("(p e) -> p e", e=EC)),
                                 (dst_col_i, A["dst"].rearrange("(p e) -> p e", e=EC)),
                                 (src_row_i, A["src"].unsqueeze(0).to_broadcast([P, EDGES])),
                                 (dst_row_i, A["dst"].unsqueeze(0).to_broadcast([P, EDGES]))):
                    eng.dma_start(dst[:], src).then_inc(s_load, 16)
                    n += 1
                eng.wait_ge(s_zero, 1)
                for h in range(HEADS):
                    eng.dma_start(a_blocks[h * DH:(h + 1) * DH, h:h + 1],
                                  A["a"][h].unsqueeze(1)).then_inc(s_load, 16)
                    n += 1
                eng.wait_ge(s_load, 16 * n)

            loads = 16 * (7 + HEADS)

            @block.gpsimd
            def _(pool):
                pool.iota(node_i[:], [[1, GT]], base=0, channel_multiplier=GT).then_inc(s_iota, 1)
                pool.iota(nodes_i[:], [[1, GT], [GT, P]], base=0, channel_multiplier=0).then_inc(s_iota, 1)
                pool.wait_ge(s_idx, 1)
                for ec in range(EC):
                    pool.indirect_dma_start(out=A0[:, ec:ec + 1], out_offset=None,
                                            in_=A["adj"].rearrange("a (b o) -> (a b) o", o=1),
                                            in_offset=bass.IndirectOffsetOnAxis(ap=place_idx_i[:, ec:ec + 1], axis=0),
                                            ).then_inc(s_A0, 16)

            @block.scalar
            def _(act):
                act.wait_ge(s_Aeps, 1)
                nc.scalar.activation(logA[:], A0[:], ACT.Ln).then_inc(s_log, 1)

            @block.tensor
            def _(pe):
                pe.wait_ge(s_diag, 1)
                for ec in range(EC):
                    last = nc.tensor.matmul(psR[:, ec * P:(ec + 1) * P], k["ones"][:], diag[:, ec, :],
                                            start=True, stop=True)
                last.then_inc(s_row, 1)

            @block.vector
            def _(dve):
                v = nc.vector
                link = Steps(dve, s_link)
                v.memset(a_blocks[:], 0.0).then_inc(s_zero, 1)
                dve.wait_ge(s_iota, 2)
                dve.wait_ge(s_load, loads)
                for out, src in ((node, node_i), (nodes, nodes_i), (src_col, src_col_i), (dst_col, dst_col_i),
                                 (src_row, src_row_i), (dst_row, dst_row_i)):
                    link.done(v.tensor_copy(out[:], src[:]))
                link.done(v.scalar_tensor_tensor(place_idx[:], src_col[:], float(NODES), dst_col[:], ALU.mult, ALU.add))
                v.tensor_copy(place_idx_i[:], place_idx[:]).then_inc(s_idx, 1)
                by_chunk = lambda row: row[:].rearrange("q (p e) -> q e p", e=EC)
                for c in range(GT):
                    both = pick[:, c, 0:EDGES].rearrange("q (e p) -> q e p", e=EC)
                    dst = pick[:, c, EDGES:2 * EDGES].rearrange("q (e p) -> q e p", e=EC)
                    link.done(v.tensor_scalar(dst, by_chunk(dst_row), node[:, c:c + 1], None, ALU.is_equal))
                    link.done(v.scalar_tensor_tensor(both, by_chunk(src_row), node[:, c:c + 1], dst,
                                                     ALU.is_equal, ALU.add))
                for ec in range(EC):
                    v.tensor_scalar(place[:, ec, :], nodes[:], src_col[:, ec:ec + 1], None, ALU.is_equal)
                    link.done(v.tensor_scalar(same[:, ec, :].rearrange("q (e p) -> q e p", e=EC), by_chunk(src_row),
                                              src_col[:, ec:ec + 1], None, ALU.is_equal))
                link.done(v.tensor_scalar(away[:], same[:], 1.0, 1e30, ALU.subtract, ALU.mult))
                v.tensor_copy(a_wide[:], spread(a_blocks[:], P))
                dve.wait_ge(s_A0, 16 * EC)
                v.tensor_scalar(A0[:], A0[:], 1e-8, None, ALU.add).then_inc(s_Aeps, 1)
                dve.wait_ge(s_log, 1)
                for ec in range(EC):
                    last = v.tensor_scalar(diag[:, ec, :], k["ident"][:], logA[:, ec:ec + 1], None, ALU.mult)
                last.then_inc(s_diag, 1)
                dve.wait_ge(s_row, 1)
                for ec in range(EC):
                    v.tensor_tensor(bias[:, ec, :], away[:, ec, :], psR[:, 0:EDGES], ALU.add)

        total, mean, sqsum, var, rstd = (sp.sb(n, [P, 2, GT]) for n in ("total", "mean", "sqsum", "var", "rstd"))
        centred, squares, xn = (sp.sb(n, [P, 2, GT, C]) for n in ("centred", "squares", "xn"))
        GT_, QV = sp.sb("gathered", [P, 2, 2 * EDGES]), sp.sb("QV", [P, 2, 2 * EDGES])
        L = sp.sb("L", [P, 2, EDGES])
        junk = sp.sb("junk", [P, EC * HEADS, EDGES])
        top, z, ex, den, attn = (sp.sb(n, [P, 2, EC, HEADS]) for n in ("top", "z", "ex", "den", "attn"))
        weighed = sp.sb("weighed", [P, 2, EC, C])
        YT = sp.sb("YT", [P, 2, NODES])
        psA = sp.ps("psA", [P, 2, 512])
        psB = sp.ps("psB", [P, 2, 512])
        (s_centred, s_squared, s_var, s_rstd, s_normed, s_g, s_GT, s_qv, s_QV, s_L, s_e, s_z, s_ex, s_den,
         s_w, s_y, s_YT, s_out, s_added) = (sp.sems(n) for n in (
             "centred", "squared", "var", "rstd", "normed", "g", "GT", "qv", "QV", "L", "e", "z", "ex",
             "den", "w", "y", "YT", "out", "added"))
        s_steps = sp.sem("steps")
        with ExitStack() as ctx2, nc.Block() as block:
            psC = [ctx2.enter_context(nc.psum_tensor(f"edge_psC{i}", [P, 512], F32)) for i in range(3)]
            wide = [[psC[0], psC[1]], [psC[2], psR]]

            @block.sync
            def _(eng):
                credit(eng, ((s_steps,), 14), (s_centred + s_squared + s_var + s_rstd + s_normed, 1),
                       (s_g + s_GT + s_qv + s_QV + s_L + s_e + s_z + s_ex + s_den + s_w, 1),
                       (s_y + s_YT + s_out + s_added, 1))

            @block.tensor
            def _(pe):
                with pe.Fori(1, PAIRS + 1) as j:
                    for u in range(2):
                        pe.wait_ge(s_normed[u], j + 1)
                        pe.wait_ge(s_YT[u], j)
                        for c in range(GT):
                            last = nc.tensor.matmul(psA[:, u, :], xn[:, u, c, :], pick[:, c, :], start=(c == 0),
                                                    stop=(c == GT - 1))
                        last.then_inc(s_g[u], 1)
                    for u in range(2):
                        pe.wait_ge(s_GT[u], j + 1)
                        pe.wait_ge(s_added[u], j)
                        nc.tensor.matmul(psB[:, u, 0:EDGES], W_linT[:], GT_[:, u, 0:EDGES], start=True, stop=True)
                        for ec in range(EC):
                            at = EDGES + ec * P
                            last = nc.tensor.matmul(psB[:, u, at:at + C], GT_[:, u, at:at + P], W_valT[:],
                                                    start=True, stop=True)
                        last.then_inc(s_qv[u], 1)
                    for u in range(2):
                        pe.wait_ge(s_L[u], j + 1)
                        for h in range(HEADS):
                            nc.tensor.matmul(wide[u][h // 2][:, (h % 2) * EDGES:(h % 2 + 1) * EDGES], a_wide[:, h, :],
                                             L[:, u, :], start=True, stop=True)
                        for ec in range(EC):
                            last = nc.tensor.matmul(psA[:, u, ec * HEADS:(ec + 1) * HEADS], L[:, u, ec * P:(ec + 1) * P],
                                                    a_blocks[:], start=True, stop=True)
                        last.then_inc(s_e[u], 1)
                    for u in range(2):
                        pe.wait_ge(s_ex[u], j + 1)
                        for ec in range(EC):
                            at = 8 + ec * HEADS
                            for e2 in range(EC):
                                last = nc.tensor.matmul(psA[:, u, at:at + HEADS], same[:, e2, ec * P:(ec + 1) * P],
                                                        ex[:, u, e2, :], start=(e2 == 0), stop=(e2 == EC - 1))
                        last.then_inc(s_den[u], 1)
                    for u in range(2):
                        pe.wait_ge(s_w[u], j + 1)
                        for ec in range(EC):
                            last = nc.tensor.matmul(psA[:, u, :], weighed[:, u, ec, :], place[:, ec, :],
                                                    start=(ec == 0), stop=(ec == EC - 1))
                        last.then_inc(s_y[u], 1)
                    for u in range(2):
                        pe.wait_ge(s_YT[u], j + 1)
                        for c in range(GT):
                            last = nc.tensor.matmul(psB[:, u, c * P:(c + 1) * P], YT[:, u, c * P:(c + 1) * P], W_outT[:],
                                                    start=True, stop=True)
                        last.then_inc(s_out[u], 1)

            @block.scalar
            def _(act):
                with act.Fori(1, PAIRS + 1) as j:
                    for u in range(2):
                        act.wait_ge(s_g[u], j + 1)
                        nc.scalar.copy(GT_[:, u, :], psA[:, u, :]).then_inc(s_GT[u], 1)
                    for u in range(2):
                        act.wait_ge(s_qv[u], j + 1)
                        nc.scalar.copy(QV[:, u, :], psB[:, u, :]).then_inc(s_QV[u], 1)
                    for u in range(2):
                        act.wait_ge(s_z[u], j + 1)
                        nc.scalar.activation(ex[:, u], z[:, u], ACT.Exp).then_inc(s_ex[u], 1)
                    for u in range(2):
                        act.wait_ge(s_y[u], j + 1)
                        nc.scalar.copy(YT[:, u, :], psA[:, u, :]).then_inc(s_YT[u], 1)

            @block.gpsimd
            def _(pool):
                with pool.Fori(1, PAIRS + 1) as j:
                    for u in range(2):
                        pool.wait_ge(s_centred[u], j + 1)
                        pool.tensor_tensor(squares[:, u], centred[:, u], centred[:, u],
                                           ALU.mult).then_inc(s_squared[u], 1)
                    for u in range(2):
                        pool.wait_ge(s_var[u], j + 1)
                        pool.tensor_tensor(rstd[:, u], var[:, u], k["minus_half"][:],
                                           ALU.pow).then_inc(s_rstd[u], 1)

            @block.vector
            def _(dve):
                v = nc.vector
                with dve.Fori(1, PAIRS + 1) as j:
                    link = Steps(dve, s_steps, j * 14)
                    for u in range(2):
                        x4 = X[:, bass.ds((2 * (j - 1) + u) * GT, GT), :]
                        link.done(v.tensor_reduce(total[:, u], x4, AX, ALU.add))
                        link.done(v.tensor_scalar(mean[:, u], total[:, u], 1.0 / C, None, ALU.mult))
                        v.tensor_tensor(centred[:, u], x4, spread(mean[:, u], C), ALU.subtract).then_inc(s_centred[u], 1)
                    for u in range(2):
                        dve.wait_ge(s_squared[u], j + 1)
                        link.done(v.tensor_reduce(sqsum[:, u], squares[:, u], AX, ALU.add))
                        v.tensor_scalar(var[:, u], sqsum[:, u], 1.0 / C, LN_EPS, ALU.mult, ALU.add).then_inc(s_var[u], 1)
                    for u in range(2):
                        dve.wait_ge(s_rstd[u], j + 1)
                        v.tensor_tensor(xn[:, u], centred[:, u], spread(rstd[:, u], C),
                                        ALU.mult).then_inc(s_normed[u], 1)
                    for u in range(2):
                        dve.wait_ge(s_QV[u], j + 1)
                        v.scalar_tensor_tensor(L[:, u, :], QV[:, u, 0:EDGES], 0.2, QV[:, u, 0:EDGES], ALU.mult,
                                               ALU.max).then_inc(s_L[u], 1)
                    for u in range(2):
                        dve.wait_ge(s_e[u], j + 1)
                        link.mark(v.tensor_tensor(z[:, u], psA[:, u, 0:8].rearrange("p (e h) -> p e h", e=EC),
                                                  spread(logA[:], HEADS), ALU.add))
                        for ec in range(EC):
                            for h in range(HEADS):
                                last = v.tensor_tensor_reduce(
                                    junk[:, ec * HEADS + h, :], wide[u][h // 2][:, (h % 2) * EDGES:(h % 2 + 1) * EDGES], bias[:, ec, :], 1.0,
                                    -3e38, ALU.add, ALU.max, top[:, u, ec, h:h + 1])
                        link.done(last)
                        v.tensor_tensor(z[:, u], z[:, u], top[:, u], ALU.subtract).then_inc(s_z[u], 1)
                    for u in range(2):
                        dve.wait_ge(s_den[u], j + 1)
                        link.done(v.reciprocal(den[:, u], psA[:, u, 8:16].rearrange("p (e h) -> p e h", e=EC)))
                        dve.wait_ge(s_ex[u], j + 1)
                        link.done(v.tensor_tensor(attn[:, u], ex[:, u], den[:, u], ALU.mult))
                        v.tensor_tensor(weighed[:, u].rearrange("p e (h d) -> p (e h) d", h=HEADS),
                                        QV[:, u, EDGES:2 * EDGES].rearrange("p (e d) -> p e d", e=EC * HEADS),
                                        spread(attn[:, u].rearrange("p e h -> p (e h)"), DH),
                                        ALU.mult).then_inc(s_w[u], 1)
                    for u in range(2):
                        x4 = X[:, bass.ds((2 * (j - 1) + u) * GT, GT), :]
                        dve.wait_ge(s_out[u], j + 1)
                        v.tensor_tensor(x4, x4, psB[:, u, :].rearrange("p (t c) -> p t c", t=GT),
                                        ALU.add).then_inc(s_added[u], 1)
                    assert link.n == 14, link.n


def dense_attention_stage(nc, k, X, xnT, A):
    SCALE = float(np.float32(1.0) / np.sqrt(np.float32(C)))
    with ExitStack() as ctx:
        sp = Space(nc, ctx, "att")
        normalise(nc, "att_ln", k, X, xnT, None, None, 0)
        Wq, Wk, WvT, Wo = (sp.sb(n, [C, C]) for n in ("Wq", "Wk", "WvT", "Wo"))
        bq, bk, bv, bo = (sp.sb(n, [C, 1]) for n in ("bq", "bk", "bv", "bo"))
        Wvo, bvo = sp.sb("Wvo", [C, C]), sp.sb("bvo", [C, 1])
        alpha, gamma = sp.sb("alpha", [P, 1]), sp.sb("gamma", [P, 1])
        bias = sp.sb("bias", [P, GT, NODES])
        mixT = sp.sb("mixT", [P, GT, NODES])
        keepers = sp.sb("keepers", [P, NODES])
        with ExitStack() as ctx2:
            s2 = Space(nc, ctx2, "att_set")
            adjN, adj, mix = (s2.sb(n, [P, GT, NODES]) for n in ("adjN", "adj", "mix"))
            linked = s2.sb("linked", [P, GT, NODES])
            degree, parent, has, rest = (s2.sb(n, [P, GT]) for n in ("degree", "parent", "has", "rest"))
            diag = s2.sb("diag", [P, GT, P])
            psM, psK, psW = s2.ps("psM", [P, 2, 512]), s2.ps("psK", [P, 512]), s2.ps("psW", [P, 512])
            s_load, s_link, s_diag, s_mix, s_turn, s_out, s_keep, s_w = (
                s2.sem(n) for n in ("load", "link", "diag", "mix", "turn", "out", "keep", "w"))
            with nc.Block() as block:
                loads = [(Wq, A["Wq"]), (Wk, A["Wk"]), (WvT, A["WvT"]), (Wo, A["Wo"]),
                         (bq, A["bq"].unsqueeze(1)), (bk, A["bk"].unsqueeze(1)), (bv, A["bv"].unsqueeze(1)),
                         (bo, A["bo"].unsqueeze(1)),
                         (alpha, A["alpha"].unsqueeze(0).to_broadcast([P, 1])),
                         (gamma, A["gamma"].unsqueeze(0).to_broadcast([P, 1])),
                         (adjN, A["adj"].rearrange("(p c) m -> p c m", c=GT))]

                @block.sync
                def _(eng):
                    for dst, src in loads:
                        eng.dma_start(dst[:], src).then_inc(s_load, 16)

                @block.tensor
                def _(pe):
                    pe.wait_ge(s_load, 16 * len(loads))
                    nc.tensor.matmul(psW[:, 0:C], WvT[:], Wo[:], start=True, stop=True)
                    nc.tensor.matmul(psW[:, C:C + 1], Wo[:], bv[:], start=True, stop=True).then_inc(s_w, 1)
                    pe.wait_ge(s_diag, 1)
                    for c in range(GT):
                        last = nc.tensor.matmul(psK[:, c * P:(c + 1) * P], k["ones"][:], diag[:, c, :], start=True,
                                                stop=True)
                    last.then_inc(s_keep, 1)
                    pe.wait_ge(s_mix, 1)
                    for m in range(GT):
                        if m >= 2:
                            pe.wait_ge(s_out, m - 1)
                        for c in range(GT):
                            last = nc.tensor.transpose(psM[:, m % 2, c * P:(c + 1) * P], mix[:, c, m * P:(m + 1) * P],
                                                       k["ident"][:])
                        last.then_inc(s_turn, 1)

                @block.scalar
                def _(act):
                    for m in range(GT):
                        act.wait_ge(s_turn, m + 1)
                        nc.scalar.copy(mixT[:, m, :], psM[:, m % 2, :]).then_inc(s_out, 1)

                @block.vector
                def _(dve):
                    v = nc.vector
                    link = Steps(dve, s_link)
                    dve.wait_ge(s_load, 16 * len(loads))
                    for c in range(GT):
                        link.mark(v.tensor_copy(adj[:, c, :].rearrange("q (c p) -> q c p", c=GT),
                                                adjN[:, c, :].rearrange("q (p c) -> q c p", c=GT)))
                    link.done(v.tensor_reduce(degree[:], adjN[:], AX, ALU.add))
                    link.done(v.tensor_scalar(linked[:], adj[:], 0.0, None, ALU.not_equal))
                    link.done(v.tensor_reduce(has[:], linked[:], AX, ALU.max))
                    for c in range(GT):
                        last = v.tensor_scalar(diag[:, c, :], k["ident"][:], has[:, c:c + 1], SCALE, ALU.mult, ALU.mult)
                    last.then_inc(s_diag, 1)
                    link.done(v.tensor_scalar(linked[:], linked[:], 1.0, 1e9, ALU.subtract, ALU.mult))
                    v.scalar_tensor_tensor(bias[:], adj[:], alpha[:, 0:1], linked[:], ALU.mult, ALU.add)
                    link.done(v.tensor_scalar(parent[:], degree[:], 0.0, gamma[:, 0:1], ALU.is_gt, ALU.mult))
                    link.done(v.tensor_scalar(rest[:], parent[:], -1.0, 1.0, ALU.mult, ALU.add))
                    for c in range(GT):
                        link.mark(v.tensor_scalar(mix[:, c, :], adj[:, c, :], parent[:, c:c + 1], None, ALU.mult))
                    dve.wait_ge(s_link, link.n)
                    for c in range(GT):
                        block_c = mix[:, c, c * P:(c + 1) * P]
                        last = v.scalar_tensor_tensor(block_c, k["ident"][:], rest[:, c:c + 1], block_c, ALU.mult, ALU.add)
                    last.then_inc(s_mix, 1)
                    dve.wait_ge(s_keep, 1)
                    v.tensor_copy(keepers[:], psK[:])
                    dve.wait_ge(s_w, 1)
                    v.tensor_copy(Wvo[:], psW[:, 0:C])
                    v.tensor_tensor(bvo[:], psW[:, C:C + 1], bo[:], ALU.add)

        QT, KT, U, rT, r, fT = (sp.sb(n, [P, 2, NODES]) for n in ("QT", "KT", "U", "rT", "r", "fT"))
        xg = sp.sb("xg", [P, 2, NODES])
        PT = sp.sb("PT", [P, 2, GT, NODES])
        SC, Pn = sp.sb("SC", [P, 2, NODES]), sp.sb("Pn", [P, 2, NODES])
        Pe = sp.sb("Pe", [P, 2, NODES])
        top, ntop, rowsum, rinv = (sp.sb(n, [P, 2]) for n in ("top", "ntop", "rowsum", "rinv"))
        carrier = sp.sb("carrier", [P, 2])
        psG = [sp.ps(f"psG{i}", [P, 512]) for i in range(4)]
        psS, psT = sp.ps("psS", [P, 2, 512]), sp.ps("psT", [P, 2, 512])
        (s_xg, s_q, s_k, s_u, s_QT, s_KT, s_U, s_o, s_rT, s_rt, s_r, s_f, s_fT, s_ft, s_added) = (sp.sems(n) for n in (
            "xg", "q", "k", "u", "QT", "KT", "U", "o", "rT", "rt", "r", "f", "fT", "ft", "added"))
        s_S, s_top, s_ntop, s_exp, s_inv, s_Pn, s_pt, s_PT = (sp.sem(n) for n in (
            "S", "top", "ntop", "exp", "inv", "Pn", "pt", "PT"))
        ITEMS = 2 * GT
        with nc.Block() as block:
            @block.sync
            def _(eng):
                credit(eng, (s_xg + s_q + s_k + s_u + s_QT + s_KT + s_U + s_o + s_rT + s_rt + s_r + s_f + s_fT, 1),
                       (s_ft + s_added, 1), ((s_S, s_top, s_ntop, s_exp, s_inv, s_Pn, s_pt, s_PT), ITEMS))

            @block.gpsimd
            def _(pool):
                with pool.Fori(1, PAIRS + 1) as j:
                    for u in range(2):
                        pool.wait_ge(s_rT[u], j)
                        pool.tensor_copy(xg[:, u, :], xnT[:, bass.ds((2 * (j - 1) + u) * NODES, NODES)]).then_inc(s_xg[u], 1)

            @block.tensor
            def _(pe):
                mm = nc.tensor.matmul
                with pe.Fori(1, PAIRS + 1) as j:
                    plan = [[(0, s_fT[0], 0), (1, s_fT[1], 0), (2, s_added[0], 0)],
                            [(3, s_added[1], 0), (0, s_QT[0], 1), (1, s_KT[0], 1)]]
                    for u in range(2):
                        pe.wait_ge(s_xg[u], j + 1)
                        for step, (bank, free, more) in enumerate(plan[u]):
                            pe.wait_ge(free, j + more)
                            if step < 2:
                                mm(psG[bank][:], (Wq, Wk)[step][:], xg[:, u, :], start=True,
                                   stop=True).then_inc((s_q, s_k)[step][u], 1)
                            else:
                                for c in range(GT):
                                    last = mm(psG[bank][:, c * P:(c + 1) * P], xg[:, u, c * P:(c + 1) * P], Wvo[:],
                                              start=True, stop=True)
                                last.then_inc(s_u[u], 1)

                    def scores(q):
                        c, u = q // 2, q % 2
                        pe.wait_ge(s_QT[u], j + 1)
                        pe.wait_ge(s_KT[u], j + 1)
                        pe.wait_ge(s_top, ITEMS * j + max(q - 1, 0))
                        mm(psS[:, q % 2, :], QT[:, u, c * P:(c + 1) * P], KT[:, u, :], start=True,
                           stop=True).then_inc(s_S, 1)

                    def turn(q):
                        pe.wait_ge(s_Pn, ITEMS * j + q + 1)
                        pe.wait_ge(s_PT, ITEMS * j + max(q - 1, 0))
                        for m in range(GT):
                            last = nc.tensor.transpose(psT[:, q % 2, m * P:(m + 1) * P],
                                                       Pn[:, q % 2, m * P:(m + 1) * P], k["ident"][:])
                        last.then_inc(s_pt, 1)

                    for q in range(ITEMS + 4):
                        if q < ITEMS:
                            scores(q)
                        if q >= 4:
                            turn(q - 4)
                    for u in range(2):
                        pe.wait_ge(s_KT[1], j + 1)
                        pe.wait_ge(s_U[1], j + 1)
                        pe.wait_ge(s_PT, ITEMS * j + ITEMS - 1 + u)
                        for m in range(GT):
                            last = mm(psG[u][:], U[:, u, m * P:(m + 1) * P], PT[:, u, m, :], start=(m == 0),
                                      stop=(m == GT - 1))
                        last.then_inc(s_o[u], 1)
                    for u in range(2):
                        pe.wait_ge(s_rT[u], j + 1)
                        for c in range(GT):
                            last = nc.tensor.transpose(psG[2 + u][:, c * P:(c + 1) * P], rT[:, u, c * P:(c + 1) * P],
                                                       k["ident"][:])
                        last.then_inc(s_rt[u], 1)
                    for u in range(2):
                        pe.wait_ge(s_r[u], j + 1)
                        for m in range(GT):
                            last = mm(psG[u][:], r[:, u, m * P:(m + 1) * P], mixT[:, m, :], start=(m == 0),
                                      stop=(m == GT - 1))
                        last.then_inc(s_f[u], 1)
                    for u in range(2):
                        pe.wait_ge(s_fT[u], j + 1)
                        for c in range(GT):
                            last = nc.tensor.transpose(psG[2 + u][:, c * P:(c + 1) * P], fT[:, u, c * P:(c + 1) * P],
                                                       k["ident"][:])
                        last.then_inc(s_ft[u], 1)

            @block.scalar
            def _(act):
                with act.Fori(1, PAIRS + 1) as j:
                    for u in range(2):
                        act.wait_ge(s_k[u], j + 1)
                        nc.scalar.activation(KT[:, u, :], psG[(1, 0)[u]][:], ACT.Identity, bias=bk[:, 0:1]).then_inc(s_KT[u], 1)
                        act.wait_ge(s_u[u], j + 1)
                        nc.scalar.copy(U[:, u, :], psG[(2, 1)[u]][:]).then_inc(s_U[u], 1)

                    def exps(q):
                        act.wait_ge(s_ntop, ITEMS * j + q + 1)
                        act.wait_ge(s_Pn, ITEMS * j + max(q - 1, 0))
                        nc.scalar.activation(Pe[:, q % 2, :], SC[:, q % 2, :], ACT.Exp, bias=ntop[:, q % 2:q % 2 + 1],
                                             accum_out=rowsum[:, q % 2:q % 2 + 1]).then_inc(s_exp, 1)

                    def out(q):
                        c, u = q // 2, q % 2
                        act.wait_ge(s_pt, ITEMS * j + q + 1)
                        nc.scalar.copy(PT[:, u, :, c * P:(c + 1) * P],
                                       psT[:, q % 2, :].rearrange("p (m n) -> p m n", m=GT)).then_inc(s_PT, 1)

                    for q in range(ITEMS + 4):
                        if q < ITEMS:
                            exps(q)
                        if q >= 4:
                            out(q - 4)
                    for u in range(2):
                        act.wait_ge(s_rt[u], j + 1)
                        nc.scalar.copy(r[:, u, :], psG[2 + u][:]).then_inc(s_r[u], 1)
                    for u in range(2):
                        act.wait_ge(s_f[u], j + 1)
                        nc.scalar.copy(fT[:, u, :], psG[u][:]).then_inc(s_fT[u], 1)

            @block.vector
            def _(dve):
                v = nc.vector
                with dve.Fori(1, PAIRS + 1) as j:
                    for u in range(2):
                        dve.wait_ge(s_q[u], j + 1)
                        v.scalar_tensor_tensor(QT[:, u, :], psG[(0, 3)[u]][:], bq[:, 0:1], keepers[:], ALU.add,
                                               ALU.mult).then_inc(s_QT[u], 1)
                    for q in range(ITEMS + 2):
                        b, old = q % 2, q - 2
                        if q < ITEMS:
                            dve.wait_ge(s_S, ITEMS * j + q + 1)
                        if old < 0:
                            dve.wait_ge(s_exp, ITEMS * j)
                            v.memset(carrier[:, q:q + 1], 0.0)
                        else:
                            dve.wait_ge(s_exp, ITEMS * j + old + 1)
                            v.reciprocal(rinv[:, b:b + 1], rowsum[:, b:b + 1]).then_inc(s_inv, 1)
                        if q < ITEMS:
                            v.tensor_tensor_reduce(SC[:, b, :], psS[:, b, :], bias[:, q // 2, :], 1.0, -3e38, ALU.add, ALU.max,
                                                   top[:, b:b + 1]).then_inc(s_top, 1)
                        if old >= 0:
                            dve.wait_ge(s_inv, ITEMS * j + old + 1)
                            dve.wait_ge(s_pt, ITEMS * j + max(old - 1, 0))
                            v.tensor_scalar(Pn[:, b, :], Pe[:, b, :], rinv[:, b:b + 1], None, ALU.mult).then_inc(s_Pn, 1)
                        if q < ITEMS:
                            dve.wait_ge(s_top, ITEMS * j + q + 1)
                            v.tensor_scalar(ntop[:, b:b + 1], top[:, b:b + 1], -1.0, None, ALU.mult).then_inc(s_ntop, 1)
                    for u in range(2):
                        dve.wait_ge(s_o[u], j + 1)
                        v.scalar_tensor_tensor(rT[:, u, :], psG[u][:], bvo[:, 0:1], xg[:, u, :], ALU.add,
                                               ALU.add).then_inc(s_rT[u], 1)
                    for u in range(2):
                        x4 = X[:, bass.ds((2 * (j - 1) + u) * GT, GT), :]
                        dve.wait_ge(s_ft[u], j + 1)
                        v.tensor_tensor(x4, x4, psG[2 + u][:].rearrange("p (t c) -> p t c", t=GT),
                                        ALU.add).then_inc(s_added[u], 1)


EDGES2 = 524288
LANE = EDGES2 // P
GAT_HEADS, GAT_EXPERTS = 4, 4
HEAD_COLS = GAT_HEADS * GAT_EXPERTS
LAST_NODE = SRC_NODES - 1
KEY_MARK = 1 << 29
NODE_BITS = 13
HCOLS = 8
FEATURES = HEAD_COLS + GAT_HEADS


def edge_keys_stage(nc, k, A, keys, far_count, cell):
    with ExitStack() as ctx:
        sp = Space(nc, ctx, "keys")
        src, dst = sp.sb("src", [P, LANE], I32), sp.sb("dst", [P, LANE], I32)
        real, live = sp.sb("real", [P, LANE]), sp.sb("live", [P, LANE])
        lo16, hi16 = sp.sb("lo16", [P, LANE], BF16), sp.sb("hi16", [P, LANE], BF16)
        iota_i = sp.sb("iota_i", [P, P, 2], I32)
        iota16 = sp.sb("iota16", [P, P, 2], BF16)
        iota1_16 = sp.sb("iota1_16", [P, TILES, 2], BF16)
        LO = sp.sb("LO", [P, 2, HCOLS // 2, P, 2], BF16)
        HI = sp.sb("HI", [P, 2, HCOLS // 2, TILES, 2], BF16)
        zeros = sp.sb("zeros", [P, P], BF16)
        count, most = sp.sb("count", [P, 1]), sp.sb("most", [P, 1])
        passes_f = sp.sb("passes_f", [P, 1])
        passes = sp.sb("passes", [P, 1], I32)
        hist = sp.ps("hist", [P, 512])
        s_load, s_iota, s_link, s_count, s_most, s_zero, s_hist, s_ready = (
            sp.sem(n) for n in ("load", "iota", "link", "count", "most", "zero", "hist", "ready"))
        s_hot, s_used = sp.sems("hot"), sp.sems("used")
        edges = A["edge_index"].rearrange("a (p i) -> a p i", p=P)
        turns = LANE // (2 * HCOLS)
        with nc.Block() as block:
            @block.sync
            def _(eng):
                credit(eng, (s_hot + s_used, 1))
                eng.dma_start(src[:], edges[0]).then_inc(s_load, 16)
                eng.dma_start(dst[:], edges[1]).then_inc(s_load, 16)

            @block.gpsimd
            def _(pool):
                pool.iota(iota_i[:], [[1, P], [0, 2]], base=0, channel_multiplier=0).then_inc(s_iota, 1)
                pool.wait_ge(s_count, 1)
                pool.partition_all_reduce(most[:], count[:], P, bass.bass_isa.ReduceOp.max).then_inc(s_most, 1)

            @block.tensor
            def _(pe):
                pe.wait_ge(s_zero, 1)
                nc.tensor.matmul(hist[:, 0:TILES], zeros[:], zeros[:, 0:TILES], start=True, stop=False)
                with pe.Fori(1, turns + 1) as j:
                    for u in range(2):
                        pe.wait_ge(s_hot[u], j + 1)
                        for i in range(HCOLS):
                            last = nc.tensor.matmul(hist[:, 0:TILES], LO[:, u, i // 2, :, i % 2], HI[:, u, i // 2, :, i % 2],
                                                    start=False, stop=False)
                        last.then_inc(s_used[u], 1)
                nc.tensor.matmul(hist[:, 0:TILES], zeros[:], zeros[:, 0:TILES], start=False, stop=True).then_inc(s_hist, 1)

            @block.vector
            def _(dve):
                v = nc.vector
                link = Steps(dve, s_link)
                v.memset(zeros[:], 0.0).then_inc(s_zero, 1)
                dve.wait_ge(s_iota, 1)
                v.tensor_copy(iota16[:], iota_i[:])
                v.tensor_scalar(iota1_16[:], iota_i[:, 0:TILES, :], 1.0, None, ALU.add)
                dve.wait_ge(s_load, 32)
                keys_i = keys[:].bitcast(I32)
                link.mark(v.tensor_scalar(keys_i, dst[:], NODE_BITS, KEY_MARK, ALU.logical_shift_left, ALU.bitwise_or))
                link.done(v.tensor_scalar(real[:], dst[:], float(SRC_NODES), None, ALU.is_lt))
                link.done(v.tensor_tensor(keys_i, keys_i, src[:], ALU.bitwise_or))
                link.done(v.scalar_tensor_tensor(live[:], src[:], float(LAST_NODE), real[:], ALU.is_lt, ALU.mult))
                link.mark(v.tensor_tensor(real[:], real[:], live[:], ALU.subtract))
                link.mark(v.tensor_tensor(keys[:], keys[:], live[:], ALU.mult))
                v.tensor_reduce(count[:], live[:], AX, ALU.add).then_inc(s_count, 1)
                link.done(v.tensor_scalar(src[:], dst[:], 2, P - 1, ALU.logical_shift_right, ALU.bitwise_and))
                link.done(v.tensor_copy(lo16[:], src[:]))
                link.done(v.tensor_scalar(src[:], dst[:], 9, 2, ALU.logical_shift_right, ALU.logical_shift_left))
                link.done(v.tensor_scalar(dst[:], dst[:], GT - 1, None, ALU.bitwise_and))
                link.done(v.tensor_tensor(src[:], src[:], dst[:], ALU.bitwise_or))
                link.done(v.scalar_tensor_tensor(hi16[:], src[:], 1.0, real[:], ALU.add, ALU.mult))
                dve.wait_ge(s_most, 1)
                link.done(v.tensor_scalar(passes_f[:], most[:], 31.0, 32.0, ALU.add, ALU.max))
                link.done(v.tensor_copy(passes[:], passes_f[:]))
                v.tensor_scalar(cell[:], passes[:], 4, None, ALU.logical_shift_right)
                with dve.Fori(1, turns + 1) as j:
                    for u in range(2):
                        at = bass.ds((j - 1) * (2 * HCOLS) + u * HCOLS, HCOLS)
                        dve.wait_ge(s_used[u], j)
                        v.tensor_tensor(LO[:, u], iota16[:].unsqueeze(1).to_broadcast([P, HCOLS // 2, P, 2]),
                                        lo16[:, at].rearrange("p (a b) -> p a b", b=2).unsqueeze(2)
                                        .to_broadcast([P, HCOLS // 2, P, 2]), ALU.is_equal)
                        v.tensor_tensor(HI[:, u], iota1_16[:].unsqueeze(1).to_broadcast([P, HCOLS // 2, TILES, 2]),
                                        hi16[:, at].rearrange("p (a b) -> p a b", b=2).unsqueeze(2)
                                        .to_broadcast([P, HCOLS // 2, TILES, 2]), ALU.is_equal).then_inc(s_hot[u], 1)
                dve.wait_ge(s_hist, 1)
                v.tensor_copy(far_count[:], hist[:, 0:TILES])


def gat_stage(nc, k, X, xnT, A, keys, far_count, cell, parts):
    NH, W = GAT_HEADS, FEATURES
    with ExitStack() as ctx:
        sp = Space(nc, ctx, "gat")
        w_node = sp.sb("w_node", [C, W + NH])
        node = sp.sb("node", [P, TILES, W + NH])
        with ExitStack() as ctx2:
            s2 = Space(nc, ctx2, "gat_set")
            WgT, att = s2.sb("WgT", [HEAD_COLS, C]), s2.sb("att", [HEAD_COLS, 2 * NH])
            psW = s2.ps("psW", [C, 512])
            s_load, s_zero, s_w = (s2.sem(n) for n in ("load", "zero", "w"))
            with nc.Block() as block:
                @block.sync
                def _(eng):
                    eng.dma_start(WgT[:], A["W_gatT"]).then_inc(s_load, 16)
                    eng.dma_start(w_node[:, 0:HEAD_COLS], A["W_gat"]).then_inc(s_load, 16)
                    eng.wait_ge(s_zero, 1)
                    for i, name in enumerate(("att_src", "att_dst")):
                        for h in range(NH):
                            eng.dma_start(att[h * NH:(h + 1) * NH, i * NH + h:i * NH + h + 1],
                                          A[name][h].unsqueeze(1)).then_inc(s_load, 16)

                @block.tensor
                def _(pe):
                    pe.wait_ge(s_load, 16 * (2 + 2 * NH))
                    nc.tensor.matmul(psW[:, 0:2 * NH], WgT[:], att[:], start=True, stop=True).then_inc(s_w, 1)

                @block.vector
                def _(dve):
                    nc.vector.memset(att[:], 0.0).then_inc(s_zero, 1)
                    dve.wait_ge(s_w, 1)
                    nc.vector.tensor_copy(w_node[:, HEAD_COLS:], psW[:, 0:2 * NH])
        normalise(nc, "gat_ln", k, X, xnT, w_node[:], node, W + NH)

        src_table = nc.dram_tensor("src_table", [SRC_NODES, W], F32, kind="Internal").ap()
        dst_table = nc.dram_tensor("dst_table", [SRC_NODES, NH], F32, kind="Internal").ap()
        src_rows, dst_rows = sp.sb("src_rows", [P, TILES, W]), sp.sb("dst_rows", [P, TILES, NH])
        most, bound = sp.sb("most", [P, NH]), sp.sb("bound", [P, NH])
        last_row = sp.sb("last_row", [P, W])
        floor = sp.sb("floor", [P, TILES, NH])
        sums = sp.sb("sums", [P, W, TILES])
        iota_i, iota, iota1 = sp.sb("iota_i", [P, P], I32), sp.sb("iota", [P, P]), sp.sb("iota1", [P, TILES])
        CH = 8
        top8 = sp.sb("top8", [P, 2, CH])
        sidx, didx, part_i, tile_i, low_i, mark_i = (sp.sb(n, [P, 2, CH], I32) for n in (
            "sidx", "didx", "part_i", "tile_i", "low_i", "mark_i"))
        part_f, tile_f, mark_f = (sp.sb(n, [P, 2, CH]) for n in ("part_f", "tile_f", "mark_f"))
        rows, drows = sp.sb("rows", [P, 2, CH, W]), sp.sb("drows", [P, 2, CH, NH])
        z, y, w = (sp.sb(n, [P, 2, CH, NH]) for n in ("z", "y", "w"))
        val = sp.sb("val", [P, 2, CH, W])
        LO, HI = sp.sb("LO", [P, 2, CH, P]), sp.sb("HI", [P, 2, CH, TILES])
        spreadv = sp.sb("spreadv", [P, 4, W, TILES])
        zeros = sp.sb("zeros", [P, 512])
        ps = [sp.ps(f"acc{i}", [P, 512]) for i in range(3)]
        FB = 512 // TILES
        cutsf = [(0, FB), (FB, 2 * FB), (2 * FB, W)]
        (s_table, s_most, s_bound, s_last, s_iota, s_link, s_loop, s_zero, s_sum, s_mat) = (sp.sem(n) for n in (
            "table", "most", "bound", "last", "iota", "link", "loop", "zero", "sum", "mat"))
        s_idx, s_rows, s_z, s_w, s_val, s_used = (sp.sems(n) for n in ("idx", "rows", "z", "w", "val", "used"))
        s_packed = sp.sem("packed")
        s_tick = sp.sems("tick")
        tick = sp.sb("tick", [P, 2])
        STEPS = 2 * 20
        with nc.Block() as block:
            @block.sync
            def _(eng):
                tv = lambda t, n: t.rearrange("(b p c) f -> p b c f", p=P, c=GT)
                credit(eng, ((s_loop,), STEPS), ((s_mat,), 2 * CH), (s_used, CH),
                       (s_idx + s_z + s_w + s_val + s_tick, 1))
                eng.wait_ge(s_packed, 2)
                eng.dma_start(tv(src_table, W), src_rows[:].rearrange("p (b c) f -> p b c f", c=GT)).then_inc(s_table, 16)
                eng.dma_start(tv(dst_table, NH), dst_rows[:].rearrange("p (b c) f -> p b c f", c=GT)).then_inc(s_table, 16)
                eng.wait_ge(s_table, 32)
                eng.dma_start(last_row[:], src_table[LAST_NODE:LAST_NODE + 1, :].to_broadcast([P, W])).then_inc(s_last, 16)

            @block.gpsimd
            def _(pool):
                pool.iota(iota_i[:], [[1, P]], base=0, channel_multiplier=0).then_inc(s_iota, 1)
                pool.wait_ge(s_most, 1)
                pool.partition_all_reduce(bound[:], most[:], P, bass.bass_isa.ReduceOp.max).then_inc(s_bound, 1)
                pool.wait_ge(s_table, 32)
                turns = pool.value_load(cell[0:1, 0:1], min_val=2, max_val=LANE // (2 * CH) + 1)
                with pool.Fori(1, turns) as j:
                    for u in range(2):
                        pool.wait_ge(s_idx[u], j + 1)
                        pool.wait_ge(s_val[u], j)
                        pool.wait_ge(s_tick[u], j)
                        pool.tensor_tensor(tick[:, u:u + 1], k["ones"][:, 0:1], k["ones"][:, 0:1], ALU.mult).then_inc(s_tick[u], 1)
                        for i in range(CH):
                            pool.indirect_dma_start(out=rows[:, u, i, :], out_offset=None, in_=src_table,
                                                    in_offset=bass.IndirectOffsetOnAxis(ap=sidx[:, u, i:i + 1], axis=0)
                                                    ).then_inc(s_rows[u], 16)
                            pool.indirect_dma_start(out=drows[:, u, i, :], out_offset=None, in_=dst_table,
                                                    in_offset=bass.IndirectOffsetOnAxis(ap=didx[:, u, i:i + 1], axis=0)
                                                    ).then_inc(s_rows[u], 16)

            @block.scalar
            def _(act):
                turns = act.value_load(cell[0:1, 0:1], min_val=2, max_val=LANE // (2 * CH) + 1)
                with act.Fori(1, turns) as j:
                    for u in range(2):
                        act.wait_ge(s_z[u], j + 1)
                        nc.scalar.activation(w[:, u], z[:, u], ACT.Exp).then_inc(s_w[u], 1)

            @block.tensor
            def _(pe):
                mm = nc.tensor.matmul
                pe.wait_ge(s_zero, 1)
                for b, (f0, f1) in enumerate(cutsf):
                    mm(ps[b][:, 0:(f1 - f0) * TILES], zeros[:, 0:P], zeros[:, 0:(f1 - f0) * TILES], start=True, stop=False)
                turns = pe.value_load(cell[0:1, 0:1], min_val=2, max_val=LANE // (2 * CH) + 1)
                with pe.Fori(1, turns) as j:
                    for u in range(2):
                        for i in range(CH):
                            pe.wait_ge(s_mat, j * (2 * CH) + u * CH + i + 1)
                            for b, (f0, f1) in enumerate(cutsf):
                                last = mm(ps[b][:, 0:(f1 - f0) * TILES], LO[:, u, i, :],
                                          spreadv[:, i % 4, f0:f1, :].rearrange("p f t -> p (f t)"), start=False, stop=False)
                            last.then_inc(s_used[u], 1)
                for b, (f0, f1) in enumerate(cutsf):
                    last = mm(ps[b][:, 0:(f1 - f0) * TILES], zeros[:, 0:P], zeros[:, 0:(f1 - f0) * TILES], start=False, stop=True)
                last.then_inc(s_sum, 1)

            @block.vector
            def _(dve):
                v = nc.vector
                link = Steps(dve, s_link)
                v.tensor_copy(src_rows[:], node[:, :, 0:W]).then_inc(s_packed, 1)
                v.tensor_copy(dst_rows[:], node[:, :, W:W + NH]).then_inc(s_packed, 1)
                v.memset(zeros[:], 0.0).then_inc(s_zero, 1)
                v.tensor_reduce(most[:], node[:, :, HEAD_COLS:W].rearrange("p t h -> p h t"), AX, ALU.max).then_inc(s_most, 1)
                dve.wait_ge(s_iota, 1)
                v.tensor_copy(iota[:], iota_i[:])
                link.done(v.tensor_scalar(iota1[:], iota_i[:, 0:TILES], 1.0, None, ALU.add))
                dve.wait_ge(s_bound, 1)
                turns = dve.value_load(cell[0:1, 0:1], min_val=2, max_val=LANE // (2 * CH) + 1)
                with dve.Fori(1, turns) as j:
                    step = Steps(dve, s_loop, j * STEPS)
                    for u in range(2):
                        t8 = top8[:, u].bitcast(I32)
                        step.done(v.max(out=top8[:, u], in_=keys[:]))
                        step.mark(v.tensor_scalar(mark_i[:, u], t8, 29, None, ALU.logical_shift_right))
                        step.mark(v.match_replace(out=keys[:], in_to_replace=top8[:, u], in_values=keys[:], imm_value=0.0))
                        v.tensor_scalar(didx[:, u], t8, NODE_BITS, SRC_NODES - 1, ALU.logical_shift_right, ALU.bitwise_and)
                        v.tensor_scalar(sidx[:, u], t8, SRC_NODES - 1, None, ALU.bitwise_and).then_inc(s_idx[u], 1)
                        v.tensor_scalar(part_i[:, u], t8, NODE_BITS + 2, P - 1, ALU.logical_shift_right, ALU.bitwise_and)
                        step.done(v.tensor_scalar(low_i[:, u], t8, NODE_BITS, GT - 1, ALU.logical_shift_right, ALU.bitwise_and))
                        step.done(v.tensor_scalar(tile_i[:, u], t8, NODE_BITS + 9, BATCH - 1, ALU.logical_shift_right, ALU.bitwise_and))
                        step.mark(v.tensor_copy(part_f[:, u], part_i[:, u]))
                        step.mark(v.tensor_copy(mark_f[:, u], mark_i[:, u]))
                        step.done(v.scalar_tensor_tensor(tile_f[:, u], tile_i[:, u], float(GT), low_i[:, u], ALU.mult, ALU.add))
                        step.done(v.scalar_tensor_tensor(tile_f[:, u], tile_f[:, u], 1.0, mark_f[:, u], ALU.add, ALU.mult))
                        dve.wait_ge(s_used[u], j * CH)
                        step.mark(v.tensor_tensor(LO[:, u], iota[:].unsqueeze(1).to_broadcast([P, CH, P]),
                                                  spread(part_f[:, u], P), ALU.is_equal))
                        step.mark(v.tensor_tensor(HI[:, u], iota1[:].unsqueeze(1).to_broadcast([P, CH, TILES]),
                                                  spread(tile_f[:, u], TILES), ALU.is_equal))
                    for u in range(2):
                        dve.wait_ge(s_rows[u], j * (32 * CH))
                        step.mark(v.tensor_tensor(z[:, u], rows[:, u, :, HEAD_COLS:W], drows[:, u], ALU.add))
                        step.done(v.tensor_tensor(y[:, u], drows[:, u], bound[:].unsqueeze(1).to_broadcast([P, CH, NH]), ALU.add))
                        step.mark(v.scalar_tensor_tensor(z[:, u], z[:, u], 0.2, z[:, u], ALU.mult, ALU.max))
                        step.done(v.scalar_tensor_tensor(y[:, u], y[:, u], 0.2, y[:, u], ALU.mult, ALU.max))
                        v.tensor_tensor(z[:, u], z[:, u], y[:, u], ALU.subtract).then_inc(s_z[u], 1)
                    for u in range(2):
                        dve.wait_ge(s_w[u], j + 1)
                        step.mark(v.tensor_copy(val[:, u, :, HEAD_COLS:W], w[:, u]))
                        for h in range(NH):
                            cols = slice(h * NH, (h + 1) * NH)
                            ins = v.tensor_tensor(val[:, u, :, cols], rows[:, u, :, cols],
                                                  w[:, u, :, h:h + 1].to_broadcast([P, CH, NH]), ALU.mult)
                            step.mark(ins)
                        dve.wait_ge(s_loop, step.base + step.n)
                        v.tensor_copy(y[:, u], w[:, u]).then_inc(s_val[u], 1)
                        for i in range(CH):
                            if i >= 4:
                                dve.wait_ge(s_used[u], j * CH + i - 3)
                            else:
                                dve.wait_ge(s_used[1 - u], j * CH + u * (CH - 3 + i))
                            v.tensor_tensor(spreadv[:, i % 4], spread(val[:, u, i, :], TILES),
                                            HI[:, u, i, :].unsqueeze(1).to_broadcast([P, W, TILES]),
                                            ALU.mult).then_inc(s_mat, 1)
                    assert step.n == STEPS, step.n
                dve.wait_ge(s_sum, 1)
                for b, (f0, f1) in enumerate(cutsf):
                    v.tensor_copy(sums[:, f0:f1, :].rearrange("p f t -> p (f t)"), ps[b][:, 0:(f1 - f0) * TILES])

        def rows3(ap, n=TILES):
            return ap.unsqueeze(1).to_broadcast([P, n, ap.shape[-1]])
        own, far, lead = (sp.sb(n, [P, TILES, NH]) for n in ("own", "far", "lead"))
        eown, efar = sp.sb("eown", [P, TILES, NH]), sp.sb("efar", [P, TILES, NH])
        agg, tmp = sp.sb("agg", [P, TILES, HEAD_COLS]), sp.sb("tmp", [P, TILES, HEAD_COLS])
        dens = sp.sb("dens", [P, TILES, NH])
        b_gat, gamma, beta = (sp.sb(n, [P, HEAD_COLS]) for n in ("b_gat", "gamma", "beta"))
        m64, v64, r64, half = (sp.sb(n, [P, TILES]) for n in ("m64", "v64", "r64", "half"))
        scores = sp.sb("scores", [P, TILES, GAT_EXPERTS])
        f_load, f_z, f_e, f_var, f_r, f_link = (sp.sem(n) for n in ("f_load", "f_z", "f_e", "f_var", "f_r", "f_link"))
        with nc.Block() as block:
            @block.sync
            def _(eng):
                eng.wait_ge(s_last, 16)
                for dst, name in ((b_gat, "b_gat"), (gamma, "ln_gamma"), (beta, "ln_beta")):
                    eng.dma_start(dst[:], A[name].unsqueeze(0).to_broadcast([P, HEAD_COLS])).then_inc(f_load, 16)

            @block.scalar
            def _(act):
                act.wait_ge(f_z, 1)
                nc.scalar.activation(eown[:], own[:], ACT.Exp)
                nc.scalar.activation(efar[:], far[:], ACT.Exp).then_inc(f_e, 1)

            @block.gpsimd
            def _(pool):
                pool.memset(half[:], -0.5).then_inc(f_r, 1)
                pool.wait_ge(f_r, 1)
                pool.wait_ge(f_var, 1)
                pool.tensor_tensor(r64[:], v64[:], half[:], ALU.pow).then_inc(f_r, 1)

            @block.vector
            def _(dve):
                v = nc.vector
                L = Steps(dve, f_link)
                do = L.done
                a_src, a_dst = node[:, :, HEAD_COLS:W], node[:, :, W:W + NH]
                dve.wait_ge(s_last, 16)
                dve.wait_ge(f_load, 48)
                do(v.tensor_tensor(lead[:], a_dst, rows3(bound[:]), ALU.add))
                do(v.scalar_tensor_tensor(floor[:], lead[:], 0.2, lead[:], ALU.mult, ALU.max))
                do(v.tensor_tensor(own[:], a_src, a_dst, ALU.add))
                do(v.scalar_tensor_tensor(lead[:], own[:], 0.2, own[:], ALU.mult, ALU.max))
                do(v.tensor_tensor(own[:], lead[:], floor[:], ALU.subtract))
                do(v.tensor_tensor(far[:], a_dst, rows3(last_row[:, HEAD_COLS:W]), ALU.add))
                do(v.scalar_tensor_tensor(lead[:], far[:], 0.2, far[:], ALU.mult, ALU.max))
                v.tensor_tensor(far[:], lead[:], floor[:], ALU.subtract).then_inc(f_z, 1)
                dve.wait_ge(f_e, 1)
                do(v.tensor_tensor(efar[:], efar[:], spread(far_count[:], NH), ALU.mult))
                do(v.tensor_tensor(dens[:], eown[:], efar[:], ALU.add))
                do(v.tensor_tensor(dens[:], dens[:], sums[:, HEAD_COLS:W, :].rearrange("p f t -> p t f"), ALU.add))
                do(v.tensor_scalar(dens[:], dens[:], 1e-37, None, ALU.max))
                do(v.reciprocal(dens[:], dens[:]))
                for h in range(NH):
                    c = slice(h * NH, (h + 1) * NH)
                    L.mark(v.tensor_tensor(agg[:, :, c], node[:, :, c], spread(eown[:, :, h], NH), ALU.mult))
                    L.mark(v.tensor_tensor(tmp[:, :, c], rows3(last_row[:, c]), spread(efar[:, :, h], NH), ALU.mult))
                dve.wait_ge(f_link, L.n)
                do(v.tensor_tensor(agg[:], agg[:], tmp[:], ALU.add))
                do(v.tensor_tensor(agg[:], agg[:], sums[:, 0:HEAD_COLS, :].rearrange("p f t -> p t f"), ALU.add))
                for h in range(NH):
                    c = slice(h * NH, (h + 1) * NH)
                    L.mark(v.tensor_tensor(tmp[:, :, c], agg[:, :, c], spread(dens[:, :, h], NH), ALU.mult))
                dve.wait_ge(f_link, L.n)
                do(v.tensor_tensor(agg[:], tmp[:], rows3(b_gat[:]), ALU.add))
                do(v.tensor_reduce(m64[:], agg[:], AX, ALU.add))
                do(v.tensor_scalar(m64[:], m64[:], 1.0 / HEAD_COLS, None, ALU.mult))
                do(v.tensor_tensor(agg[:], agg[:], spread(m64[:], HEAD_COLS), ALU.subtract))
                do(v.tensor_tensor(tmp[:], agg[:], agg[:], ALU.mult))
                do(v.tensor_reduce(m64[:], tmp[:], AX, ALU.add))
                v.tensor_scalar(v64[:], m64[:], 1.0 / HEAD_COLS, LN_EPS, ALU.mult, ALU.add).then_inc(f_var, 1)
                dve.wait_ge(f_r, 2)
                do(v.tensor_tensor(agg[:], agg[:], spread(r64[:], HEAD_COLS), ALU.mult))
                do(v.tensor_tensor(agg[:], agg[:], rows3(gamma[:]), ALU.mult))
                do(v.tensor_tensor(agg[:], agg[:], rows3(beta[:]), ALU.add))
                do(v.tensor_reduce(scores[:], agg[:].rearrange("p t (h e) -> p t e h", h=NH), AX, ALU.add))
                do(v.tensor_scalar(scores[:], scores[:], 1.0 / NH, None, ALU.mult))
        gates_of(nc, "gat_gate", scores[:], GAT_EXPERTS, 0.0, parts)


def second_ffn_stage(nc, k, X, xnT, A, parts):
    E, hid = GAT_EXPERTS, 2 * C
    cuts = [(0, P), (P, P)]
    with ExitStack() as ctx:
        sp = Space(nc, ctx, "ffn")
        w1 = sp.sb("w1", [P, E * hid])
        w2 = sp.sb("w2", [P, E * len(cuts), C])
        b1 = sp.sb("b1", [P, E * len(cuts)])
        b2, rest = sp.sb("b2", [3 * E, C]), sp.sb("rest", [3 * E, 2, C])
        b2_parts = sp.sb("b2_parts", [3 * E, 3, C], BF16)
        load_now(nc, "ffn_b2", [(b2[part * E:(part + 1) * E, :], A["b2"]) for part in range(3)])
        s_split = sp.sem("split")
        with nc.Block() as block:
            @block.vector
            def _(dve):
                v = nc.vector
                link = Steps(dve, s_split)
                link.done(v.tensor_copy(b2_parts[:, 0, :], b2[:]))
                link.done(v.tensor_tensor(rest[:, 0, :], b2[:], b2_parts[:, 0, :], ALU.subtract))
                link.done(v.tensor_copy(b2_parts[:, 1, :], rest[:, 0, :]))
                link.done(v.tensor_tensor(rest[:, 1, :], rest[:, 0, :], b2_parts[:, 1, :], ALU.subtract))
                v.tensor_copy(b2_parts[:, 2, :], rest[:, 1, :])
        pairs = [(w1[:].rearrange("c (e h) -> c e h", e=E), A["W1"].rearrange("e c h -> c e h")),
                 (w2[:], A["W2"].rearrange("e (k p) c -> p (e k) c", p=P)),
                 (b1[:], A["b1"])]
        experts(nc, "ffn_mix", k, X, xnT, parts, E, cuts, (w1, None), w2, Loads(pairs),
                (ACT.Gelu, lambda i: b1[:, i:i + 1]), b2=b2_parts)


def program(nc, A, out):
    rows = lambda ap: ap.rearrange("(b p c) d -> p b c d", p=P, c=GT)
    with ExitStack() as ctx:
        k = constants(nc, ctx)
        sp = Space(nc, ctx, "all")
        X = sp.sb("X", [P, TILES, C])
        x4 = X[:].rearrange("p (b c) d -> p b c d", c=GT)
        load_now(nc, "x_in", [(x4, rows(A["x"]))])
        edge_attention_stage(nc, k, X, A)
        xnT = sp.sb("xnT", [C, TOKENS])
        moe_stage(nc, k, X, xnT, A)
        dense_attention_stage(nc, k, X, xnT, A)
        parts = sp.sb("gate_parts", [P, TILES, 3, GAT_EXPERTS], BF16)
        with ExitStack() as ctx2:
            s2 = Space(nc, ctx2, "graph")
            keys, far_count, cell = s2.sb("keys", [P, LANE]), s2.sb("far_count", [P, TILES]), s2.sb("cell", [P, 1], I32)
            edge_keys_stage(nc, k, A, keys, far_count, cell)
            gat_stage(nc, k, X, xnT, A, keys, far_count, cell, parts)
        second_ffn_stage(nc, k, X, xnT, A, parts)
        load_now(nc, "x_out", [(rows(out), x4)])


def kernel(**inputs):
    import concourse.bacc as bacc
    from concourse.bass_utils import run_bass_kernel_spmd

    def plain(name):
        return np.ascontiguousarray(inputs[name])

    def turned(name, *order):
        return np.ascontiguousarray(np.transpose(inputs[name], order))

    hid = inputs["L0_ffn_w1"].shape[1]
    arrays = {
        "x": plain("x").reshape(TOKENS, C), "adj": plain("adj"),
        "W_linT": turned("L0_gnn_W_lin", 1, 0), "W_valT": turned("L0_gnn_W_val", 1, 0),
        "W_outT": turned("L0_gnn_W_out", 1, 0), "a": plain("L0_gnn_a"),
        "src": plain("L0_gnn_src"), "dst": plain("L0_gnn_dst"),
        "router_wT": turned("L0_ffn_router_w", 1, 0),
        "w1T": turned("L0_ffn_w1", 2, 0, 1).reshape(C, -1), "w3T": turned("L0_ffn_w3", 2, 0, 1).reshape(C, -1),
        "w2T": turned("L0_ffn_w2", 0, 2, 1),
        **{n: plain("L1_gnn_" + n) for n in ("Wq", "Wk", "Wo", "bq", "bk", "bv", "bo")},
        "WvT": turned("L1_gnn_Wv", 1, 0),
        "alpha": plain("L1_gnn_alpha").reshape(1), "gamma": plain("L1_gnn_gamma").reshape(1),
        "W_gat": plain("L1_ffn_W_gat"), "W_gatT": turned("L1_ffn_W_gat", 1, 0),
        **{n: plain("L1_ffn_" + n) for n in ("att_src", "att_dst", "b_gat", "ln_gamma", "ln_beta", "W1", "W2", "b2", "edge_index")},
        "b1": np.ascontiguousarray(np.transpose(np.reshape(inputs["L1_ffn_b1"], (-1, P)))),
    }
    nc = bacc.Bacc("TRN2", target_bir_lowering=False, num_devices=1)
    A = {n: nc.dram_tensor(f"in_{n}", a.shape, mybir.dt.from_np(a.dtype), kind="ExternalInput").ap()
         for n, a in arrays.items()}
    out = nc.dram_tensor("out_x", (TOKENS, C), F32, kind="ExternalOutput").ap()
    program(nc, A, out)
    r = run_bass_kernel_spmd(nc, [{f"in_{n}": a for n, a in arrays.items()}], core_ids=[0])
    return r.results[0]["out_x"].reshape(BATCH, NODES, C)
```

```python
from contextlib import ExitStack

import numpy as np

import concourse.bass as bass
from concourse import mybir

ALU = mybir.AluOpType
ACT = mybir.ActivationFunctionType
AX = mybir.AxisListType.X
F32 = mybir.dt.float32
BF16 = mybir.dt.bfloat16
I32 = mybir.dt.int32
P = 128
BATCH, NODES, C = 16, 512, 128
TOKENS = BATCH * NODES
TILES = TOKENS // P
GT = NODES // P
GROUPS = BATCH
PAIRS = GROUPS // 2
LN_EPS = 1e-5
SRC_NODES = TOKENS


class Steps:

    def __init__(self, eng, sem, base=0):
        self.eng, self.sem, self.base, self.n = eng, sem, base, 0

    def mark(self, ins):
        self.n += 1
        ins.then_inc(self.sem, 1)

    def done(self, ins):
        self.n += 1
        ins.then_inc(self.sem, 1)
        self.eng.wait_ge(self.sem, self.base + self.n)


def credit(eng, *counts):
    for sems, n in counts:
        for sem in sems:
            eng.sem_inc(sem, n)


def spread(ap, n):
    return ap.unsqueeze(2).to_broadcast([*ap.shape, n])


class Space:

    def __init__(self, nc, ctx, stage):
        self.nc, self.ctx, self.stage = nc, ctx, stage
        self.taken = []
        ctx.callback(self.release)

    def release(self):
        if self.taken:
            self.nc.clear_and_free_semaphores(self.taken)
            self.nc.all_engine_barrier()

    def sb(self, name, shape, dt=F32):
        return self.ctx.enter_context(self.nc.sbuf_tensor(f"{self.stage}_{name}", shape, dt))

    def ps(self, name, shape, dt=F32):
        return self.ctx.enter_context(self.nc.psum_tensor(f"{self.stage}_{name}", shape, dt))

    def sem(self, name):
        self.taken.append(self.nc.alloc_semaphore(f"{self.stage}_{name}"))
        return self.taken[-1]

    def sems(self, name, n=2):
        return [self.sem(f"{name}{i}") for i in range(n)]


def constants(nc, ctx):
    sp = Space(nc, ctx, "const")
    ident = sp.sb("ident", [P, P])
    ident16 = sp.sb("ident16", [P, P], BF16)
    minus_half = sp.sb("minus_half", [P, GT])
    ones = sp.sb("ones", [P, P])
    cleared, drawn = sp.sem("cleared"), sp.sem("drawn")
    with nc.Block() as block:
        @block.gpsimd
        def _(pool):
            pool.memset(ident[:], 0.0).then_inc(cleared, 1)
            pool.memset(minus_half[:], -0.5)
            pool.memset(ones[:], 1.0)
            pool.wait_ge(cleared, 1)
            pool.affine_select(out=ident[:], in_=ident[:], compare_op=ALU.not_equal, fill=1.0, base=0,
                               pattern=[[-1, P]], channel_multiplier=1).then_inc(drawn, 1)
            pool.wait_ge(drawn, 1)
            pool.tensor_copy(ident16[:], ident[:])
    return {"ident": ident, "ident16": ident16, "minus_half": minus_half, "ones": ones}


def normalise(nc, stage, k, X, xnT, w_small, small, width):
    with ExitStack() as ctx:
        sp = Space(nc, ctx, stage)
        total, mean = sp.sb("total", [P, 2, GT]), sp.sb("mean", [P, 2, GT])
        centred, squares = sp.sb("centred", [P, 2, GT, C]), sp.sb("squares", [P, 2, GT, C])
        sqsum, var, rstd = (sp.sb(n, [P, 2, GT]) for n in ("sqsum", "var", "rstd"))
        xn, xT = sp.sb("xn", [P, 2, GT, C]), sp.sb("xT", [P, 2, NODES])
        psT = sp.ps("psT", [P, 2, 512])
        psS = sp.ps("psS", [P, 2, 512])
        s_link = sp.sem("link")
        s_centred, s_squared, s_var, s_rstd = (sp.sems(n) for n in ("s_centred", "s_squared", "s_var", "s_rstd"))
        s_normed, s_turned, s_xT, s_small, s_kept = (
            sp.sems(n) for n in ("s_normed", "s_turned", "s_xT", "s_small", "s_kept"))
        with nc.Block() as block:
            @block.sync
            def _(eng):
                credit(eng, ((s_link,), 6), (s_centred + s_squared + s_var + s_rstd, 1),
                       (s_normed + s_turned + s_xT + s_small + s_kept, 1))

            @block.vector
            def _(dve):
                with dve.Fori(1, PAIRS + 1) as j:
                    link = Steps(dve, s_link, j * 6)
                    for u in range(2):
                        x4 = X[:, bass.ds((2 * (j - 1) + u) * GT, GT), :]
                        link.done(nc.vector.tensor_reduce(total[:, u], x4, AX, ALU.add))
                        link.done(nc.vector.tensor_scalar(mean[:, u], total[:, u], 1.0 / C, None, ALU.mult))
                        nc.vector.tensor_tensor(centred[:, u], x4, spread(mean[:, u], C),
                                                ALU.subtract).then_inc(s_centred[u], 1)
                    for u in range(2):
                        dve.wait_ge(s_squared[u], j + 1)
                        link.done(nc.vector.tensor_reduce(sqsum[:, u], squares[:, u], AX, ALU.add))
                        nc.vector.tensor_scalar(var[:, u], sqsum[:, u], 1.0 / C, LN_EPS, ALU.mult,
                                                ALU.add).then_inc(s_var[u], 1)
                    for u in range(2):
                        dve.wait_ge(s_rstd[u], j + 1)
                        dve.wait_ge(s_turned[u], j)
                        nc.vector.tensor_tensor(xn[:, u], centred[:, u], spread(rstd[:, u], C),
                                                ALU.mult).then_inc(s_normed[u], 1)

            @block.gpsimd
            def _(pool):
                with pool.Fori(1, PAIRS + 1) as j:
                    for u in range(2):
                        pool.wait_ge(s_centred[u], j + 1)
                        pool.tensor_tensor(squares[:, u], centred[:, u], centred[:, u],
                                           ALU.mult).then_inc(s_squared[u], 1)
                    for u in range(2):
                        pool.wait_ge(s_var[u], j + 1)
                        pool.tensor_tensor(rstd[:, u], var[:, u], k["minus_half"][:],
                                           ALU.pow).then_inc(s_rstd[u], 1)

            @block.tensor
            def _(pe):
                with pe.Fori(1, PAIRS + 1) as j:
                    for u in range(2):
                        pe.wait_ge(s_normed[u], j + 1)
                        pe.wait_ge(s_xT[u], j)
                        for t in range(GT):
                            last = nc.tensor.transpose(psT[:, u, t * P:(t + 1) * P], xn[:, u, t, :], k["ident"][:])
                        last.then_inc(s_turned[u], 1)
                    for u in range(2):
                        if w_small is None:
                            continue
                        pe.wait_ge(s_xT[u], j + 1)
                        pe.wait_ge(s_kept[u], j)
                        for t in range(GT):
                            last = nc.tensor.matmul(psS[:, u, t * width:(t + 1) * width], xT[:, u, t * P:(t + 1) * P],
                                                    w_small, start=True, stop=True)
                        last.then_inc(s_small[u], 1)

            @block.scalar
            def _(act):
                with act.Fori(1, PAIRS + 1) as j:
                    for u in range(2):
                        g = 2 * (j - 1) + u
                        act.wait_ge(s_turned[u], j + 1)
                        if w_small is not None:
                            act.wait_ge(s_small[u], j)
                            nc.scalar.copy(xT[:, u, :], psT[:, u, :])
                        nc.scalar.copy(xnT[:, bass.ds(g * NODES, NODES)], psT[:, u, :]).then_inc(s_xT[u], 1)
                    for u in range(2):
                        if w_small is None:
                            continue
                        g = 2 * (j - 1) + u
                        act.wait_ge(s_small[u], j + 1)
                        nc.scalar.copy(small[:, bass.ds(g * GT, GT), :],
                                       psS[:, u, 0:GT * width].rearrange("p (t w) -> p t w", t=GT)).then_inc(s_kept[u], 1)


def top_two(dve, link, sp, logits, rank, d, both, m, n):
    eq, one = sp.sb("eq", [P, TILES, n]), sp.sb("one", [P, TILES, n])
    place = sp.sb("place", [P, TILES])
    rank_b = rank.unsqueeze(1).to_broadcast([P, TILES, n])
    link.done(dve.tensor_reduce(m[:], logits, AX, ALU.max))
    link.done(dve.tensor_tensor(d[:], logits, spread(m[:], n), ALU.subtract))
    link.done(dve.scalar_tensor_tensor(eq[:], d[:], 0.0, rank_b, ALU.is_equal, ALU.mult))
    link.done(dve.tensor_reduce(place[:], eq[:], AX, ALU.max))
    link.done(dve.tensor_tensor(both[:], rank_b, spread(place[:], n), ALU.is_equal))
    link.done(dve.scalar_tensor_tensor(one[:], both[:], -1e30, d[:], ALU.mult, ALU.add))
    link.done(dve.tensor_reduce(m[:], one[:], AX, ALU.max))
    link.done(dve.tensor_tensor(eq[:], one[:], spread(m[:], n), ALU.is_equal))
    link.done(dve.tensor_tensor(eq[:], eq[:], rank_b, ALU.mult))
    link.done(dve.tensor_reduce(place[:], eq[:], AX, ALU.max))
    link.done(dve.tensor_tensor(eq[:], rank_b, spread(place[:], n), ALU.is_equal))
    link.done(dve.tensor_tensor(both[:], both[:], eq[:], ALU.add))


def gates_of(nc, stage, logits, n, eps, gate_parts):
    with ExitStack() as ctx:
        sp = Space(nc, ctx, stage)
        rank_i, rank = sp.sb("rank_i", [P, n], I32), sp.sb("rank", [P, n])
        d, both, e, g, rest = (sp.sb(x, [P, TILES, n]) for x in ("d", "both", "e", "g", "rest"))
        m, s = sp.sb("m", [P, TILES]), sp.sb("s", [P, TILES])
        s_rank, s_link, s_d, s_e = (sp.sem(x) for x in ("s_rank", "s_link", "s_d", "s_e"))
        with nc.Block() as block:
            @block.gpsimd
            def _(pool):
                pool.iota(rank_i[:], [[-1, n]], base=n, channel_multiplier=0).then_inc(s_rank, 1)

            @block.scalar
            def _(act):
                act.wait_ge(s_d, 1)
                nc.scalar.activation(e[:], d[:], ACT.Exp).then_inc(s_e, 1)

            @block.vector
            def _(dve):
                link = Steps(dve, s_link)
                dve.wait_ge(s_rank, 1)
                link.done(nc.vector.tensor_copy(rank[:], rank_i[:]))
                top_two(nc.vector, link, sp, logits, rank[:], d, both, m, n)
                nc.vector.tensor_copy(s[:], m[:]).then_inc(s_d, 1)
                dve.wait_ge(s_e, 1)
                dve.wait_ge(s_d, 1)
                link.done(nc.vector.tensor_reduce(s[:], e[:], AX, ALU.add))
                link.done(nc.vector.reciprocal(m[:], s[:]))
                link.done(nc.vector.tensor_tensor(g[:], e[:], spread(m[:], n), ALU.mult))
                link.done(nc.vector.tensor_tensor(g[:], g[:], both[:], ALU.mult))
                link.done(nc.vector.tensor_reduce(s[:], g[:], AX, ALU.add))
                link.done(nc.vector.tensor_scalar(s[:], s[:], eps, None, ALU.add))
                link.done(nc.vector.reciprocal(m[:], s[:]))
                link.done(nc.vector.tensor_tensor(g[:], g[:], spread(m[:], n), ALU.mult))
                link.done(nc.vector.tensor_copy(gate_parts[:, :, 0, :], g[:]))
                link.done(nc.vector.tensor_tensor(rest[:], g[:], gate_parts[:, :, 0, :], ALU.subtract))
                link.done(nc.vector.tensor_copy(gate_parts[:, :, 1, :], rest[:]))
                link.done(nc.vector.tensor_tensor(g[:], rest[:], gate_parts[:, :, 1, :], ALU.subtract))
                nc.vector.tensor_copy(gate_parts[:, :, 2, :], g[:])


def experts(nc, stage, k, X, xnT, gate_parts, n, cuts, first, second, load, act_func, b2=None, tally=None):
    w1, w3 = first
    hidden = sum(c for _, c in cuts)
    K = n * len(cuts)
    GB = 1 if tally else 2
    with ExitStack() as ctx:
        sp = Space(nc, ctx, stage)
        picks = sp.sb("picks", [3 * n, n, P], BF16)
        picks_f = sp.sb("picks_f", [3 * n, n, P])
        gate_now = sp.sb("gate_now", [P, 2, GT, 3 * n], BF16)
        gT = sp.sb("gT", [3 * n, 2, NODES], BF16)
        S, T, H = (sp.sb(x, [P, 2, NODES]) for x in ("S", "T", "H"))
        yT = sp.sb("yT", [P, 2, NODES])
        ps1 = sp.ps("ps1", [P, 2, 512])
        ps3 = sp.ps("ps3", [P, 2, 512]) if w3 is not None else None
        psG = sp.ps("psG", [P, GB, 512])
        acc = sp.ps("acc", [P, 512])
        psX = sp.ps("psX", [P, 512])
        psX16 = psX[:, 0:256].bitcast(BF16)
        (s_load, s_picks0, s_picks, s_up, s_S, s_gate, s_T, s_H, s_down) = (
            sp.sem(x) for x in ("s_load", "s_picks0", "s_picks", "s_up", "s_S", "s_gate", "s_T", "s_H", "s_down"))
        if w3 is None:
            s_H = s_T
        s_now, s_gturn, s_gT, s_acc, s_y, s_yturn, s_added = (
            sp.sems(x) for x in ("s_now", "s_gturn", "s_gT", "s_acc", "s_y", "s_yturn", "s_added"))
        with nc.Block() as block:
            @block.sync
            def _(sp_eng):
                own_H = (s_H,) if w3 is not None else ()
                credit(sp_eng, ((s_up, s_S, s_T, s_down) + own_H, 2 * K), ((s_gate,), 2 * n),
                       (s_now + s_gturn + s_gT + s_acc + s_y + s_yturn + s_added, 1))
                if tally:
                    tally.start(sp_eng)
                loads = load(sp_eng, s_load)
                sp_eng.wait_ge(s_load, loads)

            @block.gpsimd
            def _(pool):
                pool.memset(picks_f[:], 0.0).then_inc(s_picks0, 1)
                for part in range(3):
                    pool.wait_ge(s_picks0, part + 1)
                    pool.affine_select(out=picks_f[:], in_=picks_f[:], compare_op=ALU.not_equal, fill=1.0,
                                       base=-part * n, pattern=[[-1, n], [0, P]],
                                       channel_multiplier=1).then_inc(s_picks0, 1)
                pool.wait_ge(s_picks0, 4)
                pool.tensor_copy(picks[:], picks_f[:]).then_inc(s_picks, 1)
                with pool.Fori(1, PAIRS + 1) as j:
                    for u in range(2):
                        g = 2 * (j - 1) + u
                        pool.wait_ge(s_gturn[u], j)
                        pool.tensor_copy(gate_now[:, u], gate_parts[:, bass.ds(g * GT, GT), :, :]
                                         .rearrange("p t a e -> p t (a e)")).then_inc(s_now[u], 1)

            @block.tensor
            def _(pe):
                pe.wait_ge(s_load, load.total)
                pe.wait_ge(s_picks, 1)
                if tally:
                    tally.open()
                with pe.Fori(1, PAIRS + 1) as j:
                    for u in range(2):
                        g = 2 * (j - 1) + u
                        xg = xnT[:, bass.ds(g * NODES, NODES)]
                        at = lambda per, i: j * (2 * per) + max(u * per + i, 0)
                        pe.wait_ge(s_now[u], j + 1)
                        pe.wait_ge(s_added[1 - u], j + u)
                        for t in range(GT):
                            last = nc.tensor.transpose(psX16[0:3 * n, t * P:(t + 1) * P], gate_now[:, u, t, :],
                                                       k["ident16"][:])
                        last.then_inc(s_gturn[u], 1)
                        pe.wait_ge(s_gT[u], j + 1)

                        def gates(i):
                            e = i // len(cuts)
                            pe.wait_ge(s_T, at(K, i - (GB - 1) * len(cuts)))
                            nc.tensor.matmul(psG[:, e % GB, :], picks[:, e, :], gT[:, u, :], start=True,
                                             stop=True).then_inc(s_gate, 1)

                        def up(i):
                            e, (c0, rows) = i // len(cuts), cuts[i % len(cuts)]
                            col = e * hidden + c0
                            pe.wait_ge(s_S, at(K, i - 1))
                            last = nc.tensor.matmul(ps1[0:rows, i % 2, :], w1[:, col:col + rows], xg, start=True, stop=True)
                            if w3 is not None:
                                pe.wait_ge(s_H, at(K, i - 1))
                                last = nc.tensor.matmul(ps3[0:rows, i % 2, :], w3[:, col:col + rows], xg, start=True,
                                                        stop=True)
                            last.then_inc(s_up, 1)

                        def down(i):
                            rows = cuts[i % len(cuts)][1]
                            pe.wait_ge(s_H, at(K, i + 1))
                            if i == 0:
                                pe.wait_ge(s_y[1 - u], j + u)
                            last = nc.tensor.matmul(acc[:], second[0:rows, i, :], H[0:rows, i % 2, :],
                                                    start=(i == 0), stop=(i == K - 1 and b2 is None))
                            if i == K - 1 and b2 is not None:
                                for q in range(3):
                                    last = nc.tensor.matmul(acc[:], b2[:, q, :], gT[:, u, :], start=False, stop=(q == 2))
                            last.then_inc(s_down, 1)

                        for i in range(K):
                            up(i)
                            if i:
                                down(i - 1)
                            if i % len(cuts) == 0:
                                gates(i)
                            if tally:
                                tally.add(pe, j, u, i - 1)
                        down(K - 1)
                        if tally:
                            tally.add(pe, j, u, K - 1)
                        pe.wait_ge(s_y[u], j + 1)
                        for t in range(GT):
                            last = nc.tensor.transpose(psX[:, t * P:(t + 1) * P], yT[:, u, t * P:(t + 1) * P],
                                                       k["ident"][:])
                        last.then_inc(s_yturn[u], 1)
                if tally:
                    tally.close()

            @block.scalar
            def _(act):
                with act.Fori(1, PAIRS + 1) as j:
                    for u in range(2):
                        at = lambda per, i: j * (2 * per) + max(u * per + i, 0)
                        act.wait_ge(s_gturn[u], j + 1)
                        nc.scalar.copy(gT[:, u, :], psX16[0:3 * n, :]).then_inc(s_gT[u], 1)
                        for i in range(K):
                            e, rows = i // len(cuts), cuts[i % len(cuts)][1]
                            act.wait_ge(s_up, at(K, i + 1))
                            act.wait_ge(s_T, at(K, i - 1))
                            b = act_func[1](i)
                            kw = {"bias": b} if b is not None else {}
                            nc.scalar.activation(S[0:rows, i % 2, :], ps1[0:rows, i % 2, :], act_func[0],
                                                 **kw).then_inc(s_S, 1)
                        act.wait_ge(s_down, at(K, K))
                        nc.scalar.copy(yT[:, u, :], acc[:]).then_inc(s_y[u], 1)

            @block.vector
            def _(dve):
                with dve.Fori(1, PAIRS + 1) as j:
                    for u in range(2):
                        g = 2 * (j - 1) + u
                        at = lambda per, i: j * (2 * per) + max(u * per + i, 0)
                        for i in range(K):
                            e, rows = i // len(cuts), cuts[i % len(cuts)][1]
                            dve.wait_ge(s_gate, at(n, e + 1))
                            dve.wait_ge(s_S, at(K, i + 1))
                            dve.wait_ge(s_down, at(K, i - 1))
                            out = T if w3 is not None else H
                            ins = nc.vector.tensor_tensor(out[0:rows, i % 2, :], S[0:rows, i % 2, :],
                                                          psG[0:rows, e % GB, :], ALU.mult)
                            ins.then_inc(s_T, 1)
                            if w3 is not None:
                                dve.wait_ge(s_T, at(K, i + 1))
                                nc.vector.tensor_tensor(H[0:rows, i % 2, :], T[0:rows, i % 2, :],
                                                        ps3[0:rows, i % 2, :], ALU.mult).then_inc(s_H, 1)
                            if tally:
                                tally.make(dve, j, u, i)
                        dve.wait_ge(s_yturn[u], j + 1)
                        x4 = X[:, bass.ds(g * GT, GT), :]
                        nc.vector.tensor_tensor(x4, x4, psX[:].rearrange("p (t c) -> p t c", t=GT),
                                                ALU.add).then_inc(s_added[u], 1)
                if tally:
                    tally.read(dve)


class Loads:

    def __init__(self, pairs):
        self.pairs = pairs
        self.total = 16 * len(pairs)

    def __call__(self, eng, sem):
        for dst, src in self.pairs:
            eng.dma_start(dst, src).then_inc(sem, 16)
        return self.total


def load_now(nc, name, pairs):
    with ExitStack() as ctx:
        sem = Space(nc, ctx, name).sem("loaded")
        block = ctx.enter_context(nc.Block())

        @block.sync
        def _(sp_eng):
            for dst, src in pairs:
                sp_eng.dma_start(dst, src).then_inc(sem, 16)
            sp_eng.wait_ge(sem, 16 * len(pairs))


def moe_stage(nc, k, X, xnT, A, tally_of):
    E, hid = 8, 341
    cuts = [(0, 128), (128, 128), (256, hid - 256)]
    with ExitStack() as ctx:
        sp = Space(nc, ctx, "moe")
        router = sp.sb("router", [P, E])
        logits = sp.sb("logits", [P, TILES, E])
        parts = sp.sb("parts", [P, TILES, 3, E], BF16)
        w1, w3 = sp.sb("w1", [P, E * hid]), sp.sb("w3", [P, E * hid])
        w2 = sp.sb("w2", [P, E * len(cuts), C])
        load_now(nc, "moe_first", [(router[:], A["router_wT"])])
        normalise(nc, "moe_ln", k, X, xnT, router[:], logits, E)
        gates_of(nc, "moe_gate", logits[:], E, 1e-9, parts)
        w2v = w2[:].rearrange("p (e c) d -> p e c d", c=len(cuts))
        pairs = [(w1[:], A["w1T"]), (w3[:], A["w3T"])]
        for c, (c0, r) in enumerate(cuts):
            pairs.append((w2v[0:r, :, c, :], A["w2T"][:, c0:c0 + r, :].rearrange("e h d -> h e d")))
        with ExitStack() as ctx2:
            tally = tally_of(Space(nc, ctx2, "tally"), E * len(cuts))
            experts(nc, "moe_mix", k, X, xnT, parts, E, cuts, (w1, w3), w2, Loads(pairs), (ACT.Silu, lambda i: None),
                    tally=tally)


def edge_attention_stage(nc, k, X, A):
    EDGES, HEADS, DH = 256, 4, 32
    EC = EDGES // P
    with ExitStack() as ctx:
        sp = Space(nc, ctx, "edge")
        W_linT, W_valT, W_outT = (sp.sb(n, [C, C]) for n in ("W_linT", "W_valT", "W_outT"))
        a_blocks = sp.sb("a_blocks", [C, HEADS])
        a_wide = sp.sb("a_wide", [C, HEADS, P])
        src_col_i, dst_col_i = sp.sb("src_col_i", [P, EC], I32), sp.sb("dst_col_i", [P, EC], I32)
        src_row_i, dst_row_i = sp.sb("src_row_i", [P, EDGES], I32), sp.sb("dst_row_i", [P, EDGES], I32)
        src_col, dst_col = sp.sb("src_col", [P, EC]), sp.sb("dst_col", [P, EC])
        src_row, dst_row = sp.sb("src_row", [P, EDGES]), sp.sb("dst_row", [P, EDGES])
        node_i, node = sp.sb("node_i", [P, GT], I32), sp.sb("node", [P, GT])
        nodes_i, nodes = sp.sb("nodes_i", [P, NODES], I32), sp.sb("nodes", [P, NODES])
        pick = sp.sb("pick", [P, GT, 2 * EDGES])
        place = sp.sb("place", [P, EC, NODES])
        same = sp.sb("same", [P, EC, EDGES])
        place_idx, place_idx_i = sp.sb("place_idx", [P, EC]), sp.sb("place_idx_i", [P, EC], I32)
        A0, logA = sp.sb("A0", [P, EC]), sp.sb("logA", [P, EC])
        diag = sp.sb("diag", [P, EC, P])
        away = sp.sb("away", [P, EC, EDGES])
        bias = sp.sb("bias", [P, EC, EDGES])
        psR = sp.ps("psR", [P, 512])
        s_load, s_iota, s_zero, s_link, s_idx, s_A0, s_Aeps, s_log, s_diag, s_row = (
            sp.sem(n) for n in ("s_load", "s_iota", "s_zero", "s_link", "s_idx", "s_A0", "s_Aeps", "s_log",
                                "s_diag", "s_row"))
        with nc.Block() as block:
            @block.sync
            def _(eng):
                n = 0
                for dst, src in ((W_linT, A["W_linT"]), (W_valT, A["W_valT"]), (W_outT, A["W_outT"]),
                                 (src_col_i, A["src"].rearrange("(p e) -> p e", e=EC)),
                                 (dst_col_i, A["dst"].rearrange("(p e) -> p e", e=EC)),
                                 (src_row_i, A["src"].unsqueeze(0).to_broadcast([P, EDGES])),
                                 (dst_row_i, A["dst"].unsqueeze(0).to_broadcast([P, EDGES]))):
                    eng.dma_start(dst[:], src).then_inc(s_load, 16)
                    n += 1
                eng.wait_ge(s_zero, 1)
                for h in range(HEADS):
                    eng.dma_start(a_blocks[h * DH:(h + 1) * DH, h:h + 1],
                                  A["a"][h].unsqueeze(1)).then_inc(s_load, 16)
                    n += 1
                eng.wait_ge(s_load, 16 * n)

            loads = 16 * (7 + HEADS)

            @block.gpsimd
            def _(pool):
                pool.iota(node_i[:], [[1, GT]], base=0, channel_multiplier=GT).then_inc(s_iota, 1)
                pool.iota(nodes_i[:], [[1, GT], [GT, P]], base=0, channel_multiplier=0).then_inc(s_iota, 1)
                pool.wait_ge(s_idx, 1)
                for ec in range(EC):
                    pool.indirect_dma_start(out=A0[:, ec:ec + 1], out_offset=None,
                                            in_=A["adj"].rearrange("a (b o) -> (a b) o", o=1),
                                            in_offset=bass.IndirectOffsetOnAxis(ap=place_idx_i[:, ec:ec + 1], axis=0),
                                            ).then_inc(s_A0, 16)

            @block.scalar
            def _(act):
                act.wait_ge(s_Aeps, 1)
                nc.scalar.activation(logA[:], A0[:], ACT.Ln).then_inc(s_log, 1)

            @block.tensor
            def _(pe):
                pe.wait_ge(s_diag, 1)
                for ec in range(EC):
                    last = nc.tensor.matmul(psR[:, ec * P:(ec + 1) * P], k["ones"][:], diag[:, ec, :],
                                            start=True, stop=True)
                last.then_inc(s_row, 1)

            @block.vector
            def _(dve):
                v = nc.vector
                link = Steps(dve, s_link)
                v.memset(a_blocks[:], 0.0).then_inc(s_zero, 1)
                dve.wait_ge(s_iota, 2)
                dve.wait_ge(s_load, loads)
                for out, src in ((node, node_i), (nodes, nodes_i), (src_col, src_col_i), (dst_col, dst_col_i),
                                 (src_row, src_row_i), (dst_row, dst_row_i)):
                    link.done(v.tensor_copy(out[:], src[:]))
                link.done(v.scalar_tensor_tensor(place_idx[:], src_col[:], float(NODES), dst_col[:], ALU.mult, ALU.add))
                v.tensor_copy(place_idx_i[:], place_idx[:]).then_inc(s_idx, 1)
                by_chunk = lambda row: row[:].rearrange("q (p e) -> q e p", e=EC)
                for c in range(GT):
                    both = pick[:, c, 0:EDGES].rearrange("q (e p) -> q e p", e=EC)
                    dst = pick[:, c, EDGES:2 * EDGES].rearrange("q (e p) -> q e p", e=EC)
                    link.done(v.tensor_scalar(dst, by_chunk(dst_row), node[:, c:c + 1], None, ALU.is_equal))
                    link.done(v.scalar_tensor_tensor(both, by_chunk(src_row), node[:, c:c + 1], dst,
                                                     ALU.is_equal, ALU.add))
                for ec in range(EC):
                    v.tensor_scalar(place[:, ec, :], nodes[:], src_col[:, ec:ec + 1], None, ALU.is_equal)
                    link.done(v.tensor_scalar(same[:, ec, :].rearrange("q (e p) -> q e p", e=EC), by_chunk(src_row),
                                              src_col[:, ec:ec + 1], None, ALU.is_equal))
                link.done(v.tensor_scalar(away[:], same[:], 1.0, 1e30, ALU.subtract, ALU.mult))
                v.tensor_copy(a_wide[:], spread(a_blocks[:], P))
                dve.wait_ge(s_A0, 16 * EC)
                v.tensor_scalar(A0[:], A0[:], 1e-8, None, ALU.add).then_inc(s_Aeps, 1)
                dve.wait_ge(s_log, 1)
                for ec in range(EC):
                    last = v.tensor_scalar(diag[:, ec, :], k["ident"][:], logA[:, ec:ec + 1], None, ALU.mult)
                last.then_inc(s_diag, 1)
                dve.wait_ge(s_row, 1)
                for ec in range(EC):
                    v.tensor_tensor(bias[:, ec, :], away[:, ec, :], psR[:, 0:EDGES], ALU.add)

        total, mean, sqsum, var, rstd = (sp.sb(n, [P, 2, GT]) for n in ("total", "mean", "sqsum", "var", "rstd"))
        centred, squares, xn = (sp.sb(n, [P, 2, GT, C]) for n in ("centred", "squares", "xn"))
        GT_, QV = sp.sb("gathered", [P, 2, 2 * EDGES]), sp.sb("QV", [P, 2, 2 * EDGES])
        L = sp.sb("L", [P, 2, EDGES])
        junk = sp.sb("junk", [P, EC * HEADS, EDGES])
        top, z, ex, den, attn = (sp.sb(n, [P, 2, EC, HEADS]) for n in ("top", "z", "ex", "den", "attn"))
        weighed = sp.sb("weighed", [P, 2, EC, C])
        YT = sp.sb("YT", [P, 2, NODES])
        psA = sp.ps("psA", [P, 2, 512])
        psB = sp.ps("psB", [P, 2, 512])
        (s_centred, s_squared, s_var, s_rstd, s_normed, s_g, s_GT, s_qv, s_QV, s_L, s_e, s_z, s_ex, s_den,
         s_w, s_y, s_YT, s_out, s_added) = (sp.sems(n) for n in (
             "centred", "squared", "var", "rstd", "normed", "g", "GT", "qv", "QV", "L", "e", "z", "ex",
             "den", "w", "y", "YT", "out", "added"))
        s_steps = sp.sem("steps")
        with ExitStack() as ctx2, nc.Block() as block:
            psC = [ctx2.enter_context(nc.psum_tensor(f"edge_psC{i}", [P, 512], F32)) for i in range(3)]
            wide = [[psC[0], psC[1]], [psC[2], psR]]

            @block.sync
            def _(eng):
                credit(eng, ((s_steps,), 14), (s_centred + s_squared + s_var + s_rstd + s_normed, 1),
                       (s_g + s_GT + s_qv + s_QV + s_L + s_e + s_z + s_ex + s_den + s_w, 1),
                       (s_y + s_YT + s_out + s_added, 1))

            @block.tensor
            def _(pe):
                with pe.Fori(1, PAIRS + 1) as j:
                    for u in range(2):
                        pe.wait_ge(s_normed[u], j + 1)
                        pe.wait_ge(s_YT[u], j)
                        for c in range(GT):
                            last = nc.tensor.matmul(psA[:, u, :], xn[:, u, c, :], pick[:, c, :], start=(c == 0),
                                                    stop=(c == GT - 1))
                        last.then_inc(s_g[u], 1)
                    for u in range(2):
                        pe.wait_ge(s_GT[u], j + 1)
                        pe.wait_ge(s_added[u], j)
                        nc.tensor.matmul(psB[:, u, 0:EDGES], W_linT[:], GT_[:, u, 0:EDGES], start=True, stop=True)
                        for ec in range(EC):
                            at = EDGES + ec * P
                            last = nc.tensor.matmul(psB[:, u, at:at + C], GT_[:, u, at:at + P], W_valT[:],
                                                    start=True, stop=True)
                        last.then_inc(s_qv[u], 1)
                    for u in range(2):
                        pe.wait_ge(s_L[u], j + 1)
                        for h in range(HEADS):
                            nc.tensor.matmul(wide[u][h // 2][:, (h % 2) * EDGES:(h % 2 + 1) * EDGES], a_wide[:, h, :],
                                             L[:, u, :], start=True, stop=True)
                        for ec in range(EC):
                            last = nc.tensor.matmul(psA[:, u, ec * HEADS:(ec + 1) * HEADS], L[:, u, ec * P:(ec + 1) * P],
                                                    a_blocks[:], start=True, stop=True)
                        last.then_inc(s_e[u], 1)
                    for u in range(2):
                        pe.wait_ge(s_ex[u], j + 1)
                        for ec in range(EC):
                            at = 8 + ec * HEADS
                            for e2 in range(EC):
                                last = nc.tensor.matmul(psA[:, u, at:at + HEADS], same[:, e2, ec * P:(ec + 1) * P],
                                                        ex[:, u, e2, :], start=(e2 == 0), stop=(e2 == EC - 1))
                        last.then_inc(s_den[u], 1)
                    for u in range(2):
                        pe.wait_ge(s_w[u], j + 1)
                        for ec in range(EC):
                            last = nc.tensor.matmul(psA[:, u, :], weighed[:, u, ec, :], place[:, ec, :],
                                                    start=(ec == 0), stop=(ec == EC - 1))
                        last.then_inc(s_y[u], 1)
                    for u in range(2):
                        pe.wait_ge(s_YT[u], j + 1)
                        for c in range(GT):
                            last = nc.tensor.matmul(psB[:, u, c * P:(c + 1) * P], YT[:, u, c * P:(c + 1) * P], W_outT[:],
                                                    start=True, stop=True)
                        last.then_inc(s_out[u], 1)

            @block.scalar
            def _(act):
                with act.Fori(1, PAIRS + 1) as j:
                    for u in range(2):
                        act.wait_ge(s_g[u], j + 1)
                        nc.scalar.copy(GT_[:, u, :], psA[:, u, :]).then_inc(s_GT[u], 1)
                    for u in range(2):
                        act.wait_ge(s_qv[u], j + 1)
                        nc.scalar.copy(QV[:, u, :], psB[:, u, :]).then_inc(s_QV[u], 1)
                    for u in range(2):
                        act.wait_ge(s_z[u], j + 1)
                        nc.scalar.activation(ex[:, u], z[:, u], ACT.Exp).then_inc(s_ex[u], 1)
                    for u in range(2):
                        act.wait_ge(s_y[u], j + 1)
                        nc.scalar.copy(YT[:, u, :], psA[:, u, :]).then_inc(s_YT[u], 1)

            @block.gpsimd
            def _(pool):
                with pool.Fori(1, PAIRS + 1) as j:
                    for u in range(2):
                        pool.wait_ge(s_centred[u], j + 1)
                        pool.tensor_tensor(squares[:, u], centred[:, u], centred[:, u],
                                           ALU.mult).then_inc(s_squared[u], 1)
                    for u in range(2):
                        pool.wait_ge(s_var[u], j + 1)
                        pool.tensor_tensor(rstd[:, u], var[:, u], k["minus_half"][:],
                                           ALU.pow).then_inc(s_rstd[u], 1)

            @block.vector
            def _(dve):
                v = nc.vector
                with dve.Fori(1, PAIRS + 1) as j:
                    link = Steps(dve, s_steps, j * 14)
                    for u in range(2):
                        x4 = X[:, bass.ds((2 * (j - 1) + u) * GT, GT), :]
                        link.done(v.tensor_reduce(total[:, u], x4, AX, ALU.add))
                        link.done(v.tensor_scalar(mean[:, u], total[:, u], 1.0 / C, None, ALU.mult))
                        v.tensor_tensor(centred[:, u], x4, spread(mean[:, u], C), ALU.subtract).then_inc(s_centred[u], 1)
                    for u in range(2):
                        dve.wait_ge(s_squared[u], j + 1)
                        link.done(v.tensor_reduce(sqsum[:, u], squares[:, u], AX, ALU.add))
                        v.tensor_scalar(var[:, u], sqsum[:, u], 1.0 / C, LN_EPS, ALU.mult, ALU.add).then_inc(s_var[u], 1)
                    for u in range(2):
                        dve.wait_ge(s_rstd[u], j + 1)
                        v.tensor_tensor(xn[:, u], centred[:, u], spread(rstd[:, u], C),
                                        ALU.mult).then_inc(s_normed[u], 1)
                    for u in range(2):
                        dve.wait_ge(s_QV[u], j + 1)
                        v.scalar_tensor_tensor(L[:, u, :], QV[:, u, 0:EDGES], 0.2, QV[:, u, 0:EDGES], ALU.mult,
                                               ALU.max).then_inc(s_L[u], 1)
                    for u in range(2):
                        dve.wait_ge(s_e[u], j + 1)
                        link.mark(v.tensor_tensor(z[:, u], psA[:, u, 0:8].rearrange("p (e h) -> p e h", e=EC),
                                                  spread(logA[:], HEADS), ALU.add))
                        for ec in range(EC):
                            for h in range(HEADS):
                                last = v.tensor_tensor_reduce(
                                    junk[:, ec * HEADS + h, :], wide[u][h // 2][:, (h % 2) * EDGES:(h % 2 + 1) * EDGES], bias[:, ec, :], 1.0,
                                    -3e38, ALU.add, ALU.max, top[:, u, ec, h:h + 1])
                        link.done(last)
                        v.tensor_tensor(z[:, u], z[:, u], top[:, u], ALU.subtract).then_inc(s_z[u], 1)
                    for u in range(2):
                        dve.wait_ge(s_den[u], j + 1)
                        link.done(v.reciprocal(den[:, u], psA[:, u, 8:16].rearrange("p (e h) -> p e h", e=EC)))
                        dve.wait_ge(s_ex[u], j + 1)
                        link.done(v.tensor_tensor(attn[:, u], ex[:, u], den[:, u], ALU.mult))
                        v.tensor_tensor(weighed[:, u].rearrange("p e (h d) -> p (e h) d", h=HEADS),
                                        QV[:, u, EDGES:2 * EDGES].rearrange("p (e d) -> p e d", e=EC * HEADS),
                                        spread(attn[:, u].rearrange("p e h -> p (e h)"), DH),
                                        ALU.mult).then_inc(s_w[u], 1)
                    for u in range(2):
                        x4 = X[:, bass.ds((2 * (j - 1) + u) * GT, GT), :]
                        dve.wait_ge(s_out[u], j + 1)
                        v.tensor_tensor(x4, x4, psB[:, u, :].rearrange("p (t c) -> p t c", t=GT),
                                        ALU.add).then_inc(s_added[u], 1)
                    assert link.n == 14, link.n


def dense_attention_stage(nc, k, X, xnT, A):
    SCALE = float(np.float32(1.0) / np.sqrt(np.float32(C)))
    with ExitStack() as ctx:
        sp = Space(nc, ctx, "att")
        normalise(nc, "att_ln", k, X, xnT, None, None, 0)
        Wq, Wk, WvT, Wo = (sp.sb(n, [C, C]) for n in ("Wq", "Wk", "WvT", "Wo"))
        bq, bk, bv, bo = (sp.sb(n, [C, 1]) for n in ("bq", "bk", "bv", "bo"))
        Wvo, bvo = sp.sb("Wvo", [C, C]), sp.sb("bvo", [C, 1])
        alpha, gamma = sp.sb("alpha", [P, 1]), sp.sb("gamma", [P, 1])
        bias = sp.sb("bias", [P, GT, NODES])
        mixT = sp.sb("mixT", [P, GT, NODES])
        keepers = sp.sb("keepers", [P, NODES])
        with ExitStack() as ctx2:
            s2 = Space(nc, ctx2, "att_set")
            adjN, adj, mix = (s2.sb(n, [P, GT, NODES]) for n in ("adjN", "adj", "mix"))
            linked = s2.sb("linked", [P, GT, NODES])
            degree, parent, has, rest = (s2.sb(n, [P, GT]) for n in ("degree", "parent", "has", "rest"))
            diag = s2.sb("diag", [P, GT, P])
            psM, psK, psW = s2.ps("psM", [P, 2, 512]), s2.ps("psK", [P, 512]), s2.ps("psW", [P, 512])
            s_load, s_link, s_diag, s_mix, s_turn, s_out, s_keep, s_w = (
                s2.sem(n) for n in ("load", "link", "diag", "mix", "turn", "out", "keep", "w"))
            with nc.Block() as block:
                loads = [(Wq, A["Wq"]), (Wk, A["Wk"]), (WvT, A["WvT"]), (Wo, A["Wo"]),
                         (bq, A["bq"].unsqueeze(1)), (bk, A["bk"].unsqueeze(1)), (bv, A["bv"].unsqueeze(1)),
                         (bo, A["bo"].unsqueeze(1)),
                         (alpha, A["alpha"].unsqueeze(0).to_broadcast([P, 1])),
                         (gamma, A["gamma"].unsqueeze(0).to_broadcast([P, 1])),
                         (adjN, A["adj"].rearrange("(p c) m -> p c m", c=GT))]

                @block.sync
                def _(eng):
                    for dst, src in loads:
                        eng.dma_start(dst[:], src).then_inc(s_load, 16)

                @block.tensor
                def _(pe):
                    pe.wait_ge(s_load, 16 * len(loads))
                    nc.tensor.matmul(psW[:, 0:C], WvT[:], Wo[:], start=True, stop=True)
                    nc.tensor.matmul(psW[:, C:C + 1], Wo[:], bv[:], start=True, stop=True).then_inc(s_w, 1)
                    pe.wait_ge(s_diag, 1)
                    for c in range(GT):
                        last = nc.tensor.matmul(psK[:, c * P:(c + 1) * P], k["ones"][:], diag[:, c, :], start=True,
                                                stop=True)
                    last.then_inc(s_keep, 1)
                    pe.wait_ge(s_mix, 1)
                    for m in range(GT):
                        if m >= 2:
                            pe.wait_ge(s_out, m - 1)
                        for c in range(GT):
                            last = nc.tensor.transpose(psM[:, m % 2, c * P:(c + 1) * P], mix[:, c, m * P:(m + 1) * P],
                                                       k["ident"][:])
                        last.then_inc(s_turn, 1)

                @block.scalar
                def _(act):
                    for m in range(GT):
                        act.wait_ge(s_turn, m + 1)
                        nc.scalar.copy(mixT[:, m, :], psM[:, m % 2, :]).then_inc(s_out, 1)

                @block.vector
                def _(dve):
                    v = nc.vector
                    link = Steps(dve, s_link)
                    dve.wait_ge(s_load, 16 * len(loads))
                    for c in range(GT):
                        link.mark(v.tensor_copy(adj[:, c, :].rearrange("q (c p) -> q c p", c=GT),
                                                adjN[:, c, :].rearrange("q (p c) -> q c p", c=GT)))
                    link.done(v.tensor_reduce(degree[:], adjN[:], AX, ALU.add))
                    link.done(v.tensor_scalar(linked[:], adj[:], 0.0, None, ALU.not_equal))
                    link.done(v.tensor_reduce(has[:], linked[:], AX, ALU.max))
                    for c in range(GT):
                        last = v.tensor_scalar(diag[:, c, :], k["ident"][:], has[:, c:c + 1], SCALE, ALU.mult, ALU.mult)
                    last.then_inc(s_diag, 1)
                    link.done(v.tensor_scalar(linked[:], linked[:], 1.0, 1e9, ALU.subtract, ALU.mult))
                    v.scalar_tensor_tensor(bias[:], adj[:], alpha[:, 0:1], linked[:], ALU.mult, ALU.add)
                    link.done(v.tensor_scalar(parent[:], degree[:], 0.0, gamma[:, 0:1], ALU.is_gt, ALU.mult))
                    link.done(v.tensor_scalar(rest[:], parent[:], -1.0, 1.0, ALU.mult, ALU.add))
                    for c in range(GT):
                        link.mark(v.tensor_scalar(mix[:, c, :], adj[:, c, :], parent[:, c:c + 1], None, ALU.mult))
                    dve.wait_ge(s_link, link.n)
                    for c in range(GT):
                        block_c = mix[:, c, c * P:(c + 1) * P]
                        last = v.scalar_tensor_tensor(block_c, k["ident"][:], rest[:, c:c + 1], block_c, ALU.mult, ALU.add)
                    last.then_inc(s_mix, 1)
                    dve.wait_ge(s_keep, 1)
                    v.tensor_copy(keepers[:], psK[:])
                    dve.wait_ge(s_w, 1)
                    v.tensor_copy(Wvo[:], psW[:, 0:C])
                    v.tensor_tensor(bvo[:], psW[:, C:C + 1], bo[:], ALU.add)

        QT, KT, U, rT, r, fT = (sp.sb(n, [P, 2, NODES]) for n in ("QT", "KT", "U", "rT", "r", "fT"))
        xg = sp.sb("xg", [P, 2, NODES])
        PT = sp.sb("PT", [P, 2, GT, NODES])
        SC, Pn = sp.sb("SC", [P, 2, NODES]), sp.sb("Pn", [P, 2, NODES])
        Pe = sp.sb("Pe", [P, 2, NODES])
        top, ntop, rowsum, rinv = (sp.sb(n, [P, 2]) for n in ("top", "ntop", "rowsum", "rinv"))
        carrier = sp.sb("carrier", [P, 2])
        psG = [sp.ps(f"psG{i}", [P, 512]) for i in range(4)]
        psS, psT = sp.ps("psS", [P, 2, 512]), sp.ps("psT", [P, 2, 512])
        (s_xg, s_q, s_k, s_u, s_QT, s_KT, s_U, s_o, s_rT, s_rt, s_r, s_f, s_fT, s_ft, s_added) = (sp.sems(n) for n in (
            "xg", "q", "k", "u", "QT", "KT", "U", "o", "rT", "rt", "r", "f", "fT", "ft", "added"))
        s_S, s_top, s_ntop, s_exp, s_inv, s_Pn, s_pt, s_PT = (sp.sem(n) for n in (
            "S", "top", "ntop", "exp", "inv", "Pn", "pt", "PT"))
        ITEMS = 2 * GT
        with nc.Block() as block:
            @block.sync
            def _(eng):
                credit(eng, (s_xg + s_q + s_k + s_u + s_QT + s_KT + s_U + s_o + s_rT + s_rt + s_r + s_f + s_fT, 1),
                       (s_ft + s_added, 1), ((s_S, s_top, s_ntop, s_exp, s_inv, s_Pn, s_pt, s_PT), ITEMS))

            @block.gpsimd
            def _(pool):
                with pool.Fori(1, PAIRS + 1) as j:
                    for u in range(2):
                        pool.wait_ge(s_rT[u], j)
                        pool.tensor_copy(xg[:, u, :], xnT[:, bass.ds((2 * (j - 1) + u) * NODES, NODES)]).then_inc(s_xg[u], 1)

            @block.tensor
            def _(pe):
                mm = nc.tensor.matmul
                with pe.Fori(1, PAIRS + 1) as j:
                    plan = [[(0, s_fT[0], 0), (1, s_fT[1], 0), (2, s_added[0], 0)],
                            [(3, s_added[1], 0), (0, s_QT[0], 1), (1, s_KT[0], 1)]]
                    for u in range(2):
                        pe.wait_ge(s_xg[u], j + 1)
                        for step, (bank, free, more) in enumerate(plan[u]):
                            pe.wait_ge(free, j + more)
                            if step < 2:
                                mm(psG[bank][:], (Wq, Wk)[step][:], xg[:, u, :], start=True,
                                   stop=True).then_inc((s_q, s_k)[step][u], 1)
                            else:
                                for c in range(GT):
                                    last = mm(psG[bank][:, c * P:(c + 1) * P], xg[:, u, c * P:(c + 1) * P], Wvo[:],
                                              start=True, stop=True)
                                last.then_inc(s_u[u], 1)

                    def scores(q):
                        c, u = q // 2, q % 2
                        pe.wait_ge(s_QT[u], j + 1)
                        pe.wait_ge(s_KT[u], j + 1)
                        pe.wait_ge(s_top, ITEMS * j + max(q - 1, 0))
                        mm(psS[:, q % 2, :], QT[:, u, c * P:(c + 1) * P], KT[:, u, :], start=True,
                           stop=True).then_inc(s_S, 1)

                    def turn(q):
                        pe.wait_ge(s_Pn, ITEMS * j + q + 1)
                        pe.wait_ge(s_PT, ITEMS * j + max(q - 1, 0))
                        for m in range(GT):
                            last = nc.tensor.transpose(psT[:, q % 2, m * P:(m + 1) * P],
                                                       Pn[:, q % 2, m * P:(m + 1) * P], k["ident"][:])
                        last.then_inc(s_pt, 1)

                    for q in range(ITEMS + 4):
                        if q < ITEMS:
                            scores(q)
                        if q >= 4:
                            turn(q - 4)
                    for u in range(2):
                        pe.wait_ge(s_KT[1], j + 1)
                        pe.wait_ge(s_U[1], j + 1)
                        pe.wait_ge(s_PT, ITEMS * j + ITEMS - 1 + u)
                        for m in range(GT):
                            last = mm(psG[u][:], U[:, u, m * P:(m + 1) * P], PT[:, u, m, :], start=(m == 0),
                                      stop=(m == GT - 1))
                        last.then_inc(s_o[u], 1)
                    for u in range(2):
                        pe.wait_ge(s_rT[u], j + 1)
                        for c in range(GT):
                            last = nc.tensor.transpose(psG[2 + u][:, c * P:(c + 1) * P], rT[:, u, c * P:(c + 1) * P],
                                                       k["ident"][:])
                        last.then_inc(s_rt[u], 1)
                    for u in range(2):
                        pe.wait_ge(s_r[u], j + 1)
                        for m in range(GT):
                            last = mm(psG[u][:], r[:, u, m * P:(m + 1) * P], mixT[:, m, :], start=(m == 0),
                                      stop=(m == GT - 1))
                        last.then_inc(s_f[u], 1)
                    for u in range(2):
                        pe.wait_ge(s_fT[u], j + 1)
                        for c in range(GT):
                            last = nc.tensor.transpose(psG[2 + u][:, c * P:(c + 1) * P], fT[:, u, c * P:(c + 1) * P],
                                                       k["ident"][:])
                        last.then_inc(s_ft[u], 1)

            @block.scalar
            def _(act):
                with act.Fori(1, PAIRS + 1) as j:
                    for u in range(2):
                        act.wait_ge(s_k[u], j + 1)
                        nc.scalar.activation(KT[:, u, :], psG[(1, 0)[u]][:], ACT.Identity, bias=bk[:, 0:1]).then_inc(s_KT[u], 1)
                        act.wait_ge(s_u[u], j + 1)
                        nc.scalar.copy(U[:, u, :], psG[(2, 1)[u]][:]).then_inc(s_U[u], 1)

                    def exps(q):
                        act.wait_ge(s_ntop, ITEMS * j + q + 1)
                        act.wait_ge(s_Pn, ITEMS * j + max(q - 1, 0))
                        nc.scalar.activation(Pe[:, q % 2, :], SC[:, q % 2, :], ACT.Exp, bias=ntop[:, q % 2:q % 2 + 1],
                                             accum_out=rowsum[:, q % 2:q % 2 + 1]).then_inc(s_exp, 1)

                    def out(q):
                        c, u = q // 2, q % 2
                        act.wait_ge(s_pt, ITEMS * j + q + 1)
                        nc.scalar.copy(PT[:, u, :, c * P:(c + 1) * P],
                                       psT[:, q % 2, :].rearrange("p (m n) -> p m n", m=GT)).then_inc(s_PT, 1)

                    for q in range(ITEMS + 4):
                        if q < ITEMS:
                            exps(q)
                        if q >= 4:
                            out(q - 4)
                    for u in range(2):
                        act.wait_ge(s_rt[u], j + 1)
                        nc.scalar.copy(r[:, u, :], psG[2 + u][:]).then_inc(s_r[u], 1)
                    for u in range(2):
                        act.wait_ge(s_f[u], j + 1)
                        nc.scalar.copy(fT[:, u, :], psG[u][:]).then_inc(s_fT[u], 1)

            @block.vector
            def _(dve):
                v = nc.vector
                with dve.Fori(1, PAIRS + 1) as j:
                    for u in range(2):
                        dve.wait_ge(s_q[u], j + 1)
                        v.scalar_tensor_tensor(QT[:, u, :], psG[(0, 3)[u]][:], bq[:, 0:1], keepers[:], ALU.add,
                                               ALU.mult).then_inc(s_QT[u], 1)
                    for q in range(ITEMS + 2):
                        b, old = q % 2, q - 2
                        if q < ITEMS:
                            dve.wait_ge(s_S, ITEMS * j + q + 1)
                        if old < 0:
                            dve.wait_ge(s_exp, ITEMS * j)
                            v.memset(carrier[:, q:q + 1], 0.0)
                        else:
                            dve.wait_ge(s_exp, ITEMS * j + old + 1)
                            v.reciprocal(rinv[:, b:b + 1], rowsum[:, b:b + 1]).then_inc(s_inv, 1)
                        if q < ITEMS:
                            v.tensor_tensor_reduce(SC[:, b, :], psS[:, b, :], bias[:, q // 2, :], 1.0, -3e38, ALU.add, ALU.max,
                                                   top[:, b:b + 1]).then_inc(s_top, 1)
                        if old >= 0:
                            dve.wait_ge(s_inv, ITEMS * j + old + 1)
                            dve.wait_ge(s_pt, ITEMS * j + max(old - 1, 0))
                            v.tensor_scalar(Pn[:, b, :], Pe[:, b, :], rinv[:, b:b + 1], None, ALU.mult).then_inc(s_Pn, 1)
                        if q < ITEMS:
                            dve.wait_ge(s_top, ITEMS * j + q + 1)
                            v.tensor_scalar(ntop[:, b:b + 1], top[:, b:b + 1], -1.0, None, ALU.mult).then_inc(s_ntop, 1)
                    for u in range(2):
                        dve.wait_ge(s_o[u], j + 1)
                        v.scalar_tensor_tensor(rT[:, u, :], psG[u][:], bvo[:, 0:1], xg[:, u, :], ALU.add,
                                               ALU.add).then_inc(s_rT[u], 1)
                    for u in range(2):
                        x4 = X[:, bass.ds((2 * (j - 1) + u) * GT, GT), :]
                        dve.wait_ge(s_ft[u], j + 1)
                        v.tensor_tensor(x4, x4, psG[2 + u][:].rearrange("p (t c) -> p t c", t=GT),
                                        ALU.add).then_inc(s_added[u], 1)


EDGES2 = 524288
LANE = EDGES2 // P
GAT_HEADS, GAT_EXPERTS = 4, 4
HEAD_COLS = GAT_HEADS * GAT_EXPERTS
LAST_NODE = SRC_NODES - 1
NODE_BITS, PART_BITS = 13, 7
TILE_SHIFT = NODE_BITS + PART_BITS
KEY_MARK = 1 << 29
MARKED = KEY_MARK >> TILE_SHIFT
SEGMENTS = 8
SEGMENT = LANE // SEGMENTS
TAKEN = 56
MAX_PASSES = -(-SEGMENT // TAKEN)
PICKED = SEGMENTS * TAKEN
WINDOWS = 4
WT = TILES // WINDOWS
CH = 8
HCOLS = 8
HOTS = 4
FEATURES = HEAD_COLS + GAT_HEADS


class Tally:

    def __init__(self, nc, sp, chunks, lo16, hi16, iota16, iota1_16, far_count):
        self.nc, self.lo16, self.hi16, self.iota16, self.iota1_16 = nc, lo16, hi16, iota16, iota1_16
        self.far_count = far_count
        self.LO = sp.sb("LO", [P, HOTS, HCOLS // 2, P, 2], BF16)
        self.HI = sp.sb("HI", [P, HOTS, HCOLS // 2, TILES, 2], BF16)
        self.zeros = sp.sb("zeros", [P, P], BF16)
        self.hist = sp.ps("hist", [P, 512])
        self.s_zero, self.s_hot, self.s_used, self.s_hist = (sp.sem(n) for n in ("zero", "hot", "used", "hist"))
        self.batches = LANE // HCOLS // GROUPS
        self.of_chunk = [[q for q in range(self.batches) if q * chunks // self.batches == i] for i in range(chunks)]
        with nc.Block() as block:
            @block.vector
            def _(dve):
                nc.vector.memset(self.zeros[:], 0.0)

    def start(self, eng):
        credit(eng, ((self.s_hot, self.s_used), 2 * self.batches))

    def open(self):
        self.nc.tensor.matmul(self.hist[:, 0:TILES], self.zeros[:], self.zeros[:, 0:TILES], start=True, stop=False)

    def close(self):
        self.nc.tensor.matmul(self.hist[:, 0:TILES], self.zeros[:], self.zeros[:, 0:TILES], start=False,
                              stop=True).then_inc(self.s_hist, 1)

    def count(self, j, u, q):
        return j * (2 * self.batches) + (u * self.batches + q)

    def make(self, dve, j, u, i):
        for q in self.of_chunk[i]:
            at = bass.ds((j - 1) * (2 * self.batches * HCOLS) + (u * self.batches + q) * HCOLS, HCOLS)
            b = q % HOTS
            dve.wait_ge(self.s_used, self.count(j, u, q + 1 - HOTS))
            for out, pattern, column, width in ((self.LO, self.iota16, self.lo16, P), (self.HI, self.iota1_16, self.hi16, TILES)):
                last = self.nc.vector.tensor_tensor(
                    out[:, b], pattern[:].unsqueeze(1).to_broadcast([P, HCOLS // 2, width, 2]),
                    column[:, at].rearrange("p (a b) -> p a b", b=2).unsqueeze(2).to_broadcast([P, HCOLS // 2, width, 2]),
                    ALU.is_equal)
            last.then_inc(self.s_hot, 1)

    def add(self, pe, j, u, i):
        for q in self.of_chunk[i] if i >= 0 else ():
            b = q % HOTS
            pe.wait_ge(self.s_hot, self.count(j, u, q + 1))
            for c in range(HCOLS):
                last = self.nc.tensor.matmul(self.hist[:, 0:TILES], self.LO[:, b, c // 2, :, c % 2],
                                             self.HI[:, b, c // 2, :, c % 2], start=False, stop=False)
            last.then_inc(self.s_used, 1)

    def read(self, dve):
        dve.wait_ge(self.s_hist, 1)
        self.nc.vector.tensor_copy(self.far_count[:], self.hist[:, 0:TILES])


def edge_keys_stage(nc, k, A, keys, lo16, hi16, iota16, iota1_16, cell):
    with ExitStack() as ctx:
        sp = Space(nc, ctx, "keys")
        src, dst = sp.sb("src", [P, LANE], I32), sp.sb("dst", [P, LANE], I32)
        part, tile = sp.sb("part", [P, LANE], I32), sp.sb("tile", [P, LANE], I32)
        real, live = sp.sb("real", [P, LANE]), sp.sb("live", [P, LANE])
        iota_i = sp.sb("iota_i", [P, P, 2], I32)
        count, most = sp.sb("count", [P, SEGMENTS]), sp.sb("most", [P, SEGMENTS])
        full, fuller = sp.sb("full", [P, 1]), sp.sb("fuller", [P, MAX_PASSES])
        levels_i, levels = sp.sb("levels_i", [P, MAX_PASSES], I32), sp.sb("levels", [P, MAX_PASSES])
        passes_f = sp.sb("passes_f", [P, 1])
        s_load, s_iota, s_link, s_count, s_most = (sp.sem(n) for n in ("load", "iota", "link", "count", "most"))
        edges = A["edge_index"].rearrange("a (p i) -> a p i", p=P)
        with nc.Block() as block:
            @block.sync
            def _(eng):
                eng.dma_start(src[:], edges[0]).then_inc(s_load, 16)
                eng.dma_start(dst[:], edges[1]).then_inc(s_load, 16)

            @block.gpsimd
            def _(pool):
                pool.iota(iota_i[:], [[1, P], [0, 2]], base=0, channel_multiplier=0).then_inc(s_iota, 1)
                pool.iota(levels_i[:], [[TAKEN, MAX_PASSES]], base=0, channel_multiplier=0).then_inc(s_iota, 1)
                pool.wait_ge(s_count, 1)
                pool.partition_all_reduce(most[:], count[:], P, bass.bass_isa.ReduceOp.max).then_inc(s_most, 1)

            @block.vector
            def _(dve):
                v = nc.vector
                link = Steps(dve, s_link)
                dve.wait_ge(s_iota, 2)
                v.tensor_copy(iota16[:], iota_i[:])
                v.tensor_copy(levels[:], levels_i[:])
                v.tensor_scalar(iota1_16[:], iota_i[:, 0:TILES, :], 1.0, None, ALU.add)
                dve.wait_ge(s_load, 32)
                link.done(v.tensor_scalar(real[:], dst[:], float(SRC_NODES), None, ALU.is_lt))
                link.done(v.scalar_tensor_tensor(live[:], src[:], float(LAST_NODE), real[:], ALU.is_lt, ALU.mult))
                link.mark(v.tensor_tensor(real[:], real[:], live[:], ALU.subtract))
                v.tensor_reduce(count[:], live[:].rearrange("p (s i) -> p s i", s=SEGMENTS), AX, ALU.add).then_inc(s_count, 1)
                keys_i = keys[:].bitcast(I32)
                link.done(v.tensor_scalar(part[:], dst[:], 2, P - 1, ALU.logical_shift_right, ALU.bitwise_and))
                link.mark(v.tensor_copy(lo16[:], part[:]))
                link.mark(v.tensor_scalar(tile[:], dst[:], 9, 2, ALU.logical_shift_right, ALU.logical_shift_left))
                link.done(v.tensor_scalar(dst[:], dst[:], GT - 1, None, ALU.bitwise_and))
                link.done(v.tensor_tensor(tile[:], tile[:], dst[:], ALU.bitwise_or))
                link.mark(v.scalar_tensor_tensor(hi16[:], tile[:], 1.0, real[:], ALU.add, ALU.mult))
                link.mark(v.tensor_scalar(keys_i, tile[:], TILE_SHIFT, KEY_MARK, ALU.logical_shift_left, ALU.bitwise_or))
                link.done(v.tensor_scalar(part[:], part[:], NODE_BITS, None, ALU.logical_shift_left))
                link.done(v.tensor_tensor(src[:], src[:], part[:], ALU.bitwise_or))
                link.done(v.tensor_tensor(keys_i, keys_i, src[:], ALU.bitwise_or))
                link.mark(v.tensor_tensor(keys[:], keys[:], live[:], ALU.mult))
                dve.wait_ge(s_most, 1)
                link.done(v.tensor_reduce(full[:], most[:], AX, ALU.max))
                link.done(v.tensor_scalar(full[:], full[:], 1.0, None, ALU.max))
                link.done(v.tensor_tensor(fuller[:], levels[:], full[:].to_broadcast([P, MAX_PASSES]), ALU.is_lt))
                link.done(v.tensor_reduce(passes_f[:], fuller[:], AX, ALU.add))
                v.tensor_copy(cell[:], passes_f[:])


def pick_keys(nc, keys, picked, split, there, count, fullest, turns_f, turns_i, turns_of):
    rounds = TAKEN // CH
    with ExitStack() as ctx:
        sp = Space(nc, ctx, "pick")
        s_taken, s_link, s_count, s_fullest = (sp.sem(n) for n in ("taken", "link", "count", "fullest"))
        with nc.Block() as block:
            @block.gpsimd
            def _(pool):
                pool.wait_ge(s_count, 1)
                pool.partition_all_reduce(fullest[:], count[:], P, bass.bass_isa.ReduceOp.max).then_inc(s_fullest, 1)

            @block.vector
            def _(dve):
                v = nc.vector
                take = Steps(dve, s_taken)
                for i in range(rounds):
                    for s in range(SEGMENTS):
                        if i:
                            dve.wait_ge(s_taken, (2 * i - 1) * SEGMENTS + s + 1)
                        take.mark(v.max(out=picked[:, s, i * CH:(i + 1) * CH], in_=keys[:, s * SEGMENT:(s + 1) * SEGMENT]))
                    for s in range(SEGMENTS):
                        dve.wait_ge(s_taken, 2 * i * SEGMENTS + s + 1)
                        seg = keys[:, s * SEGMENT:(s + 1) * SEGMENT]
                        take.mark(v.match_replace(out=seg, in_to_replace=picked[:, s, i * CH:(i + 1) * CH],
                                                  in_values=seg, imm_value=0.0))
                link = Steps(dve, s_link)
                flat = picked[:].rearrange("p s i -> p (s i)")
                begins = [float(np.array(KEY_MARK + (w * WT << TILE_SHIFT), np.uint32).view(np.float32)) for w in range(WINDOWS + 1)]
                for w in range(WINDOWS):
                    link.mark(v.scalar_tensor_tensor(split[:, w, :], flat, begins[w], flat, ALU.is_ge, ALU.mult))
                for w in range(WINDOWS):
                    dve.wait_ge(s_link, w + 1)
                    link.mark(v.scalar_tensor_tensor(split[:, w, :], split[:, w, :], begins[w + 1], split[:, w, :],
                                                     ALU.is_lt, ALU.mult))
                dve.wait_ge(s_link, link.n)
                link.done(v.tensor_scalar(there[:], split[:], 0.0, None, ALU.is_gt))
                v.tensor_reduce(count[:], there[:], AX, ALU.add).then_inc(s_count, 1)
                dve.wait_ge(s_fullest, 1)
                link.done(v.tensor_scalar(turns_f[:], fullest[:], float(4 * CH - 1), float(4 * CH), ALU.add, ALU.max))
                link.done(v.tensor_copy(turns_i[:], turns_f[:]))
                v.tensor_scalar(turns_of[:], turns_i[:], 4, None, ALU.logical_shift_right)


def edge_window(nc, sp, w, B):
    (node, now, split, turns_of, bound, tile_marks, iota16, ident16, src_table) = (
        B[n] for n in ("node", "now", "split", "turns_of", "bound", "tile_marks", "iota16", "ident16", "src_table"))
    (a_dst_now, marks_now, top8, sidx, part_i, tile_i, part16, tile_f, rows) = (
        B[n] for n in ("a_dst_now", "marks_now", "top8", "sidx", "part_i", "tile_i", "part16", "tile_f", "rows"))
    (LO16, LO, LOT, HI, choice, a_dst_e, z, zd, val, spreadv, tick, sums, zeros) = (
        B[n] for n in ("LO16", "LO", "LOT", "HI", "choice", "a_dst_e", "z", "zd", "val", "spreadv", "tick", "sums", "zeros"))
    acc, psA, psT16, ones = B["acc"], B["psA"], B["psT16"], B["ones"]
    NH, W = GAT_HEADS, FEATURES
    MOST_TURNS = -(-PICKED // (2 * CH)) + 1
    s_set, s_loop, s_sum = (sp.sem(n) for n in ("set", "loop", "sum"))
    (s_idx, s_rows, s_hot, s_turned, s_lot, s_lo, s_a, s_z, s_w, s_val, s_spread, s_used, s_tick) = (sp.sems(n) for n in (
        "idx", "rows", "hot", "turned", "lot", "lo", "a", "z", "w", "val", "spread", "used", "tick"))
    STEPS = 2 * 12
    cells = turns_of[0:1, bass.ds(w, 1)]

    def after(j, u):
        return (j, 1) if u == 0 else (j + 1, 0)

    with nc.Block() as block:
        @block.sync
        def _(eng):
            credit(eng, (s_idx + s_hot + s_turned + s_lot + s_lo + s_a + s_z + s_w + s_val + s_spread + s_used + s_tick, 1),
                   ((s_loop,), STEPS))

        @block.gpsimd
        def _(pool):
            with pool.Fori(1, pool.value_load(cells, min_val=2, max_val=MOST_TURNS)) as j:
                for u in range(2):
                    pool.wait_ge(s_idx[u], j + 1)
                    pool.wait_ge(s_val[u], j)
                    pool.wait_ge(s_tick[u], j)
                    pool.tensor_tensor(tick[:, u:u + 1], ones[:, 0:1], ones[:, 0:1], ALU.mult).then_inc(s_tick[u], 1)
                    for i in range(CH):
                        pool.indirect_dma_start(out=rows[:, u, i, :], out_offset=None, in_=src_table,
                                                in_offset=bass.IndirectOffsetOnAxis(ap=sidx[:, u, i:i + 1], axis=0)
                                                ).then_inc(s_rows[u], 16)

        @block.scalar
        def _(act):
            def one_hots(nj, nu):
                act.wait_ge(s_turned[nu], nj + 1)
                act.wait_ge(s_a[nu], nj)
                nc.scalar.copy(LOT[:, nu], psT16[nu]).then_inc(s_lot[nu], 1)
                act.wait_ge(s_hot[nu], nj + 1)
                act.wait_ge(s_used[nu], nj)
                nc.scalar.copy(LO[:, nu].rearrange("p (a b) e -> p a b e", b=2),
                               LO16[:, nu].rearrange("p a e b -> p a b e")).then_inc(s_lo[nu], 1)

            one_hots(1, 0)
            turns = act.value_load(cells, min_val=2, max_val=MOST_TURNS)
            with act.Fori(1, turns) as j:
                for u in range(2):
                    act.wait_ge(s_z[u], j + 1)
                    nc.scalar.activation(val[:, u, :, HEAD_COLS:W], zd[:, u], ACT.Exp).then_inc(s_w[u], 1)
                    one_hots(*after(j, u))
            one_hots(turns, 1)

        @block.tensor
        def _(pe):
            mm = nc.tensor.matmul

            def turn_hots(nj, nu):
                pe.wait_ge(s_hot[nu], nj + 1)
                pe.wait_ge(s_lot[nu], nj)
                for i in range(CH):
                    last = nc.tensor.transpose(psT16[nu][:, i, :], LO16[:, nu, i // 2, :, i % 2], ident16[:])
                last.then_inc(s_turned[nu], 1)

            def pick_a_dst(nj, nu):
                pe.wait_ge(s_lot[nu], nj + 1)
                pe.wait_ge(s_z[nu], nj)
                for i in range(CH):
                    last = mm(psA[:, nu, i * NH * WT:(i + 1) * NH * WT], LOT[:, nu, i, :],
                              a_dst_now[:].rearrange("p h t -> p (h t)"), start=True, stop=True)
                last.then_inc(s_a[nu], 1)

            mm(acc[:, 0:W * WT], zeros[:, 0:P], zeros[:], start=True, stop=False)
            pe.wait_ge(s_set, 1)
            for u in range(2):
                turn_hots(1, u)
                pick_a_dst(1, u)
            with pe.Fori(1, pe.value_load(cells, min_val=2, max_val=MOST_TURNS)) as j:
                for u in range(2):
                    pe.wait_ge(s_lo[u], j + 1)
                    pe.wait_ge(s_spread[u], j + 1)
                    for i in range(CH):
                        if i == CH // 2:
                            turn_hots(j + 1, u)
                        last = mm(acc[:, 0:W * WT], LO[:, u, i, :], spreadv[:, u, i].rearrange("p f t -> p (f t)"),
                                  start=False, stop=False)
                    last.then_inc(s_used[u], 1)
                    pick_a_dst(j + 1, u)
            mm(acc[:, 0:W * WT], zeros[:, 0:P], zeros[:], start=False, stop=True).then_inc(s_sum, 1)

        @block.vector
        def _(dve):
            v = nc.vector

            def select(step, u):
                t8 = top8[:, u].bitcast(I32)
                step.done(v.max(out=top8[:, u], in_=now[:]))
                v.tensor_scalar(sidx[:, u], t8, SRC_NODES - 1, None, ALU.bitwise_and).then_inc(s_idx[u], 1)
                step.mark(v.tensor_scalar(part_i[:, u], t8, NODE_BITS, P - 1, ALU.logical_shift_right, ALU.bitwise_and))
                step.mark(v.tensor_scalar(tile_i[:, u], t8, TILE_SHIFT, None, ALU.logical_shift_right))
                step.done(v.match_replace(out=now[:], in_to_replace=top8[:, u], in_values=now[:], imm_value=0.0))
                step.mark(v.tensor_copy(part16[:, u], part_i[:, u]))
                step.done(v.tensor_copy(tile_f[:, u], tile_i[:, u]))

            def one_hots(u):
                v.tensor_tensor(LO16[:, u], iota16[:].unsqueeze(1).to_broadcast([P, CH // 2, P, 2]),
                                part16[:, u].rearrange("p (a b) -> p a b", b=2).unsqueeze(2)
                                .to_broadcast([P, CH // 2, P, 2]), ALU.is_equal).then_inc(s_hot[u], 1)
                return v.tensor_tensor(HI[:, u], marks_now[:].unsqueeze(1).to_broadcast([P, CH, WT]),
                                       spread(tile_f[:, u], WT), ALU.is_equal)

            link = Steps(dve, s_set)
            link.mark(v.tensor_copy(a_dst_now[:], node[:, bass.ds(w * WT, WT), W:W + NH].rearrange("p t h -> p h t")))
            link.mark(v.tensor_copy(marks_now[:], tile_marks[:, bass.ds(w * WT, WT)]))
            link.done(v.tensor_copy(now[:], split[:, bass.ds(w, 1), :].rearrange("p a i -> p (a i)")))
            select(link, 0)
            link.done(one_hots(0))
            select(link, 1)
            turns = dve.value_load(cells, min_val=2, max_val=MOST_TURNS)
            with dve.Fori(1, turns) as j:
                step = Steps(dve, s_loop, j * STEPS)
                for u in range(2):
                    nj, nu = after(j, u)
                    dve.wait_ge(s_a[u], j + 1)
                    step.done(v.tensor_tensor(choice[:, u], psA[:, u, :].rearrange("p (i h t) -> p i h t", h=NH, t=WT),
                                              HI[:, u].unsqueeze(2).to_broadcast([P, CH, NH, WT]), ALU.mult))
                    step.done(v.tensor_reduce(a_dst_e[:, u], choice[:, u], AX, ALU.add))
                    step.mark(v.tensor_tensor(z[:, u, 1], a_dst_e[:, u], bound[:].unsqueeze(1).to_broadcast([P, CH, NH]), ALU.add))
                    dve.wait_ge(s_rows[u], j * (16 * CH))
                    step.done(v.tensor_tensor(z[:, u, 0], rows[:, u, :, HEAD_COLS:W], a_dst_e[:, u], ALU.add))
                    step.done(v.scalar_tensor_tensor(z[:, u], z[:, u], 0.2, z[:, u], ALU.mult, ALU.max))
                    v.tensor_tensor(zd[:, u], z[:, u, 0], z[:, u, 1], ALU.subtract).then_inc(s_z[u], 1)
                    dve.wait_ge(s_turned[nu], nj)
                    dve.wait_ge(s_lo[nu], nj)
                    step.mark(one_hots(nu))
                    dve.wait_ge(s_w[u], j + 1)
                    v.tensor_tensor(val[:, u, :, 0:HEAD_COLS].rearrange("p i (h e) -> p i h e", h=NH),
                                    rows[:, u, :, 0:HEAD_COLS].rearrange("p i (h e) -> p i h e", h=NH),
                                    val[:, u, :, HEAD_COLS:W].unsqueeze(3).to_broadcast([P, CH, NH, GAT_EXPERTS]),
                                    ALU.mult).then_inc(s_val[u], 1)
                    dve.wait_ge(s_val[u], j + 1)
                    dve.wait_ge(s_loop, step.base + step.n)
                    dve.wait_ge(s_used[u], j)
                    v.tensor_tensor(spreadv[:, u], val[:, u].unsqueeze(3).to_broadcast([P, CH, W, WT]),
                                    HI[:, u].unsqueeze(2).to_broadcast([P, CH, W, WT]), ALU.mult).then_inc(s_spread[u], 1)
                    select(step, u)
                assert step.n == STEPS, step.n
            dve.wait_ge(s_turned[1], turns)
            dve.wait_ge(s_lo[1], turns)
            one_hots(1)
            dve.wait_ge(s_sum, 1)
            v.tensor_tensor(sums[:, bass.ds(w, 1)], sums[:, bass.ds(w, 1)],
                            acc[:, 0:W * WT].rearrange("p (o f t) -> p o f t", o=1, f=W), ALU.add)


def gat_stage(nc, k, X, xnT, A, keys, far_count, cell, parts):
    NH, W = GAT_HEADS, FEATURES
    with ExitStack() as ctx:
        sp = Space(nc, ctx, "gat")
        w_node = sp.sb("w_node", [C, W + NH])
        node = sp.sb("node", [P, TILES, W + NH])
        with ExitStack() as ctx2:
            s2 = Space(nc, ctx2, "gat_set")
            WgT, att = s2.sb("WgT", [HEAD_COLS, C]), s2.sb("att", [HEAD_COLS, 2 * NH])
            psW = s2.ps("psW", [C, 512])
            s_load, s_zero, s_w = (s2.sem(n) for n in ("load", "zero", "w"))
            with nc.Block() as block:
                @block.sync
                def _(eng):
                    eng.dma_start(WgT[:], A["W_gatT"]).then_inc(s_load, 16)
                    eng.dma_start(w_node[:, 0:HEAD_COLS], A["W_gat"]).then_inc(s_load, 16)
                    eng.wait_ge(s_zero, 1)
                    for i, name in enumerate(("att_src", "att_dst")):
                        for h in range(NH):
                            eng.dma_start(att[h * NH:(h + 1) * NH, i * NH + h:i * NH + h + 1],
                                          A[name][h].unsqueeze(1)).then_inc(s_load, 16)

                @block.tensor
                def _(pe):
                    pe.wait_ge(s_load, 16 * (2 + 2 * NH))
                    nc.tensor.matmul(psW[:, 0:2 * NH], WgT[:], att[:], start=True, stop=True).then_inc(s_w, 1)

                @block.vector
                def _(dve):
                    nc.vector.memset(att[:], 0.0).then_inc(s_zero, 1)
                    dve.wait_ge(s_w, 1)
                    nc.vector.tensor_copy(w_node[:, HEAD_COLS:], psW[:, 0:2 * NH])
        normalise(nc, "gat_ln", k, X, xnT, w_node[:], node, W + NH)

        src_table = nc.dram_tensor("src_table", [SRC_NODES, W], F32, kind="Internal").ap()
        src_rows = sp.sb("src_rows", [P, TILES, W])
        most, bound = sp.sb("most", [P, NH]), sp.sb("bound", [P, NH])
        last_row = sp.sb("last_row", [P, W])
        floor = sp.sb("floor", [P, TILES, NH])
        sums = sp.sb("sums", [P, WINDOWS, W, WT])
        iota_i, window_i = sp.sb("iota_i", [P, P, 2], I32), sp.sb("window_i", [P, TILES], I32)
        iota16, tile_marks = sp.sb("iota16", [P, P, 2], BF16), sp.sb("tile_marks", [P, TILES])
        zeros = sp.sb("zeros", [P, W * WT])
        s_table, s_last = sp.sem("table"), sp.sem("last")
        with ExitStack() as ctx2:
            s2 = Space(nc, ctx2, "gat_table")
            s_packed, s_most, s_iota = (s2.sem(n) for n in ("packed", "most", "iota"))
            with nc.Block() as block:
                @block.sync
                def _(eng):
                    eng.wait_ge(s_packed, 1)
                    eng.dma_start(src_table.rearrange("(b p c) f -> p b c f", p=P, c=GT),
                                  src_rows[:].rearrange("p (b c) f -> p b c f", c=GT)).then_inc(s_table, 16)
                    eng.wait_ge(s_table, 16)
                    eng.dma_start(last_row[:], src_table[LAST_NODE:LAST_NODE + 1, :].to_broadcast([P, W])).then_inc(s_last, 16)

                @block.gpsimd
                def _(pool):
                    pool.iota(iota_i[:], [[1, P], [0, 2]], base=0, channel_multiplier=0).then_inc(s_iota, 1)
                    pool.iota(window_i[:], [[1, TILES]], base=MARKED, channel_multiplier=0).then_inc(s_iota, 1)
                    pool.wait_ge(s_most, 1)
                    pool.partition_all_reduce(bound[:], most[:], P, bass.bass_isa.ReduceOp.max)

                @block.vector
                def _(dve):
                    v = nc.vector
                    v.tensor_copy(src_rows[:], node[:, :, 0:W]).then_inc(s_packed, 1)
                    v.tensor_reduce(most[:], node[:, :, HEAD_COLS:W].rearrange("p t h -> p h t"), AX, ALU.max).then_inc(s_most, 1)
                    v.memset(zeros[:], 0.0)
                    v.memset(sums[:], 0.0)
                    dve.wait_ge(s_iota, 2)
                    v.tensor_copy(iota16[:], iota_i[:])
                    v.tensor_copy(tile_marks[:], window_i[:])

        picked = sp.sb("picked", [P, SEGMENTS, TAKEN])
        split = sp.sb("split", [P, WINDOWS, PICKED])
        there = sp.sb("there", [P, WINDOWS, PICKED])
        count, fullest = sp.sb("count", [P, WINDOWS]), sp.sb("fullest", [P, WINDOWS])
        turns_f = sp.sb("turns_f", [P, WINDOWS])
        turns_i, turns_of = sp.sb("turns_i", [P, WINDOWS], I32), sp.sb("turns_of", [P, WINDOWS], I32)
        now = sp.sb("now", [P, PICKED])
        a_dst_now, marks_now = sp.sb("a_dst_now", [P, NH, WT]), sp.sb("marks_now", [P, WT])
        top8 = sp.sb("top8", [P, 2, CH])
        sidx, part_i, tile_i = (sp.sb(n, [P, 2, CH], I32) for n in ("sidx", "part_i", "tile_i"))
        part16, tile_f = sp.sb("part16", [P, 2, CH], BF16), sp.sb("tile_f", [P, 2, CH])
        rows = sp.sb("rows", [P, 2, CH, W])
        LO16 = sp.sb("LO16", [P, 2, CH // 2, P, 2], BF16)
        LO, LOT = sp.sb("LO", [P, 2, CH, P]), sp.sb("LOT", [P, 2, CH, P])
        HI = sp.sb("HI", [P, 2, CH, WT])
        choice = sp.sb("choice", [P, 2, CH, NH, WT])
        a_dst_e = sp.sb("a_dst_e", [P, 2, CH, NH])
        z = sp.sb("z", [P, 2, 2, CH, NH])
        zd = sp.sb("zd", [P, 2, CH, NH])
        val = sp.sb("val", [P, 2, CH, W])
        spreadv = sp.sb("spreadv", [P, 2, CH, W, WT])
        tick = sp.sb("tick", [P, 2])
        with ExitStack() as ctx2:
            s2 = Space(nc, ctx2, "gat_edges")
            acc = s2.ps("acc", [P, 512])
            psA = s2.ps("psA", [P, 2, 512])
            psT = [s2.ps(f"psT{u}", [P, 512]) for u in range(2)]
            psT16 = [p[:].bitcast(BF16).rearrange("p (i e) -> p i e", i=CH) for p in psT]
            with nc.Fori(0, nc.values_load(cell[0:1, 0:1], min_val=1, max_val=MAX_PASSES)) as _pass:
                pick_keys(nc, keys, picked, split, there, count, fullest, turns_f, turns_i, turns_of)
                with nc.Fori(0, WINDOWS) as w:
                    with ExitStack() as ctx3:
                        edge_window(nc, Space(nc, ctx3, "gat_window"), w, {**locals(), "ident16": k["ident16"], "ones": k["ones"]})

        def rows3(ap, n=TILES):
            return ap.unsqueeze(1).to_broadcast([P, n, ap.shape[-1]])
        own, far, lead = (sp.sb(n, [P, TILES, NH]) for n in ("own", "far", "lead"))
        eown, efar = sp.sb("eown", [P, TILES, NH]), sp.sb("efar", [P, TILES, NH])
        by_node = sp.sb("by_node", [P, TILES, W])
        agg, tmp = sp.sb("agg", [P, TILES, HEAD_COLS]), sp.sb("tmp", [P, TILES, HEAD_COLS])
        dens = sp.sb("dens", [P, TILES, NH])
        b_gat, gamma, beta = (sp.sb(n, [P, HEAD_COLS]) for n in ("b_gat", "gamma", "beta"))
        m64, v64, r64, half = (sp.sb(n, [P, TILES]) for n in ("m64", "v64", "r64", "half"))
        scores = sp.sb("scores", [P, TILES, GAT_EXPERTS])
        f_load, f_z, f_e, f_var, f_r, f_link = (sp.sem(n) for n in ("f_load", "f_z", "f_e", "f_var", "f_r", "f_link"))
        with nc.Block() as block:
            @block.sync
            def _(eng):
                eng.wait_ge(s_last, 16)
                for dst, name in ((b_gat, "b_gat"), (gamma, "ln_gamma"), (beta, "ln_beta")):
                    eng.dma_start(dst[:], A[name].unsqueeze(0).to_broadcast([P, HEAD_COLS])).then_inc(f_load, 16)

            @block.scalar
            def _(act):
                act.wait_ge(f_z, 1)
                nc.scalar.activation(eown[:], own[:], ACT.Exp)
                nc.scalar.activation(efar[:], far[:], ACT.Exp).then_inc(f_e, 1)

            @block.gpsimd
            def _(pool):
                pool.memset(half[:], -0.5).then_inc(f_r, 1)
                pool.wait_ge(f_r, 1)
                pool.wait_ge(f_var, 1)
                pool.tensor_tensor(r64[:], v64[:], half[:], ALU.pow).then_inc(f_r, 1)

            @block.vector
            def _(dve):
                v = nc.vector
                L = Steps(dve, f_link)
                do = L.done
                a_src, a_dst = node[:, :, HEAD_COLS:W], node[:, :, W:W + NH]
                dve.wait_ge(s_last, 16)
                dve.wait_ge(f_load, 48)
                do(v.tensor_copy(by_node[:].rearrange("p (w t) f -> p w t f", w=WINDOWS), sums[:].rearrange("p w f t -> p w t f")))
                do(v.tensor_tensor(lead[:], a_dst, rows3(bound[:]), ALU.add))
                do(v.scalar_tensor_tensor(floor[:], lead[:], 0.2, lead[:], ALU.mult, ALU.max))
                do(v.tensor_tensor(own[:], a_src, a_dst, ALU.add))
                do(v.scalar_tensor_tensor(lead[:], own[:], 0.2, own[:], ALU.mult, ALU.max))
                do(v.tensor_tensor(own[:], lead[:], floor[:], ALU.subtract))
                do(v.tensor_tensor(far[:], a_dst, rows3(last_row[:, HEAD_COLS:W]), ALU.add))
                do(v.scalar_tensor_tensor(lead[:], far[:], 0.2, far[:], ALU.mult, ALU.max))
                v.tensor_tensor(far[:], lead[:], floor[:], ALU.subtract).then_inc(f_z, 1)
                dve.wait_ge(f_e, 1)
                do(v.tensor_tensor(efar[:], efar[:], spread(far_count[:], NH), ALU.mult))
                do(v.tensor_tensor(dens[:], eown[:], efar[:], ALU.add))
                do(v.tensor_tensor(dens[:], dens[:], by_node[:, :, HEAD_COLS:W], ALU.add))
                do(v.tensor_scalar(dens[:], dens[:], 1e-37, None, ALU.max))
                do(v.reciprocal(dens[:], dens[:]))
                for h in range(NH):
                    c = slice(h * NH, (h + 1) * NH)
                    L.mark(v.tensor_tensor(agg[:, :, c], node[:, :, c], spread(eown[:, :, h], NH), ALU.mult))
                    L.mark(v.tensor_tensor(tmp[:, :, c], rows3(last_row[:, c]), spread(efar[:, :, h], NH), ALU.mult))
                dve.wait_ge(f_link, L.n)
                do(v.tensor_tensor(agg[:], agg[:], tmp[:], ALU.add))
                do(v.tensor_tensor(agg[:], agg[:], by_node[:, :, 0:HEAD_COLS], ALU.add))
                for h in range(NH):
                    c = slice(h * NH, (h + 1) * NH)
                    L.mark(v.tensor_tensor(tmp[:, :, c], agg[:, :, c], spread(dens[:, :, h], NH), ALU.mult))
                dve.wait_ge(f_link, L.n)
                do(v.tensor_tensor(agg[:], tmp[:], rows3(b_gat[:]), ALU.add))
                do(v.tensor_reduce(m64[:], agg[:], AX, ALU.add))
                do(v.tensor_scalar(m64[:], m64[:], 1.0 / HEAD_COLS, None, ALU.mult))
                do(v.tensor_tensor(agg[:], agg[:], spread(m64[:], HEAD_COLS), ALU.subtract))
                do(v.tensor_tensor(tmp[:], agg[:], agg[:], ALU.mult))
                do(v.tensor_reduce(m64[:], tmp[:], AX, ALU.add))
                v.tensor_scalar(v64[:], m64[:], 1.0 / HEAD_COLS, LN_EPS, ALU.mult, ALU.add).then_inc(f_var, 1)
                dve.wait_ge(f_r, 2)
                do(v.tensor_tensor(agg[:], agg[:], spread(r64[:], HEAD_COLS), ALU.mult))
                do(v.tensor_tensor(agg[:], agg[:], rows3(gamma[:]), ALU.mult))
                do(v.tensor_tensor(agg[:], agg[:], rows3(beta[:]), ALU.add))
                do(v.tensor_reduce(scores[:], agg[:].rearrange("p t (h e) -> p t e h", h=NH), AX, ALU.add))
                do(v.tensor_scalar(scores[:], scores[:], 1.0 / NH, None, ALU.mult))
        gates_of(nc, "gat_gate", scores[:], GAT_EXPERTS, 0.0, parts)


def second_ffn_stage(nc, k, X, xnT, A, parts):
    E, hid = GAT_EXPERTS, 2 * C
    cuts = [(0, P), (P, P)]
    with ExitStack() as ctx:
        sp = Space(nc, ctx, "ffn")
        w1 = sp.sb("w1", [P, E * hid])
        w2 = sp.sb("w2", [P, E * len(cuts), C])
        b1 = sp.sb("b1", [P, E * len(cuts)])
        b2, rest = sp.sb("b2", [3 * E, C]), sp.sb("rest", [3 * E, 2, C])
        b2_parts = sp.sb("b2_parts", [3 * E, 3, C], BF16)
        load_now(nc, "ffn_b2", [(b2[part * E:(part + 1) * E, :], A["b2"]) for part in range(3)])
        s_split = sp.sem("split")
        with nc.Block() as block:
            @block.vector
            def _(dve):
                v = nc.vector
                link = Steps(dve, s_split)
                link.done(v.tensor_copy(b2_parts[:, 0, :], b2[:]))
                link.done(v.tensor_tensor(rest[:, 0, :], b2[:], b2_parts[:, 0, :], ALU.subtract))
                link.done(v.tensor_copy(b2_parts[:, 1, :], rest[:, 0, :]))
                link.done(v.tensor_tensor(rest[:, 1, :], rest[:, 0, :], b2_parts[:, 1, :], ALU.subtract))
                v.tensor_copy(b2_parts[:, 2, :], rest[:, 1, :])
        pairs = [(w1[:].rearrange("c (e h) -> c e h", e=E), A["W1"].rearrange("e c h -> c e h")),
                 (w2[:], A["W2"].rearrange("e (k p) c -> p (e k) c", p=P)),
                 (b1[:], A["b1"])]
        experts(nc, "ffn_mix", k, X, xnT, parts, E, cuts, (w1, None), w2, Loads(pairs),
                (ACT.Gelu, lambda i: b1[:, i:i + 1]), b2=b2_parts)


def program(nc, A, out):
    rows = lambda ap: ap.rearrange("(b p c) d -> p b c d", p=P, c=GT)
    with ExitStack() as ctx:
        k = constants(nc, ctx)
        sp = Space(nc, ctx, "all")
        X = sp.sb("X", [P, TILES, C])
        x4 = X[:].rearrange("p (b c) d -> p b c d", c=GT)
        load_now(nc, "x_in", [(x4, rows(A["x"]))])
        edge_attention_stage(nc, k, X, A)
        xnT = sp.sb("xnT", [C, TOKENS])
        parts = sp.sb("gate_parts", [P, TILES, 3, GAT_EXPERTS], BF16)
        with ExitStack() as ctx2:
            s2 = Space(nc, ctx2, "graph")
            keys, far_count, cell = s2.sb("keys", [P, LANE]), s2.sb("far_count", [P, TILES]), s2.sb("cell", [P, 1], I32)
            with ExitStack() as ctx3:
                s3 = Space(nc, ctx3, "targets")
                lo16, hi16 = s3.sb("lo16", [P, LANE], BF16), s3.sb("hi16", [P, LANE], BF16)
                iota16, iota1_16 = s3.sb("iota16", [P, P, 2], BF16), s3.sb("iota1_16", [P, TILES, 2], BF16)
                edge_keys_stage(nc, k, A, keys, lo16, hi16, iota16, iota1_16, cell)
                moe_stage(nc, k, X, xnT, A,
                          lambda space, chunks: Tally(nc, space, chunks, lo16, hi16, iota16, iota1_16, far_count))
            dense_attention_stage(nc, k, X, xnT, A)
            gat_stage(nc, k, X, xnT, A, keys, far_count, cell, parts)
        second_ffn_stage(nc, k, X, xnT, A, parts)
        load_now(nc, "x_out", [(rows(out), x4)])


def kernel(**inputs):
    import concourse.bacc as bacc
    from concourse.bass_utils import run_bass_kernel_spmd

    def plain(name):
        return np.ascontiguousarray(inputs[name])

    def turned(name, *order):
        return np.ascontiguousarray(np.transpose(inputs[name], order))

    hid = inputs["L0_ffn_w1"].shape[1]
    arrays = {
        "x": plain("x").reshape(TOKENS, C), "adj": plain("adj"),
        "W_linT": turned("L0_gnn_W_lin", 1, 0), "W_valT": turned("L0_gnn_W_val", 1, 0),
        "W_outT": turned("L0_gnn_W_out", 1, 0), "a": plain("L0_gnn_a"),
        "src": plain("L0_gnn_src"), "dst": plain("L0_gnn_dst"),
        "router_wT": turned("L0_ffn_router_w", 1, 0),
        "w1T": turned("L0_ffn_w1", 2, 0, 1).reshape(C, -1), "w3T": turned("L0_ffn_w3", 2, 0, 1).reshape(C, -1),
        "w2T": turned("L0_ffn_w2", 0, 2, 1),
        **{n: plain("L1_gnn_" + n) for n in ("Wq", "Wk", "Wo", "bq", "bk", "bv", "bo")},
        "WvT": turned("L1_gnn_Wv", 1, 0),
        "alpha": plain("L1_gnn_alpha").reshape(1), "gamma": plain("L1_gnn_gamma").reshape(1),
        "W_gat": plain("L1_ffn_W_gat"), "W_gatT": turned("L1_ffn_W_gat", 1, 0),
        **{n: plain("L1_ffn_" + n) for n in ("att_src", "att_dst", "b_gat", "ln_gamma", "ln_beta", "W1", "W2", "b2", "edge_index")},
        "b1": np.ascontiguousarray(np.transpose(np.reshape(inputs["L1_ffn_b1"], (-1, P)))),
    }
    nc = bacc.Bacc("TRN2", target_bir_lowering=False, num_devices=1)
    A = {n: nc.dram_tensor(f"in_{n}", a.shape, mybir.dt.from_np(a.dtype), kind="ExternalInput").ap()
         for n, a in arrays.items()}
    out = nc.dram_tensor("out_x", (TOKENS, C), F32, kind="ExternalOutput").ap()
    program(nc, A, out)
    r = run_bass_kernel_spmd(nc, [{f"in_{n}": a for n, a in arrays.items()}], core_ids=[0])
    return r.results[0]["out_x"].reshape(BATCH, NODES, C)
```

```python
from contextlib import ExitStack

import numpy as np

import concourse.bass as bass
from concourse import mybir

ALU = mybir.AluOpType
ACT = mybir.ActivationFunctionType
AX = mybir.AxisListType.X
F32 = mybir.dt.float32
BF16 = mybir.dt.bfloat16
I32 = mybir.dt.int32
P = 128
BATCH, NODES, C = 16, 512, 128
TOKENS = BATCH * NODES
TILES = TOKENS // P
GT = NODES // P
GROUPS = BATCH
PAIRS = GROUPS // 2
LN_EPS = 1e-5
SRC_NODES = TOKENS
EDGES2 = 524288
LANE = EDGES2 // P
NODE_BITS, PART_BITS = 13, 7
TILE_SHIFT = NODE_BITS + PART_BITS
KEY_MARK = 1 << 29
MARKED = KEY_MARK >> TILE_SHIFT
SEGMENTS = 8
SEGMENT = LANE // SEGMENTS
TAKEN = 64
MAX_PASSES = -(-SEGMENT // TAKEN)
PICKED = SEGMENTS * TAKEN
CH = 8
HCOLS = 8
HOTS = 4


class Steps:

    def __init__(self, eng, sem, base=0):
        self.eng, self.sem, self.base, self.n = eng, sem, base, 0

    def mark(self, ins):
        self.n += 1
        ins.then_inc(self.sem, 1)

    def done(self, ins):
        self.n += 1
        ins.then_inc(self.sem, 1)
        self.eng.wait_ge(self.sem, self.base + self.n)


def credit(eng, *counts):
    for sems, n in counts:
        for sem in sems:
            eng.sem_inc(sem, n)


def spread(ap, n):
    return ap.unsqueeze(2).to_broadcast([*ap.shape, n])


class Space:

    def __init__(self, nc, ctx, stage):
        self.nc, self.ctx, self.stage = nc, ctx, stage
        self.taken = []
        ctx.callback(self.release)

    def release(self):
        if self.taken:
            self.nc.clear_and_free_semaphores(self.taken)
            self.nc.all_engine_barrier()

    def sb(self, name, shape, dt=F32):
        return self.ctx.enter_context(self.nc.sbuf_tensor(f"{self.stage}_{name}", shape, dt))

    def ps(self, name, shape, dt=F32):
        return self.ctx.enter_context(self.nc.psum_tensor(f"{self.stage}_{name}", shape, dt))

    def sem(self, name):
        self.taken.append(self.nc.alloc_semaphore(f"{self.stage}_{name}"))
        return self.taken[-1]

    def sems(self, name, n=2):
        return [self.sem(f"{name}{i}") for i in range(n)]


def constants(nc, ctx):
    sp = Space(nc, ctx, "const")
    ident = sp.sb("ident", [P, P])
    ident16 = sp.sb("ident16", [P, P], BF16)
    minus_half = sp.sb("minus_half", [P, GT])
    ones = sp.sb("ones", [P, P])
    cleared, drawn = sp.sem("cleared"), sp.sem("drawn")
    with nc.Block() as block:
        @block.gpsimd
        def _(pool):
            pool.memset(ident[:], 0.0).then_inc(cleared, 1)
            pool.memset(minus_half[:], -0.5)
            pool.memset(ones[:], 1.0)
            pool.wait_ge(cleared, 1)
            pool.affine_select(out=ident[:], in_=ident[:], compare_op=ALU.not_equal, fill=1.0, base=0,
                               pattern=[[-1, P]], channel_multiplier=1).then_inc(drawn, 1)
            pool.wait_ge(drawn, 1)
            pool.tensor_copy(ident16[:], ident[:])
    return {"ident": ident, "ident16": ident16, "minus_half": minus_half, "ones": ones}


def normalise(nc, stage, k, X, xnT, w_small, small, width, rows=None):
    with ExitStack() as ctx:
        sp = Space(nc, ctx, stage)
        total, mean = sp.sb("total", [P, 2, GT]), sp.sb("mean", [P, 2, GT])
        centred, squares = sp.sb("centred", [P, 2, GT, C]), sp.sb("squares", [P, 2, GT, C])
        sqsum, var, rstd = (sp.sb(n, [P, 2, GT]) for n in ("sqsum", "var", "rstd"))
        xn, xT = sp.sb("xn", [P, 2, GT, C]), sp.sb("xT", [P, 2, NODES])
        psT = sp.ps("psT", [P, 2, 512])
        psS = sp.ps("psS", [P, 2, 512])
        s_link = sp.sems("link")
        s_centred, s_squared, s_var, s_rstd = (sp.sems(n) for n in ("s_centred", "s_squared", "s_var", "s_rstd"))
        s_normed, s_turned, s_xT, s_small, s_kept = (
            sp.sems(n) for n in ("s_normed", "s_turned", "s_xT", "s_small", "s_kept"))
        with nc.Block() as block:
            @block.sync
            def _(eng):
                credit(eng, (s_link, 3), (s_centred + s_squared + s_var + s_rstd, 1),
                       (s_normed + s_turned + s_xT + s_small + s_kept, 1))

            @block.vector
            def _(dve):
                def centre(j, u):
                    link = Steps(dve, s_link[u], j * 3)
                    x4 = X[:, bass.ds((2 * (j - 1) + u) * GT, GT), :]
                    link.done(nc.vector.tensor_reduce(total[:, u], x4, AX, ALU.add))
                    link.done(nc.vector.tensor_scalar(mean[:, u], total[:, u], 1.0 / C, None, ALU.mult))
                    nc.vector.tensor_tensor(centred[:, u], x4, spread(mean[:, u], C),
                                            ALU.subtract).then_inc(s_centred[u], 1)

                def variance(j, u):
                    link = Steps(dve, s_link[u], j * 3 + 2)
                    dve.wait_ge(s_squared[u], j + 1)
                    link.done(nc.vector.tensor_reduce(sqsum[:, u], squares[:, u], AX, ALU.add))
                    nc.vector.tensor_scalar(var[:, u], sqsum[:, u], 1.0 / C, LN_EPS, ALU.mult,
                                            ALU.add).then_inc(s_var[u], 1)

                def scale(j, u):
                    dve.wait_ge(s_rstd[u], j + 1)
                    dve.wait_ge(s_turned[u], j)
                    if rows is not None:
                        dve.wait_ge(s_xT[u], j)
                    nc.vector.tensor_tensor(xn[:, u], centred[:, u], spread(rstd[:, u], C),
                                            ALU.mult).then_inc(s_normed[u], 1)

                for u in range(2):
                    centre(1, u)
                with dve.Fori(1, PAIRS) as j:
                    for u in range(2):
                        variance(j, u)
                    for u in range(2):
                        scale(j, u)
                        centre(j + 1, u)
                for u in range(2):
                    variance(PAIRS, u)
                for u in range(2):
                    scale(PAIRS, u)

            @block.gpsimd
            def _(pool):
                with pool.Fori(1, PAIRS + 1) as j:
                    for u in range(2):
                        pool.wait_ge(s_centred[u], j + 1)
                        pool.tensor_tensor(squares[:, u], centred[:, u], centred[:, u],
                                           ALU.mult).then_inc(s_squared[u], 1)
                    for u in range(2):
                        pool.wait_ge(s_var[u], j + 1)
                        pool.tensor_tensor(rstd[:, u], var[:, u], k["minus_half"][:],
                                           ALU.pow).then_inc(s_rstd[u], 1)

            @block.tensor
            def _(pe):
                with pe.Fori(1, PAIRS + 1) as j:
                    for u in range(2):
                        pe.wait_ge(s_normed[u], j + 1)
                        pe.wait_ge(s_xT[u], j)
                        for t in range(GT):
                            last = nc.tensor.transpose(psT[:, u, t * P:(t + 1) * P], xn[:, u, t, :], k["ident"][:])
                        last.then_inc(s_turned[u], 1)
                    for u in range(2):
                        if w_small is None:
                            continue
                        pe.wait_ge(s_xT[u], j + 1)
                        pe.wait_ge(s_kept[u], j)
                        for t in range(GT):
                            last = nc.tensor.matmul(psS[:, u, t * width:(t + 1) * width], xT[:, u, t * P:(t + 1) * P],
                                                    w_small, start=True, stop=True)
                        last.then_inc(s_small[u], 1)

            @block.scalar
            def _(act):
                with act.Fori(1, PAIRS + 1) as j:
                    for u in range(2):
                        g = 2 * (j - 1) + u
                        act.wait_ge(s_turned[u], j + 1)
                        if w_small is not None:
                            act.wait_ge(s_small[u], j)
                            last = nc.scalar.copy(xT[:, u, :], psT[:, u, :])
                        if rows is not None:
                            last = nc.scalar.copy(rows[:, bass.ds(g * GT, GT), :], xn[:, u])
                            last.then_inc(s_xT[u], 1)
                            continue
                        nc.scalar.copy(xnT[:, bass.ds(g * NODES, NODES)], psT[:, u, :]).then_inc(s_xT[u], 1)
                    for u in range(2):
                        if w_small is None:
                            continue
                        g = 2 * (j - 1) + u
                        act.wait_ge(s_small[u], j + 1)
                        nc.scalar.copy(small[:, bass.ds(g * GT, GT), :],
                                       psS[:, u, 0:GT * width].rearrange("p (t w) -> p t w", t=GT)).then_inc(s_kept[u], 1)


def top_two(dve, link, sp, logits, rank, d, both, m, n):
    eq, one = sp.sb("eq", [P, TILES, n]), sp.sb("one", [P, TILES, n])
    place = sp.sb("place", [P, TILES])
    rank_b = rank.unsqueeze(1).to_broadcast([P, TILES, n])
    link.done(dve.tensor_reduce(m[:], logits, AX, ALU.max))
    link.done(dve.tensor_tensor(d[:], logits, spread(m[:], n), ALU.subtract))
    link.done(dve.scalar_tensor_tensor(eq[:], d[:], 0.0, rank_b, ALU.is_equal, ALU.mult))
    link.done(dve.tensor_reduce(place[:], eq[:], AX, ALU.max))
    link.done(dve.tensor_tensor(both[:], rank_b, spread(place[:], n), ALU.is_equal))
    link.done(dve.scalar_tensor_tensor(one[:], both[:], -1e30, d[:], ALU.mult, ALU.add))
    link.done(dve.tensor_reduce(m[:], one[:], AX, ALU.max))
    link.done(dve.tensor_tensor(eq[:], one[:], spread(m[:], n), ALU.is_equal))
    link.done(dve.tensor_tensor(eq[:], eq[:], rank_b, ALU.mult))
    link.done(dve.tensor_reduce(place[:], eq[:], AX, ALU.max))
    link.done(dve.tensor_tensor(eq[:], rank_b, spread(place[:], n), ALU.is_equal))
    link.done(dve.tensor_tensor(both[:], both[:], eq[:], ALU.add))


def gates_of(nc, stage, logits, n, eps, gate_parts):
    with ExitStack() as ctx:
        sp = Space(nc, ctx, stage)
        rank_i, rank = sp.sb("rank_i", [P, n], I32), sp.sb("rank", [P, n])
        d, both, e, g, rest = (sp.sb(x, [P, TILES, n]) for x in ("d", "both", "e", "g", "rest"))
        m, s = sp.sb("m", [P, TILES]), sp.sb("s", [P, TILES])
        s_rank, s_link, s_d, s_e = (sp.sem(x) for x in ("s_rank", "s_link", "s_d", "s_e"))
        with nc.Block() as block:
            @block.gpsimd
            def _(pool):
                pool.iota(rank_i[:], [[-1, n]], base=n, channel_multiplier=0).then_inc(s_rank, 1)

            @block.scalar
            def _(act):
                act.wait_ge(s_d, 1)
                nc.scalar.activation(e[:], d[:], ACT.Exp).then_inc(s_e, 1)

            @block.vector
            def _(dve):
                link = Steps(dve, s_link)
                dve.wait_ge(s_rank, 1)
                link.done(nc.vector.tensor_copy(rank[:], rank_i[:]))
                top_two(nc.vector, link, sp, logits, rank[:], d, both, m, n)
                nc.vector.tensor_copy(s[:], m[:]).then_inc(s_d, 1)
                dve.wait_ge(s_e, 1)
                dve.wait_ge(s_d, 1)
                link.done(nc.vector.tensor_reduce(s[:], e[:], AX, ALU.add))
                link.done(nc.vector.reciprocal(m[:], s[:]))
                link.done(nc.vector.tensor_tensor(g[:], e[:], spread(m[:], n), ALU.mult))
                link.done(nc.vector.tensor_tensor(g[:], g[:], both[:], ALU.mult))
                link.done(nc.vector.tensor_reduce(s[:], g[:], AX, ALU.add))
                link.done(nc.vector.tensor_scalar(s[:], s[:], eps, None, ALU.add))
                link.done(nc.vector.reciprocal(m[:], s[:]))
                link.done(nc.vector.tensor_tensor(g[:], g[:], spread(m[:], n), ALU.mult))
                link.done(nc.vector.tensor_copy(gate_parts[:, :, 0, :], g[:]))
                link.done(nc.vector.tensor_tensor(rest[:], g[:], gate_parts[:, :, 0, :], ALU.subtract))
                link.done(nc.vector.tensor_copy(gate_parts[:, :, 1, :], rest[:]))
                link.done(nc.vector.tensor_tensor(g[:], rest[:], gate_parts[:, :, 1, :], ALU.subtract))
                nc.vector.tensor_copy(gate_parts[:, :, 2, :], g[:])


def experts(nc, stage, k, X, xnT, gate_parts, n, cuts, w1, second, load, act_func, b2):
    hidden = sum(c for _, c in cuts)
    K = n * len(cuts)
    GB = 2
    HB = 4
    with ExitStack() as ctx:
        sp = Space(nc, ctx, stage)
        picks = sp.sb("picks", [3 * n, n, P], BF16)
        picks_f = sp.sb("picks_f", [3 * n, n, P])
        gate_now = sp.sb("gate_now", [P, 2, GT, 3 * n], BF16)
        gT = sp.sb("gT", [3 * n, 2, NODES], BF16)
        S, H = (sp.sb(x, [P, HB, NODES]) for x in ("S", "H"))
        yT = sp.sb("yT", [P, 2, NODES])
        ps1 = sp.ps("ps1", [P, 2, 512])
        psG = sp.ps("psG", [P, GB, 512])
        acc = sp.ps("acc", [P, 512])
        psX = sp.ps("psX", [P, 512])
        psX16 = psX[:, 0:256].bitcast(BF16)
        (s_load, s_picks0, s_picks, s_up, s_S, s_gate, s_H, s_down) = (
            sp.sem(x) for x in ("s_load", "s_picks0", "s_picks", "s_up", "s_S", "s_gate", "s_H", "s_down"))
        s_now, s_gturn, s_gT, s_acc, s_y, s_yturn, s_added = (
            sp.sems(x) for x in ("s_now", "s_gturn", "s_gT", "s_acc", "s_y", "s_yturn", "s_added"))
        with nc.Block() as block:
            @block.sync
            def _(sp_eng):
                credit(sp_eng, ((s_up, s_S, s_H, s_down), 2 * K), ((s_gate,), 2 * n),
                       (s_now + s_gturn + s_gT + s_acc + s_y + s_yturn + s_added, 1))
                loads = load(sp_eng, s_load)
                sp_eng.wait_ge(s_load, loads)

            @block.gpsimd
            def _(pool):
                pool.memset(picks_f[:], 0.0).then_inc(s_picks0, 1)
                for part in range(3):
                    pool.wait_ge(s_picks0, part + 1)
                    pool.affine_select(out=picks_f[:], in_=picks_f[:], compare_op=ALU.not_equal, fill=1.0,
                                       base=-part * n, pattern=[[-1, n], [0, P]],
                                       channel_multiplier=1).then_inc(s_picks0, 1)
                pool.wait_ge(s_picks0, 4)
                pool.tensor_copy(picks[:], picks_f[:]).then_inc(s_picks, 1)
                with pool.Fori(1, PAIRS + 1) as j:
                    for u in range(2):
                        g = 2 * (j - 1) + u
                        pool.wait_ge(s_gturn[u], j)
                        pool.tensor_copy(gate_now[:, u], gate_parts[:, bass.ds(g * GT, GT), :, :]
                                         .rearrange("p t a e -> p t (a e)")).then_inc(s_now[u], 1)

            @block.tensor
            def _(pe):
                pe.wait_ge(s_load, load.total)
                pe.wait_ge(s_picks, 1)
                with pe.Fori(1, PAIRS + 1) as j:
                    for u in range(2):
                        g = 2 * (j - 1) + u
                        xg = xnT[:, bass.ds(g * NODES, NODES)]
                        at = lambda per, i: j * (2 * per) + max(u * per + i, 0)
                        pe.wait_ge(s_now[u], j + 1)
                        pe.wait_ge(s_added[1 - u], j + u)
                        for t in range(GT):
                            last = nc.tensor.transpose(psX16[0:3 * n, t * P:(t + 1) * P], gate_now[:, u, t, :],
                                                       k["ident16"][:])
                        last.then_inc(s_gturn[u], 1)

                        def gates(i):
                            e = i // len(cuts)
                            if i == 0:
                                pe.wait_ge(s_gT[u], j + 1)
                            pe.wait_ge(s_H, at(K, i - (GB - 1) * len(cuts)))
                            nc.tensor.matmul(psG[:, e % GB, :], picks[:, e, :], gT[:, u, :], start=True,
                                             stop=True).then_inc(s_gate, 1)

                        def up(i):
                            e, (c0, rows) = i // len(cuts), cuts[i % len(cuts)]
                            col = e * hidden + c0
                            pe.wait_ge(s_S, at(K, i - 1))
                            last = nc.tensor.matmul(ps1[0:rows, i % 2, :], w1[:, col:col + rows], xg, start=True, stop=True)
                            last.then_inc(s_up, 1)

                        def down(i):
                            rows = cuts[i % len(cuts)][1]
                            pe.wait_ge(s_H, at(K, i + 1))
                            if i == 0:
                                pe.wait_ge(s_y[1 - u], j + u)
                            last = nc.tensor.matmul(acc[:], second[0:rows, i, :], H[0:rows, i % HB, :],
                                                    start=(i == 0), stop=False)
                            if i == K - 1:
                                for q in range(3):
                                    last = nc.tensor.matmul(acc[:], b2[:, q, :], gT[:, u, :], start=False, stop=(q == 2))
                            last.then_inc(s_down, 1)

                        for i in range(K + 2):
                            if i < K:
                                up(i)
                            if i < K and i % len(cuts) == 0:
                                gates(i)
                            if i >= 2:
                                down(i - 2)
                        pe.wait_ge(s_y[u], j + 1)
                        for t in range(GT):
                            last = nc.tensor.transpose(psX[:, t * P:(t + 1) * P], yT[:, u, t * P:(t + 1) * P],
                                                       k["ident"][:])
                        last.then_inc(s_yturn[u], 1)

            @block.scalar
            def _(act):
                with act.Fori(1, PAIRS + 1) as j:
                    for u in range(2):
                        at = lambda per, i: j * (2 * per) + max(u * per + i, 0)
                        act.wait_ge(s_gturn[u], j + 1)
                        nc.scalar.copy(gT[:, u, :], psX16[0:3 * n, :]).then_inc(s_gT[u], 1)
                        for i in range(K):
                            e, rows = i // len(cuts), cuts[i % len(cuts)][1]
                            act.wait_ge(s_up, at(K, i + 1))
                            act.wait_ge(s_H, at(K, i + 1 - HB))
                            b = act_func[1](i)
                            kw = {"bias": b} if b is not None else {}
                            nc.scalar.activation(S[0:rows, i % HB, :], ps1[0:rows, i % 2, :], act_func[0],
                                                 **kw).then_inc(s_S, 1)
                        act.wait_ge(s_down, at(K, K))
                        nc.scalar.copy(yT[:, u, :], acc[:]).then_inc(s_y[u], 1)

            @block.vector
            def _(dve):
                with dve.Fori(1, PAIRS + 1) as j:
                    for u in range(2):
                        g = 2 * (j - 1) + u
                        at = lambda per, i: j * (2 * per) + max(u * per + i, 0)
                        for i in range(K):
                            e, rows = i // len(cuts), cuts[i % len(cuts)][1]
                            dve.wait_ge(s_gate, at(n, e + 1))
                            dve.wait_ge(s_S, at(K, i + 1))
                            dve.wait_ge(s_down, at(K, i + 1 - HB))
                            nc.vector.tensor_tensor(H[0:rows, i % HB, :], S[0:rows, i % HB, :],
                                                    psG[0:rows, e % GB, :], ALU.mult).then_inc(s_H, 1)
                        dve.wait_ge(s_yturn[u], j + 1)
                        x4 = X[:, bass.ds(g * GT, GT), :]
                        nc.vector.tensor_tensor(x4, x4, psX[:].rearrange("p (t c) -> p t c", t=GT),
                                                ALU.add).then_inc(s_added[u], 1)


class Loads:

    def __init__(self, pairs):
        self.pairs = pairs
        self.total = 16 * len(pairs)

    def __call__(self, eng, sem):
        for dst, src in self.pairs:
            eng.dma_start(dst, src).then_inc(sem, 16)
        return self.total


def load_now(nc, name, pairs):
    with ExitStack() as ctx:
        sem = Space(nc, ctx, name).sem("loaded")
        block = ctx.enter_context(nc.Block())

        @block.sync
        def _(sp_eng):
            for dst, src in pairs:
                sp_eng.dma_start(dst, src).then_inc(sem, 16)
            sp_eng.wait_ge(sem, 16 * len(pairs))


MOE_EXPERTS, MOE_HIDDEN = 8, 341
MOE_CUTS = [(0, P), (P, P), (2 * P, MOE_HIDDEN - 2 * P)]
SORTED_MOST = 2 * TOKENS // NODES + MOE_EXPERTS
SORTED = SORTED_MOST + 2
TALLY_BATCHES = EDGES2 // P // HCOLS
TALLY_MIX = 16
TALLY_TURNS = TOKENS // NODES
TALLY_BACK = 12
TALLY_OUT = 8
FILLS = 2 * SORTED - 2 * TALLY_TURNS


def route_stage(nc, k, logits, place_i, gates, expert_of, turns_of):
    E = MOE_EXPERTS
    with ExitStack() as ctx:
        sp = Space(nc, ctx, "route")
        rank_i, rank = sp.sb("rank_i", [P, E], I32), sp.sb("rank", [P, E])
        d, e, eq, rest, both, place = (sp.sb(n, [P, TILES, E]) for n in ("d", "e", "eq", "rest", "both", "place"))
        one = sp.sb("one", [P, 2, TILES, E])
        run = sp.sb("run", [P, 2, TILES, E])
        top, spot, total, e2 = (sp.sb(n, [P, TILES]) for n in ("top", "spot", "total", "e2"))
        prob, place_f = sp.sb("prob", [P, TILES, 2]), sp.sb("place_f", [P, TILES, 2])
        before = sp.sb("before", [P, P])
        filled, filled_i = sp.sb("filled", [P, E]), sp.sb("filled_i", [P, E], I32)
        ends = sp.sb("ends", [P, 2, E])
        start = sp.sb("start", [P, E])
        group_i, group = sp.sb("group_i", [P, SORTED], I32), sp.sb("group", [P, SORTED])
        past, which = sp.sb("past", [P, SORTED, E]), sp.sb("which", [P, SORTED])
        turns_f, turns_i = sp.sb("turns_f", [P, 1]), sp.sb("turns_i", [P, 1], I32)
        ps = sp.ps("ps", [P, 512])
        s_iota, s_link, s_d, s_e, s_counts, s_summed = (sp.sem(n) for n in ("iota", "link", "d", "e", "counts", "summed"))
        with nc.Block() as block:
            @block.gpsimd
            def _(pool):
                pool.iota(rank_i[:], [[-1, E]], base=E, channel_multiplier=0).then_inc(s_iota, 1)
                pool.iota(group_i[:], [[1, SORTED]], base=0, channel_multiplier=0).then_inc(s_iota, 1)
                pool.affine_select(out=before[:], in_=k["ones"][:], compare_op=ALU.is_gt, fill=0.0, base=0,
                                   pattern=[[1, P]], channel_multiplier=-1).then_inc(s_iota, 1)

            @block.scalar
            def _(act):
                act.wait_ge(s_d, 1)
                nc.scalar.activation(e[:], d[:], ACT.Exp)
                nc.scalar.activation(e2[:], top[:], ACT.Exp).then_inc(s_e, 1)

            @block.tensor
            def _(pe):
                pe.wait_ge(s_iota, 3)
                pe.wait_ge(s_counts, 1)
                nc.tensor.matmul(ps[:, 0:E], before[:], run[:, 0, TILES - 1, :], start=True, stop=True)
                nc.tensor.matmul(ps[:, E:2 * E], k["ones"][:], run[:, 0, TILES - 1, :], start=True, stop=True).then_inc(s_summed, 1)

            @block.vector
            def _(dve):
                v = nc.vector
                link = Steps(dve, s_link)
                do = link.done
                dve.wait_ge(s_iota, 2)
                link.mark(v.tensor_copy(group[:], group_i[:]))
                do(v.tensor_copy(rank[:], rank_i[:]))
                rank_b = rank[:].unsqueeze(1).to_broadcast([P, TILES, E])
                do(v.tensor_reduce(top[:], logits, AX, ALU.max))
                do(v.tensor_tensor(d[:], logits, spread(top[:], E), ALU.subtract))
                do(v.scalar_tensor_tensor(eq[:], d[:], 0.0, rank_b, ALU.is_equal, ALU.mult))
                do(v.tensor_reduce(spot[:], eq[:], AX, ALU.max))
                do(v.tensor_tensor(one[:, 0], rank_b, spread(spot[:], E), ALU.is_equal))
                do(v.scalar_tensor_tensor(rest[:], one[:, 0], -1e30, d[:], ALU.mult, ALU.add))
                v.tensor_reduce(top[:], rest[:], AX, ALU.max).then_inc(s_d, 1)
                dve.wait_ge(s_d, 1)
                do(v.tensor_tensor(eq[:], rest[:], spread(top[:], E), ALU.is_equal))
                do(v.tensor_tensor(eq[:], eq[:], rank_b, ALU.mult))
                do(v.tensor_reduce(spot[:], eq[:], AX, ALU.max))
                do(v.tensor_tensor(one[:, 1], rank_b, spread(spot[:], E), ALU.is_equal))
                do(v.tensor_tensor(both[:], one[:, 0], one[:, 1], ALU.add))
                src = both[:]
                for step in range(6):
                    w, dst = 1 << step, run[:, (step + 1) % 2]
                    link.mark(v.tensor_copy(dst[:, 0:w, :], src[:, 0:w, :]))
                    ins = v.tensor_tensor(dst[:, w:, :], src[:, w:, :], src[:, 0:TILES - w, :], ALU.add)
                    if step == 5:
                        link.mark(ins)
                        dve.wait_ge(s_link, link.n)
                    else:
                        do(ins)
                    src = dst
                do(v.tensor_tensor(place[:], run[:, 0], both[:], ALU.subtract))
                v.tensor_copy(start[:], rank[:]).then_inc(s_counts, 1)
                dve.wait_ge(s_e, 1)
                do(v.tensor_reduce(total[:], e[:], AX, ALU.add))
                do(v.reciprocal(prob[:, :, 0], total[:]))
                do(v.tensor_tensor(prob[:, :, 1], prob[:, :, 0], e2[:], ALU.mult))
                do(v.tensor_tensor(total[:], prob[:, :, 0], prob[:, :, 1], ALU.add))
                do(v.tensor_scalar(total[:], total[:], 1e-9, None, ALU.add))
                do(v.reciprocal(e2[:], total[:]))
                link.mark(v.tensor_tensor(gates[:], prob[:], spread(e2[:], 2), ALU.mult))
                dve.wait_ge(s_summed, 1)
                do(v.tensor_scalar(filled[:], ps[:, E:2 * E], float(NODES - 1), None, ALU.add))
                do(v.tensor_copy(filled_i[:], filled[:]))
                do(v.tensor_scalar(filled_i[:], filled_i[:], NODES.bit_length() - 1, None, ALU.logical_shift_right))
                do(v.tensor_copy(filled[:], filled_i[:]))
                src = filled[:]
                for step in range(3):
                    w, dst = 1 << step, ends[:, step % 2]
                    link.mark(v.tensor_copy(dst[:, 0:w], src[:, 0:w]))
                    do(v.tensor_tensor(dst[:, w:], src[:, w:], src[:, 0:E - w], ALU.add))
                    src = dst
                do(v.tensor_tensor(start[:], src, filled[:], ALU.subtract))
                do(v.scalar_tensor_tensor(start[:], start[:], float(NODES), ps[:, 0:E], ALU.mult, ALU.add))
                do(v.tensor_tensor(place[:], place[:], start[:].unsqueeze(1).to_broadcast([P, TILES, E]), ALU.add))
                for i in range(2):
                    do(v.tensor_tensor(eq[:], place[:], one[:, i], ALU.mult))
                    do(v.tensor_reduce(place_f[:, :, i], eq[:], AX, ALU.add))
                link.mark(v.tensor_copy(place_i[:], place_f[:]))
                do(v.tensor_tensor(past[:], spread(group[:], E), src.unsqueeze(1).to_broadcast([P, SORTED, E]), ALU.is_ge))
                do(v.tensor_reduce(which[:], past[:], AX, ALU.add))
                do(v.tensor_scalar(which[:], which[:], float(E - 1), None, ALU.min))
                link.mark(v.tensor_copy(expert_of[:], which[:]))
                do(v.tensor_scalar(turns_f[:], src[:, E - 1:E], 3.0, float(2 * (TALLY_TURNS + 2)), ALU.add, ALU.max))
                do(v.tensor_copy(turns_i[:], turns_f[:]))
                v.tensor_scalar(turns_of[:], turns_i[:], 1, None, ALU.logical_shift_right)


def moe_stage(nc, k, X, rows, A, tally, x_sorted, y_sorted, s_empty):
    E, cuts = MOE_EXPERTS, MOE_CUTS
    with ExitStack() as ctx:
        sp = Space(nc, ctx, "moe")
        router = sp.sb("router", [P, E])
        logits = sp.sb("logits", [P, TILES, E])
        place_i, gates = sp.sb("place_i", [P, TILES, 2], I32), sp.sb("gates", [P, TILES, 2])
        expert_of, turns_of = sp.sb("expert_of", [P, SORTED], I32), sp.sb("turns_of", [P, 1], I32)
        group_rows = lambda t, g: t[bass.ds(g * NODES, NODES), :].rearrange("(p c) d -> p c d", c=GT)
        load_now(nc, "moe_first", [(router[:], A["router_wT"])])
        normalise(nc, "moe_ln", k, X, None, router[:], logits, E, rows=rows)
        route_stage(nc, k, logits[:], place_i, gates, expert_of, turns_of)

        with ExitStack() as ctx2:
            s2 = Space(nc, ctx2, "send")
            s_sent = s2.sem("sent")
            turns = (TALLY_BATCHES - TALLY_MIX * TALLY_TURNS - TALLY_BACK * PAIRS) // TALLY_OUT
            with nc.Block() as block:
                @block.gpsimd
                def _(pool):
                    pool.wait_ge(s_empty, 16 * FILLS)
                    for t in range(TILES):
                        for i in range(2):
                            pool.indirect_dma_start(out=x_sorted, out_offset=bass.IndirectOffsetOnAxis(ap=place_i[:, t, i:i + 1], axis=0),
                                                    in_=rows[:, t, :], in_offset=None).then_inc(s_sent, 16)
                    pool.wait_ge(s_sent, 16 * 2 * TILES)

                @block.tensor
                def _(pe):
                    tally.open(pe)
                    with pe.Fori(1, turns + 1) as j:
                        for q in range(TALLY_OUT):
                            tally.add(pe, (j - 1) * TALLY_OUT, q)

                @block.vector
                def _(dve):
                    with dve.Fori(1, turns + 1) as j:
                        for q in range(TALLY_OUT):
                            tally.make(dve, (j - 1) * TALLY_OUT, q)

        with ExitStack() as ctx2:
            sorted_experts(nc, Space(nc, ctx2, "mix"), k, A, expert_of, turns_of, x_sorted, y_sorted, group_rows, tally,
                           turns * TALLY_OUT)

        with ExitStack() as ctx2:
            s2 = Space(nc, ctx2, "back")
            where = s2.sb("where", [P, 2, GT, 2], I32)
            got, weighed = s2.sb("got", [P, 2, GT, 2, C]), s2.sb("weighed", [P, 2, GT, 2, C])
            s_where, s_got, s_weighed = (s2.sems(n) for n in ("where", "got", "weighed"))
            s_first, s_added, s_tick = s2.sems("first"), s2.sems("added"), s2.sems("tick")
            tick = s2.sb("tick", [P, 2])
            first = TALLY_BATCHES - TALLY_BACK * PAIRS
            with nc.Block() as block:
                @block.sync
                def _(eng):
                    credit(eng, (s_where + s_weighed + s_first + s_added + s_tick, 1))

                @block.gpsimd
                def _(pool):
                    with pool.Fori(1, PAIRS + 1) as j:
                        for u in range(2):
                            pool.wait_ge(s_weighed[u], j)
                            pool.wait_ge(s_where[u], j)
                            pool.tensor_copy(where[:, u], place_i[:, bass.ds((2 * (j - 1) + u) * GT, GT), :]).then_inc(s_where[u], 1)
                            pool.wait_ge(s_where[u], j + 1)
                            pool.wait_ge(s_tick[u], j)
                            pool.tensor_tensor(tick[:, u:u + 1], k["ones"][:, 0:1], k["ones"][:, 0:1], ALU.mult).then_inc(s_tick[u], 1)
                            for t in range(GT):
                                for i in range(2):
                                    pool.indirect_dma_start(
                                        out=got[:, u, t, i, :], out_offset=None, in_=y_sorted,
                                        in_offset=bass.IndirectOffsetOnAxis(ap=where[:, u, t, i:i + 1], axis=0)).then_inc(s_got[u], 16)

                @block.tensor
                def _(pe):
                    with pe.Fori(1, PAIRS + 1) as j:
                        for q in range(TALLY_BACK):
                            tally.add(pe, (j - 1) * TALLY_BACK + first, q)
                    tally.close()

                @block.vector
                def _(dve):
                    with dve.Fori(1, PAIRS + 1) as j:
                        for u in range(2):
                            x4 = X[:, bass.ds((2 * (j - 1) + u) * GT, GT), :]
                            for q in range(u * TALLY_BACK // 2, (u + 1) * TALLY_BACK // 2):
                                tally.make(dve, (j - 1) * TALLY_BACK + first, q)
                            dve.wait_ge(s_got[u], j * (16 * 2 * GT))
                            nc.vector.tensor_tensor(weighed[:, u], got[:, u],
                                                    gates[:, bass.ds((2 * (j - 1) + u) * GT, GT), :].unsqueeze(3)
                                                    .to_broadcast([P, GT, 2, C]), ALU.mult).then_inc(s_weighed[u], 1)
                            dve.wait_ge(s_weighed[u], j + 1)
                            nc.vector.tensor_tensor(x4, x4, weighed[:, u, :, 0, :], ALU.add).then_inc(s_first[u], 1)
                            dve.wait_ge(s_first[u], j + 1)
                            nc.vector.tensor_tensor(x4, x4, weighed[:, u, :, 1, :], ALU.add).then_inc(s_added[u], 1)
                    tally.read(dve)


def sorted_experts(nc, sp, k, A, expert_of, turns_of, x_sorted, y_sorted, group_rows, tally, tally_at):
    E, hid, cuts = MOE_EXPERTS, MOE_HIDDEN, MOE_CUTS
    K = len(cuts)
    w13 = sp.sb("w13", [P, 2, 2 * hid])
    w2 = sp.sb("w2", [P, 2, K, C])
    xs, xT = sp.sb("xs", [P, 2, GT, C]), sp.sb("xT", [P, 2, NODES])
    S, H = sp.sb("S", [P, 2, NODES]), sp.sb("H", [P, 2, NODES])
    yT, ys = sp.sb("yT", [P, 2, NODES]), sp.sb("ys", [P, 2, GT, C])
    ps1, ps3 = sp.ps("ps1", [P, 2, 512]), sp.ps("ps3", [P, 2, 512])
    psX, acc, psY = (sp.ps(n, [P, 512]) for n in ("psX", "acc", "psY"))
    s_up, s_S, s_H, s_down = (sp.sem(n) for n in ("up", "S", "H", "down"))
    s_load, s_turned, s_xT, s_yT, s_yturn, s_ys, s_out = (sp.sems(n) for n in ("load", "turned", "xT", "yT", "yturn", "ys", "out"))
    LOADS = 4
    MOST = SORTED_MOST // 2 + 1

    def after(j, u):
        return (j, 1) if u == 0 else (j + 1, 0)

    def through(j, q):
        return j * (2 * K) + q + 1

    def tally_part(u, i):
        per = TALLY_MIX // 2
        return range(u * per + per * i // K, u * per + per * (i + 1) // K)

    def both_loops(eng, body):
        turns = eng.value_load(turns_of[0:1, 0:1], min_val=TALLY_TURNS + 2, max_val=MOST)
        with eng.Fori(1, TALLY_TURNS + 1) as j:
            for u in range(2):
                body(j, u, True)
        with eng.Fori(TALLY_TURNS + 1, turns) as j:
            for u in range(2):
                body(j, u, False)

    with nc.Block() as block:
        @block.sync
        def _(eng):
            credit(eng, ((s_up, s_S, s_H, s_down), 2 * K), (s_turned + s_xT + s_yT + s_yturn + s_ys, 1), (s_out, 16))

        @block.tensor
        def _(pe):
            mm = nc.tensor.matmul

            def turn(nj, nu, j=None, u=None):
                pe.wait_ge(s_load[nu], nj * (16 * LOADS))
                if j is not None:
                    pe.wait_ge(s_xT[u], j + 1)
                for t in range(GT):
                    last = nc.tensor.transpose(psX[:, t * P:(t + 1) * P], xs[:, nu, t, :], k["ident"][:])
                last.then_inc(s_turned[nu], 1)

            def up(j, q, nj, nu):
                c0, r = cuts[q % K]
                if q % K == 0:
                    pe.wait_ge(s_xT[nu], nj + 1)
                pe.wait_ge(s_S, through(j, q - 2))
                pe.wait_ge(s_H, through(j, q - 2))
                mm(ps1[0:r, q % 2, :], w13[:, nu, c0:c0 + r], xT[:, nu, :], start=True, stop=True)
                mm(ps3[0:r, q % 2, :], w13[:, nu, hid + c0:hid + c0 + r], xT[:, nu, :], start=True,
                   stop=True).then_inc(s_up, 1)

            def down(j, q, u):
                i, r = q % K, cuts[q % K][1]
                pe.wait_ge(s_H, through(j, q))
                if i == 0:
                    pe.wait_ge(s_yT[1 - u], j + u)
                mm(acc[:], w2[0:r, u, i, :], H[0:r, q % 2, :], start=(i == 0), stop=(i == K - 1)).then_inc(s_down, 1)

            def body(j, u, tallied):
                nj, nu = after(j, u)
                q0 = K * u

                def count(i):
                    for q in tally_part(u, i) if tallied else ():
                        tally.add(pe, (j - 1) * TALLY_MIX + tally_at, q)

                up(j, q0 + 1, j, u)
                down(j, q0, u)
                count(0)
                up(j, q0 + 2, j, u)
                down(j, q0 + 1, u)
                turn(nj, nu, j, u)
                down(j, q0 + 2, u)
                count(1)
                up(j, q0 + 3, nj, nu)
                pe.wait_ge(s_yT[u], j + 1)
                pe.wait_ge(s_ys[1 - u], j + u)
                for t in range(GT):
                    last = nc.tensor.transpose(psY[:, t * P:(t + 1) * P], yT[:, u, t * P:(t + 1) * P], k["ident"][:])
                last.then_inc(s_yturn[u], 1)
                count(2)

            turn(1, 0)
            up(1, 0, 1, 0)
            both_loops(pe, body)

        @block.scalar
        def _(act):
            def load(nj, nu):
                g = 2 * (nj - 1) + nu
                e = act.value_load(expert_of[0:1, bass.ds(g, 1)], min_val=0, max_val=E - 1)
                for dst, src in ((xs[:, nu], group_rows(x_sorted, g)),
                                 (w13[:, nu], A["w13T"][bass.ds(e, 1)].rearrange("o c h -> (o c) h")),
                                 (w2[:, nu, 0:2, :], A["w2T"][bass.ds(e, 1), 0:2 * P, :].rearrange("o (k p) c -> p (o k) c", p=P)),
                                 (w2[0:cuts[2][1], nu, 2, :], A["w2T"][bass.ds(e, 1), 2 * P:hid, :].rearrange("o p c -> (o p) c"))):
                    act.dma_start(dst, src).then_inc(s_load[nu], 16)

            def gate(j, q):
                r = cuts[q % K][1]
                act.wait_ge(s_up, through(j, q))
                act.wait_ge(s_H, through(j, q - 2))
                nc.scalar.activation(S[0:r, q % 2, :], ps1[0:r, q % 2, :], ACT.Silu).then_inc(s_S, 1)

            def body(j, u, tallied):
                nj, nu = after(j, u)
                q0 = K * u
                gate(j, q0 + 1)
                gate(j, q0 + 2)
                act.wait_ge(s_turned[nu], nj + 1)
                nc.scalar.copy(xT[:, nu, :], psX[:]).then_inc(s_xT[nu], 1)
                act.wait_ge(s_down, through(j, q0 + 2))
                nc.scalar.copy(yT[:, u, :], acc[:]).then_inc(s_yT[u], 1)
                load(j + 1, u)
                gate(j, q0 + 3)
                act.wait_ge(s_ys[u], j + 1)
                act.dma_start(group_rows(y_sorted, 2 * (j - 1) + u), ys[:, u]).then_inc(s_out[u], 16)

            for u in range(2):
                load(1, u)
            act.wait_ge(s_turned[0], 2)
            nc.scalar.copy(xT[:, 0, :], psX[:]).then_inc(s_xT[0], 1)
            gate(1, 0)
            both_loops(act, body)
            turns = act.value_load(turns_of[0:1, 0:1], min_val=TALLY_TURNS + 2, max_val=MOST)
            for u in range(2):
                act.wait_ge(s_out[u], turns * 16)
            act.wait_ge(s_load[1], turns * (16 * LOADS))
            nc.scalar.copy(xT[:, 0, 0:1], xT[:, 0, 0:1])

        @block.vector
        def _(dve):
            def body(j, u, tallied):
                q0 = K * u
                for i in range(K):
                    r = cuts[i][1]
                    dve.wait_ge(s_S, through(j, q0 + i))
                    dve.wait_ge(s_down, through(j, q0 + i - 2))
                    nc.vector.tensor_tensor(H[0:r, (q0 + i) % 2, :], S[0:r, (q0 + i) % 2, :],
                                            ps3[0:r, (q0 + i) % 2, :], ALU.mult).then_inc(s_H, 1)
                    for q in tally_part(u, i) if tallied else ():
                        tally.make(dve, (j - 1) * TALLY_MIX + tally_at, q)
                dve.wait_ge(s_yturn[u], j + 1)
                dve.wait_ge(s_out[u], 16 * j)
                nc.vector.tensor_copy(ys[:, u].rearrange("p t c -> p (t c)"), psY[:]).then_inc(s_ys[u], 1)

            both_loops(dve, body)


def edge_attention_stage(nc, k, X, A, x_rows, x_in, s_x):
    EDGES, HEADS, DH = 256, 4, 32
    EC = EDGES // P
    with ExitStack() as ctx:
        sp = Space(nc, ctx, "edge")
        W_linT, W_valT, W_outT = (sp.sb(n, [C, C]) for n in ("W_linT", "W_valT", "W_outT"))
        a_blocks = sp.sb("a_blocks", [C, HEADS])
        a_wide = sp.sb("a_wide", [C, HEADS, P])
        src_col_i, dst_col_i = sp.sb("src_col_i", [P, EC], I32), sp.sb("dst_col_i", [P, EC], I32)
        src_row_i, dst_row_i = sp.sb("src_row_i", [P, EDGES], I32), sp.sb("dst_row_i", [P, EDGES], I32)
        src_col, dst_col = sp.sb("src_col", [P, EC]), sp.sb("dst_col", [P, EC])
        src_row, dst_row = sp.sb("src_row", [P, EDGES]), sp.sb("dst_row", [P, EDGES])
        node_i, node = sp.sb("node_i", [P, GT], I32), sp.sb("node", [P, GT])
        nodes_i, nodes = sp.sb("nodes_i", [P, NODES], I32), sp.sb("nodes", [P, NODES])
        pick = sp.sb("pick", [P, GT, 2 * EDGES])
        place = sp.sb("place", [P, EC, NODES])
        same = sp.sb("same", [P, EC, EDGES])
        place_idx, place_idx_i = sp.sb("place_idx", [P, EC]), sp.sb("place_idx_i", [P, EC], I32)
        A0, logA = sp.sb("A0", [P, EC]), sp.sb("logA", [P, EC])
        diag = sp.sb("diag", [P, EC, P])
        away = sp.sb("away", [P, EC, EDGES])
        bias = sp.sb("bias", [P, EC, EDGES])
        psR = sp.ps("psR", [P, 512])
        s_load, s_iota, s_zero, s_link, s_idx, s_A0, s_Aeps, s_log, s_diag, s_row = (
            sp.sem(n) for n in ("s_load", "s_iota", "s_zero", "s_link", "s_idx", "s_A0", "s_Aeps", "s_log",
                                "s_diag", "s_row"))
        with nc.Block() as block:
            @block.sync
            def _(eng):
                n = 0
                eng.dma_start(x_rows, x_in).then_inc(s_x, 16)
                for dst, src in ((W_linT, A["W_linT"]), (W_valT, A["W_valT"]), (W_outT, A["W_outT"]),
                                 (src_col_i, A["src"].rearrange("(p e) -> p e", e=EC)),
                                 (dst_col_i, A["dst"].rearrange("(p e) -> p e", e=EC)),
                                 (src_row_i, A["src"].unsqueeze(0).to_broadcast([P, EDGES])),
                                 (dst_row_i, A["dst"].unsqueeze(0).to_broadcast([P, EDGES]))):
                    eng.dma_start(dst[:], src).then_inc(s_load, 16)
                    n += 1
                eng.wait_ge(s_zero, 1)
                for h in range(HEADS):
                    eng.dma_start(a_blocks[h * DH:(h + 1) * DH, h:h + 1],
                                  A["a"][h].unsqueeze(1)).then_inc(s_load, 16)
                    n += 1
                eng.wait_ge(s_load, 16 * n)
                eng.wait_ge(s_x, 16)

            loads = 16 * (7 + HEADS)

            @block.gpsimd
            def _(pool):
                pool.iota(node_i[:], [[1, GT]], base=0, channel_multiplier=GT).then_inc(s_iota, 1)
                pool.iota(nodes_i[:], [[1, GT], [GT, P]], base=0, channel_multiplier=0).then_inc(s_iota, 1)
                pool.wait_ge(s_idx, 1)
                for ec in range(EC):
                    pool.indirect_dma_start(out=A0[:, ec:ec + 1], out_offset=None,
                                            in_=A["adj"].rearrange("a (b o) -> (a b) o", o=1),
                                            in_offset=bass.IndirectOffsetOnAxis(ap=place_idx_i[:, ec:ec + 1], axis=0),
                                            ).then_inc(s_A0, 16)

            @block.scalar
            def _(act):
                act.wait_ge(s_Aeps, 1)
                nc.scalar.activation(logA[:], A0[:], ACT.Ln).then_inc(s_log, 1)

            @block.tensor
            def _(pe):
                pe.wait_ge(s_diag, 1)
                for ec in range(EC):
                    last = nc.tensor.matmul(psR[:, ec * P:(ec + 1) * P], k["ones"][:], diag[:, ec, :],
                                            start=True, stop=True)
                last.then_inc(s_row, 1)

            @block.vector
            def _(dve):
                v = nc.vector
                link = Steps(dve, s_link)
                v.memset(a_blocks[:], 0.0).then_inc(s_zero, 1)
                dve.wait_ge(s_iota, 2)
                dve.wait_ge(s_load, loads)
                for out, src in ((node, node_i), (nodes, nodes_i), (src_col, src_col_i), (dst_col, dst_col_i),
                                 (src_row, src_row_i), (dst_row, dst_row_i)):
                    link.done(v.tensor_copy(out[:], src[:]))
                link.done(v.scalar_tensor_tensor(place_idx[:], src_col[:], float(NODES), dst_col[:], ALU.mult, ALU.add))
                v.tensor_copy(place_idx_i[:], place_idx[:]).then_inc(s_idx, 1)
                by_chunk = lambda row: row[:].rearrange("q (p e) -> q e p", e=EC)
                for c in range(GT):
                    both = pick[:, c, 0:EDGES].rearrange("q (e p) -> q e p", e=EC)
                    dst = pick[:, c, EDGES:2 * EDGES].rearrange("q (e p) -> q e p", e=EC)
                    link.done(v.tensor_scalar(dst, by_chunk(dst_row), node[:, c:c + 1], None, ALU.is_equal))
                    link.done(v.scalar_tensor_tensor(both, by_chunk(src_row), node[:, c:c + 1], dst,
                                                     ALU.is_equal, ALU.add))
                for ec in range(EC):
                    v.tensor_scalar(place[:, ec, :], nodes[:], src_col[:, ec:ec + 1], None, ALU.is_equal)
                    link.done(v.tensor_scalar(same[:, ec, :].rearrange("q (e p) -> q e p", e=EC), by_chunk(src_row),
                                              src_col[:, ec:ec + 1], None, ALU.is_equal))
                link.done(v.tensor_scalar(away[:], same[:], 1.0, 1e30, ALU.subtract, ALU.mult))
                v.tensor_copy(a_wide[:], spread(a_blocks[:], P))
                dve.wait_ge(s_A0, 16 * EC)
                v.tensor_scalar(A0[:], A0[:], 1e-8, None, ALU.add).then_inc(s_Aeps, 1)
                dve.wait_ge(s_log, 1)
                for ec in range(EC):
                    last = v.tensor_scalar(diag[:, ec, :], k["ident"][:], logA[:, ec:ec + 1], None, ALU.mult)
                last.then_inc(s_diag, 1)
                dve.wait_ge(s_row, 1)
                for ec in range(EC):
                    v.tensor_tensor(bias[:, ec, :], away[:, ec, :], psR[:, 0:EDGES], ALU.add)

        total, mean, sqsum, var, rstd = (sp.sb(n, [P, 2, GT]) for n in ("total", "mean", "sqsum", "var", "rstd"))
        centred, squares, xn = (sp.sb(n, [P, 2, GT, C]) for n in ("centred", "squares", "xn"))
        GT_, QV = sp.sb("gathered", [P, 2, 2 * EDGES]), sp.sb("QV", [P, 2, 2 * EDGES])
        L = sp.sb("L", [P, 2, EDGES])
        junk = sp.sb("junk", [P, EC * HEADS, EDGES])
        top, z, ex, den, attn = (sp.sb(n, [P, 2, EC, HEADS]) for n in ("top", "z", "ex", "den", "attn"))
        weighed = sp.sb("weighed", [P, 2, EC, C])
        YT = sp.sb("YT", [P, 2, NODES])
        psA = sp.ps("psA", [P, 2, 512])
        psB = sp.ps("psB", [P, 2, 512])
        (s_centred, s_squared, s_var, s_rstd, s_normed, s_g, s_GT, s_qv, s_QV, s_L, s_e, s_z, s_ex, s_den,
         s_w, s_y, s_YT, s_out, s_added) = (sp.sems(n) for n in (
             "centred", "squared", "var", "rstd", "normed", "g", "GT", "qv", "QV", "L", "e", "z", "ex",
             "den", "w", "y", "YT", "out", "added"))
        s_steps, s_ln = sp.sem("steps"), sp.sem("ln")
        with ExitStack() as ctx2, nc.Block() as block:
            psC = [ctx2.enter_context(nc.psum_tensor(f"edge_psC{i}", [P, 512], F32)) for i in range(3)]
            wide = [[psC[0], psC[1]], [psC[2], psR]]

            @block.sync
            def _(eng):
                credit(eng, ((s_steps,), 8), ((s_ln,), 6), (s_centred + s_squared + s_var + s_rstd + s_normed, 1),
                       (s_g + s_GT + s_qv + s_QV + s_L + s_e + s_z + s_ex + s_den + s_w, 1),
                       (s_y + s_YT + s_out + s_added, 1))

            @block.tensor
            def _(pe):
                with pe.Fori(1, PAIRS + 1) as j:
                    for u in range(2):
                        pe.wait_ge(s_normed[u], j + 1)
                        pe.wait_ge(s_YT[u], j)
                        for c in range(GT):
                            last = nc.tensor.matmul(psA[:, u, :], xn[:, u, c, :], pick[:, c, :], start=(c == 0),
                                                    stop=(c == GT - 1))
                        last.then_inc(s_g[u], 1)
                    for u in range(2):
                        pe.wait_ge(s_GT[u], j + 1)
                        pe.wait_ge(s_added[u], j)
                        nc.tensor.matmul(psB[:, u, 0:EDGES], W_linT[:], GT_[:, u, 0:EDGES], start=True, stop=True)
                        for ec in range(EC):
                            at = EDGES + ec * P
                            last = nc.tensor.matmul(psB[:, u, at:at + C], GT_[:, u, at:at + P], W_valT[:],
                                                    start=True, stop=True)
                        last.then_inc(s_qv[u], 1)
                    for u in range(2):
                        pe.wait_ge(s_L[u], j + 1)
                        for h in range(HEADS):
                            nc.tensor.matmul(wide[u][h // 2][:, (h % 2) * EDGES:(h % 2 + 1) * EDGES], a_wide[:, h, :],
                                             L[:, u, :], start=True, stop=True)
                        for ec in range(EC):
                            last = nc.tensor.matmul(psA[:, u, ec * HEADS:(ec + 1) * HEADS], L[:, u, ec * P:(ec + 1) * P],
                                                    a_blocks[:], start=True, stop=True)
                        last.then_inc(s_e[u], 1)
                    for u in range(2):
                        pe.wait_ge(s_ex[u], j + 1)
                        for ec in range(EC):
                            at = 8 + ec * HEADS
                            for e2 in range(EC):
                                last = nc.tensor.matmul(psA[:, u, at:at + HEADS], same[:, e2, ec * P:(ec + 1) * P],
                                                        ex[:, u, e2, :], start=(e2 == 0), stop=(e2 == EC - 1))
                        last.then_inc(s_den[u], 1)
                    for u in range(2):
                        pe.wait_ge(s_w[u], j + 1)
                        for ec in range(EC):
                            last = nc.tensor.matmul(psA[:, u, :], weighed[:, u, ec, :], place[:, ec, :],
                                                    start=(ec == 0), stop=(ec == EC - 1))
                        last.then_inc(s_y[u], 1)
                    for u in range(2):
                        pe.wait_ge(s_YT[u], j + 1)
                        for c in range(GT):
                            last = nc.tensor.matmul(psB[:, u, c * P:(c + 1) * P], YT[:, u, c * P:(c + 1) * P], W_outT[:],
                                                    start=True, stop=True)
                        last.then_inc(s_out[u], 1)

            @block.scalar
            def _(act):
                with act.Fori(1, PAIRS + 1) as j:
                    for u in range(2):
                        act.wait_ge(s_g[u], j + 1)
                        nc.scalar.copy(GT_[:, u, :], psA[:, u, :]).then_inc(s_GT[u], 1)
                    for u in range(2):
                        act.wait_ge(s_qv[u], j + 1)
                        nc.scalar.copy(QV[:, u, :], psB[:, u, :]).then_inc(s_QV[u], 1)
                    for u in range(2):
                        act.wait_ge(s_z[u], j + 1)
                        nc.scalar.activation(ex[:, u], z[:, u], ACT.Exp).then_inc(s_ex[u], 1)
                    for u in range(2):
                        act.wait_ge(s_y[u], j + 1)
                        nc.scalar.copy(YT[:, u, :], psA[:, u, :]).then_inc(s_YT[u], 1)

            @block.gpsimd
            def _(pool):
                with pool.Fori(1, PAIRS + 1) as j:
                    for u in range(2):
                        pool.wait_ge(s_centred[u], j + 1)
                        pool.tensor_tensor(squares[:, u], centred[:, u], centred[:, u],
                                           ALU.mult).then_inc(s_squared[u], 1)
                    for u in range(2):
                        pool.wait_ge(s_var[u], j + 1)
                        pool.tensor_tensor(rstd[:, u], var[:, u], k["minus_half"][:],
                                           ALU.pow).then_inc(s_rstd[u], 1)

            @block.vector
            def _(dve):
                v = nc.vector

                def normalise_pair(j):
                    link = Steps(dve, s_ln, j * 6)
                    for u in range(2):
                        x4 = X[:, bass.ds((2 * (j - 1) + u) * GT, GT), :]
                        link.done(v.tensor_reduce(total[:, u], x4, AX, ALU.add))
                        link.done(v.tensor_scalar(mean[:, u], total[:, u], 1.0 / C, None, ALU.mult))
                        v.tensor_tensor(centred[:, u], x4, spread(mean[:, u], C), ALU.subtract).then_inc(s_centred[u], 1)
                    for u in range(2):
                        dve.wait_ge(s_squared[u], j + 1)
                        link.done(v.tensor_reduce(sqsum[:, u], squares[:, u], AX, ALU.add))
                        v.tensor_scalar(var[:, u], sqsum[:, u], 1.0 / C, LN_EPS, ALU.mult, ALU.add).then_inc(s_var[u], 1)
                    for u in range(2):
                        dve.wait_ge(s_rstd[u], j + 1)
                        v.tensor_tensor(xn[:, u], centred[:, u], spread(rstd[:, u], C),
                                        ALU.mult).then_inc(s_normed[u], 1)

                def attend(j, more):
                    link = Steps(dve, s_steps, j * 8)
                    for u in range(2):
                        dve.wait_ge(s_QV[u], j + 1)
                        v.scalar_tensor_tensor(L[:, u, :], QV[:, u, 0:EDGES], 0.2, QV[:, u, 0:EDGES], ALU.mult,
                                               ALU.max).then_inc(s_L[u], 1)
                    if more:
                        normalise_pair(j + 1)
                    for u in range(2):
                        dve.wait_ge(s_e[u], j + 1)
                        link.mark(v.tensor_tensor(z[:, u], psA[:, u, 0:8].rearrange("p (e h) -> p e h", e=EC),
                                                  spread(logA[:], HEADS), ALU.add))
                        for ec in range(EC):
                            for h in range(HEADS):
                                last = v.tensor_tensor_reduce(
                                    junk[:, ec * HEADS + h, :], wide[u][h // 2][:, (h % 2) * EDGES:(h % 2 + 1) * EDGES], bias[:, ec, :], 1.0,
                                    -3e38, ALU.add, ALU.max, top[:, u, ec, h:h + 1])
                        link.done(last)
                        v.tensor_tensor(z[:, u], z[:, u], top[:, u], ALU.subtract).then_inc(s_z[u], 1)
                    for u in range(2):
                        dve.wait_ge(s_den[u], j + 1)
                        link.done(v.reciprocal(den[:, u], psA[:, u, 8:16].rearrange("p (e h) -> p e h", e=EC)))
                        dve.wait_ge(s_ex[u], j + 1)
                        link.done(v.tensor_tensor(attn[:, u], ex[:, u], den[:, u], ALU.mult))
                        v.tensor_tensor(weighed[:, u].rearrange("p e (h d) -> p (e h) d", h=HEADS),
                                        QV[:, u, EDGES:2 * EDGES].rearrange("p (e d) -> p e d", e=EC * HEADS),
                                        spread(attn[:, u].rearrange("p e h -> p (e h)"), DH),
                                        ALU.mult).then_inc(s_w[u], 1)
                    for u in range(2):
                        x4 = X[:, bass.ds((2 * (j - 1) + u) * GT, GT), :]
                        dve.wait_ge(s_out[u], j + 1)
                        v.tensor_tensor(x4, x4, psB[:, u, :].rearrange("p (t c) -> p t c", t=GT),
                                        ALU.add).then_inc(s_added[u], 1)
                    assert link.n == 8, link.n

                normalise_pair(1)
                with dve.Fori(1, PAIRS) as j:
                    attend(j, True)
                attend(PAIRS, False)


def dense_attention_stage(nc, k, X, xnT, A, keys, picked, best):
    assert PAIRS * CH == TAKEN
    SCALE = float(np.float32(1.0) / np.sqrt(np.float32(C)))
    with ExitStack() as ctx:
        sp = Space(nc, ctx, "att")
        normalise(nc, "att_ln", k, X, xnT, None, None, 0)
        Wq, Wk, WvT, Wo = (sp.sb(n, [C, C]) for n in ("Wq", "Wk", "WvT", "Wo"))
        bq, bk, bv, bo = (sp.sb(n, [C, 1]) for n in ("bq", "bk", "bv", "bo"))
        Wvo, bvo = sp.sb("Wvo", [C, C]), sp.sb("bvo", [C, 1])
        alpha, gamma = sp.sb("alpha", [P, 1]), sp.sb("gamma", [P, 1])
        bias = sp.sb("bias", [P, GT, NODES])
        mixT = sp.sb("mixT", [P, GT, NODES])
        keepers = sp.sb("keepers", [P, NODES])
        with ExitStack() as ctx2:
            s2 = Space(nc, ctx2, "att_set")
            adjN, adj, mix = (s2.sb(n, [P, GT, NODES]) for n in ("adjN", "adj", "mix"))
            linked = s2.sb("linked", [P, GT, NODES])
            degree, parent, has, rest = (s2.sb(n, [P, GT]) for n in ("degree", "parent", "has", "rest"))
            diag = s2.sb("diag", [P, GT, P])
            psM, psK, psW = s2.ps("psM", [P, 2, 512]), s2.ps("psK", [P, 512]), s2.ps("psW", [P, 512])
            s_load, s_link, s_diag, s_mix, s_turn, s_out, s_keep, s_w = (
                s2.sem(n) for n in ("load", "link", "diag", "mix", "turn", "out", "keep", "w"))
            with nc.Block() as block:
                loads = [(Wq, A["Wq"]), (Wk, A["Wk"]), (WvT, A["WvT"]), (Wo, A["Wo"]),
                         (bq, A["bq"].unsqueeze(1)), (bk, A["bk"].unsqueeze(1)), (bv, A["bv"].unsqueeze(1)),
                         (bo, A["bo"].unsqueeze(1)),
                         (alpha, A["alpha"].unsqueeze(0).to_broadcast([P, 1])),
                         (gamma, A["gamma"].unsqueeze(0).to_broadcast([P, 1])),
                         (adjN, A["adj"].rearrange("(p c) m -> p c m", c=GT))]

                @block.sync
                def _(eng):
                    for dst, src in loads:
                        eng.dma_start(dst[:], src).then_inc(s_load, 16)

                @block.tensor
                def _(pe):
                    pe.wait_ge(s_load, 16 * len(loads))
                    nc.tensor.matmul(psW[:, 0:C], WvT[:], Wo[:], start=True, stop=True)
                    nc.tensor.matmul(psW[:, C:C + 1], Wo[:], bv[:], start=True, stop=True).then_inc(s_w, 1)
                    pe.wait_ge(s_diag, 1)
                    for c in range(GT):
                        last = nc.tensor.matmul(psK[:, c * P:(c + 1) * P], k["ones"][:], diag[:, c, :], start=True,
                                                stop=True)
                    last.then_inc(s_keep, 1)
                    pe.wait_ge(s_mix, 1)
                    for m in range(GT):
                        if m >= 2:
                            pe.wait_ge(s_out, m - 1)
                        for c in range(GT):
                            last = nc.tensor.transpose(psM[:, m % 2, c * P:(c + 1) * P], mix[:, c, m * P:(m + 1) * P],
                                                       k["ident"][:])
                        last.then_inc(s_turn, 1)

                @block.scalar
                def _(act):
                    for m in range(GT):
                        act.wait_ge(s_turn, m + 1)
                        nc.scalar.copy(mixT[:, m, :], psM[:, m % 2, :]).then_inc(s_out, 1)

                @block.vector
                def _(dve):
                    v = nc.vector
                    link = Steps(dve, s_link)
                    dve.wait_ge(s_load, 16 * len(loads))
                    for c in range(GT):
                        link.mark(v.tensor_copy(adj[:, c, :].rearrange("q (c p) -> q c p", c=GT),
                                                adjN[:, c, :].rearrange("q (p c) -> q c p", c=GT)))
                    link.done(v.tensor_reduce(degree[:], adjN[:], AX, ALU.add))
                    link.done(v.tensor_scalar(linked[:], adj[:], 0.0, None, ALU.not_equal))
                    link.done(v.tensor_reduce(has[:], linked[:], AX, ALU.max))
                    for c in range(GT):
                        last = v.tensor_scalar(diag[:, c, :], k["ident"][:], has[:, c:c + 1], SCALE, ALU.mult, ALU.mult)
                    last.then_inc(s_diag, 1)
                    link.done(v.tensor_scalar(linked[:], linked[:], 1.0, 1e9, ALU.subtract, ALU.mult))
                    v.scalar_tensor_tensor(bias[:], adj[:], alpha[:, 0:1], linked[:], ALU.mult, ALU.add)
                    link.done(v.tensor_scalar(parent[:], degree[:], 0.0, gamma[:, 0:1], ALU.is_gt, ALU.mult))
                    link.done(v.tensor_scalar(rest[:], parent[:], -1.0, 1.0, ALU.mult, ALU.add))
                    for c in range(GT):
                        link.mark(v.tensor_scalar(mix[:, c, :], adj[:, c, :], parent[:, c:c + 1], None, ALU.mult))
                    dve.wait_ge(s_link, link.n)
                    for c in range(GT):
                        block_c = mix[:, c, c * P:(c + 1) * P]
                        last = v.scalar_tensor_tensor(block_c, k["ident"][:], rest[:, c:c + 1], block_c, ALU.mult, ALU.add)
                    last.then_inc(s_mix, 1)
                    dve.wait_ge(s_keep, 1)
                    v.tensor_copy(keepers[:], psK[:])
                    dve.wait_ge(s_w, 1)
                    v.tensor_copy(Wvo[:], psW[:, 0:C])
                    v.tensor_tensor(bvo[:], psW[:, C:C + 1], bo[:], ALU.add)

        QT, KT, U, rT, r, fT = (sp.sb(n, [P, 2, NODES]) for n in ("QT", "KT", "U", "rT", "r", "fT"))
        xg = sp.sb("xg", [P, 2, NODES])
        PT = sp.sb("PT", [P, 2, GT, NODES])
        SC, Pn = sp.sb("SC", [P, 2, NODES]), sp.sb("Pn", [P, 2, NODES])
        Pe = sp.sb("Pe", [P, 2, NODES])
        top, ntop, rowsum, rinv = (sp.sb(n, [P, 2]) for n in ("top", "ntop", "rowsum", "rinv"))
        carrier = sp.sb("carrier", [P, 2])
        s_pick = sp.sem("pick")
        psG = [sp.ps(f"psG{i}", [P, 512]) for i in range(4)]
        psS, psT = sp.ps("psS", [P, 2, 512]), sp.ps("psT", [P, 2, 512])
        (s_xg, s_q, s_k, s_u, s_QT, s_KT, s_U, s_o, s_rT, s_rt, s_r, s_f, s_fT, s_ft, s_added) = (sp.sems(n) for n in (
            "xg", "q", "k", "u", "QT", "KT", "U", "o", "rT", "rt", "r", "f", "fT", "ft", "added"))
        s_S, s_top, s_ntop, s_exp, s_inv, s_Pn, s_pt, s_PT = (sp.sem(n) for n in (
            "S", "top", "ntop", "exp", "inv", "Pn", "pt", "PT"))
        ITEMS = 2 * GT
        with nc.Block() as block:
            @block.sync
            def _(eng):
                credit(eng, (s_xg + s_q + s_k + s_u + s_QT + s_KT + s_U + s_o + s_rT + s_rt + s_r + s_f + s_fT, 1),
                       (s_ft + s_added, 1), ((s_pick,), PICKS), ((s_S, s_top, s_ntop, s_exp, s_inv, s_Pn, s_pt, s_PT), ITEMS))

            @block.gpsimd
            def _(pool):
                with pool.Fori(1, PAIRS + 1) as j:
                    for u in range(2):
                        pool.wait_ge(s_rT[u], j)
                        pool.tensor_copy(xg[:, u, :], xnT[:, bass.ds((2 * (j - 1) + u) * NODES, NODES)]).then_inc(s_xg[u], 1)

            @block.tensor
            def _(pe):
                mm = nc.tensor.matmul
                with pe.Fori(1, PAIRS + 1) as j:
                    plan = [[(0, s_fT[0], 0), (1, s_fT[1], 0), (2, s_added[0], 0)],
                            [(3, s_added[1], 0), (0, s_QT[0], 1), (1, s_KT[0], 1)]]
                    for u in range(2):
                        pe.wait_ge(s_xg[u], j + 1)
                        for step, (bank, free, more) in enumerate(plan[u]):
                            pe.wait_ge(free, j + more)
                            if step < 2:
                                mm(psG[bank][:], (Wq, Wk)[step][:], xg[:, u, :], start=True,
                                   stop=True).then_inc((s_q, s_k)[step][u], 1)
                            else:
                                for c in range(GT):
                                    last = mm(psG[bank][:, c * P:(c + 1) * P], xg[:, u, c * P:(c + 1) * P], Wvo[:],
                                              start=True, stop=True)
                                last.then_inc(s_u[u], 1)

                    def scores(q):
                        c, u = q // 2, q % 2
                        pe.wait_ge(s_QT[u], j + 1)
                        pe.wait_ge(s_KT[u], j + 1)
                        pe.wait_ge(s_top, ITEMS * j + max(q - 1, 0))
                        mm(psS[:, q % 2, :], QT[:, u, c * P:(c + 1) * P], KT[:, u, :], start=True,
                           stop=True).then_inc(s_S, 1)

                    def turn(q):
                        pe.wait_ge(s_Pn, ITEMS * j + q + 1)
                        pe.wait_ge(s_PT, ITEMS * j + max(q - 1, 0))
                        for m in range(GT):
                            last = nc.tensor.transpose(psT[:, q % 2, m * P:(m + 1) * P],
                                                       Pn[:, q % 2, m * P:(m + 1) * P], k["ident"][:])
                        last.then_inc(s_pt, 1)

                    for q in range(ITEMS + 4):
                        if q < ITEMS:
                            scores(q)
                        if q >= 4:
                            turn(q - 4)
                    for u in range(2):
                        pe.wait_ge(s_KT[1], j + 1)
                        pe.wait_ge(s_U[1], j + 1)
                        pe.wait_ge(s_PT, ITEMS * j + ITEMS - 1 + u)
                        for m in range(GT):
                            last = mm(psG[u][:], U[:, u, m * P:(m + 1) * P], PT[:, u, m, :], start=(m == 0),
                                      stop=(m == GT - 1))
                        last.then_inc(s_o[u], 1)
                    for u in range(2):
                        pe.wait_ge(s_rT[u], j + 1)
                        for c in range(GT):
                            last = nc.tensor.transpose(psG[2 + u][:, c * P:(c + 1) * P], rT[:, u, c * P:(c + 1) * P],
                                                       k["ident"][:])
                        last.then_inc(s_rt[u], 1)
                    for u in range(2):
                        pe.wait_ge(s_r[u], j + 1)
                        for m in range(GT):
                            last = mm(psG[u][:], r[:, u, m * P:(m + 1) * P], mixT[:, m, :], start=(m == 0),
                                      stop=(m == GT - 1))
                        last.then_inc(s_f[u], 1)
                    for u in range(2):
                        pe.wait_ge(s_fT[u], j + 1)
                        for c in range(GT):
                            last = nc.tensor.transpose(psG[2 + u][:, c * P:(c + 1) * P], fT[:, u, c * P:(c + 1) * P],
                                                       k["ident"][:])
                        last.then_inc(s_ft[u], 1)

            @block.scalar
            def _(act):
                with act.Fori(1, PAIRS + 1) as j:
                    for u in range(2):
                        act.wait_ge(s_k[u], j + 1)
                        nc.scalar.activation(KT[:, u, :], psG[(1, 0)[u]][:], ACT.Identity, bias=bk[:, 0:1]).then_inc(s_KT[u], 1)
                        act.wait_ge(s_u[u], j + 1)
                        nc.scalar.copy(U[:, u, :], psG[(2, 1)[u]][:]).then_inc(s_U[u], 1)

                    def exps(q):
                        act.wait_ge(s_ntop, ITEMS * j + q + 1)
                        act.wait_ge(s_Pn, ITEMS * j + max(q - 1, 0))
                        nc.scalar.activation(Pe[:, q % 2, :], SC[:, q % 2, :], ACT.Exp, bias=ntop[:, q % 2:q % 2 + 1],
                                             accum_out=rowsum[:, q % 2:q % 2 + 1]).then_inc(s_exp, 1)

                    def out(q):
                        c, u = q // 2, q % 2
                        act.wait_ge(s_pt, ITEMS * j + q + 1)
                        nc.scalar.copy(PT[:, u, :, c * P:(c + 1) * P],
                                       psT[:, q % 2, :].rearrange("p (m n) -> p m n", m=GT)).then_inc(s_PT, 1)

                    for q in range(ITEMS + 4):
                        if q < ITEMS:
                            exps(q)
                        if q >= 4:
                            out(q - 4)
                    for u in range(2):
                        act.wait_ge(s_rt[u], j + 1)
                        nc.scalar.copy(r[:, u, :], psG[2 + u][:]).then_inc(s_r[u], 1)
                    for u in range(2):
                        act.wait_ge(s_f[u], j + 1)
                        nc.scalar.copy(fT[:, u, :], psG[u][:]).then_inc(s_fT[u], 1)

            @block.vector
            def _(dve):
                v = nc.vector
                with dve.Fori(1, PAIRS + 1) as j:
                    for u in range(2):
                        dve.wait_ge(s_q[u], j + 1)
                        v.scalar_tensor_tensor(QT[:, u, :], psG[(0, 3)[u]][:], bq[:, 0:1], keepers[:], ALU.add,
                                               ALU.mult).then_inc(s_QT[u], 1)
                    for q in range(ITEMS + 2):
                        b, old = q % 2, q - 2
                        if q < ITEMS:
                            dve.wait_ge(s_S, ITEMS * j + q + 1)
                        if old < 0:
                            dve.wait_ge(s_exp, ITEMS * j)
                            v.memset(carrier[:, q:q + 1], 0.0)
                        else:
                            dve.wait_ge(s_exp, ITEMS * j + old + 1)
                            v.reciprocal(rinv[:, b:b + 1], rowsum[:, b:b + 1]).then_inc(s_inv, 1)
                        if q < ITEMS:
                            v.tensor_tensor_reduce(SC[:, b, :], psS[:, b, :], bias[:, q // 2, :], 1.0, -3e38, ALU.add, ALU.max,
                                                   top[:, b:b + 1]).then_inc(s_top, 1)
                        if old >= 0:
                            dve.wait_ge(s_inv, ITEMS * j + old + 1)
                            dve.wait_ge(s_pt, ITEMS * j + max(old - 1, 0))
                            v.tensor_scalar(Pn[:, b, :], Pe[:, b, :], rinv[:, b:b + 1], None, ALU.mult).then_inc(s_Pn, 1)
                        if q < ITEMS:
                            dve.wait_ge(s_top, ITEMS * j + q + 1)
                            v.tensor_scalar(ntop[:, b:b + 1], top[:, b:b + 1], -1.0, None, ALU.mult).then_inc(s_ntop, 1)
                    for u in range(2):
                        dve.wait_ge(s_o[u], j + 1)
                        v.scalar_tensor_tensor(rT[:, u, :], psG[u][:], bvo[:, 0:1], xg[:, u, :], ALU.add,
                                               ALU.add).then_inc(s_rT[u], 1)
                    pick_round(dve, nc.vector, keys, picked, best, s_pick, j)
                    for u in range(2):
                        x4 = X[:, bass.ds((2 * (j - 1) + u) * GT, GT), :]
                        dve.wait_ge(s_ft[u], j + 1)
                        v.tensor_tensor(x4, x4, psG[2 + u][:].rearrange("p (t c) -> p t c", t=GT),
                                        ALU.add).then_inc(s_added[u], 1)


GAT_HEADS, GAT_EXPERTS = 4, 4
HEAD_COLS = GAT_HEADS * GAT_EXPERTS
LAST_NODE = SRC_NODES - 1
WINDOWS = 4
WT = TILES // WINDOWS
FEATURES = HEAD_COLS + GAT_HEADS


class Tally:

    def __init__(self, nc, sp, lo16, hi16, iota16, iota1_16, far_count):
        self.nc, self.lo16, self.hi16, self.iota16, self.iota1_16 = nc, lo16, hi16, iota16, iota1_16
        self.far_count = far_count
        self.LO = sp.sb("LO", [P, HOTS, HCOLS // 2, P, 2], BF16)
        self.HI = sp.sb("HI", [P, HOTS, HCOLS // 2, TILES, 2], BF16)
        self.zeros = sp.sb("zeros", [P, P], BF16)
        self.hist = sp.ps("hist", [P, 512])
        self.s_zero, self.s_hot, self.s_used, self.s_hist = (sp.sem(n) for n in ("zero", "hot", "used", "hist"))

    def start(self, eng):
        credit(eng, ((self.s_hot, self.s_used), HOTS))

    def open(self, pe):
        pe.wait_ge(self.s_zero, 1)
        self.nc.tensor.matmul(self.hist[:, 0:TILES], self.zeros[:], self.zeros[:, 0:TILES], start=True, stop=False)

    def close(self):
        self.nc.tensor.matmul(self.hist[:, 0:TILES], self.zeros[:], self.zeros[:, 0:TILES], start=False,
                              stop=True).then_inc(self.s_hist, 1)

    def make(self, dve, turn, q):
        b = q % HOTS
        at = bass.ds(turn * HCOLS + q * HCOLS, HCOLS)
        dve.wait_ge(self.s_used, turn + q + 1)
        for out, pattern, column, width in ((self.LO, self.iota16, self.lo16, P), (self.HI, self.iota1_16, self.hi16, TILES)):
            last = self.nc.vector.tensor_tensor(
                out[:, b], pattern[:].unsqueeze(1).to_broadcast([P, HCOLS // 2, width, 2]),
                column[:, at].rearrange("p (a b) -> p a b", b=2).unsqueeze(2).to_broadcast([P, HCOLS // 2, width, 2]),
                ALU.is_equal)
        last.then_inc(self.s_hot, 1)

    def add(self, pe, turn, q):
        b = q % HOTS
        pe.wait_ge(self.s_hot, turn + q + 1 + HOTS)
        for c in range(HCOLS):
            last = self.nc.tensor.matmul(self.hist[:, 0:TILES], self.LO[:, b, c // 2, :, c % 2],
                                         self.HI[:, b, c // 2, :, c % 2], start=False, stop=False)
        last.then_inc(self.s_used, 1)

    def read(self, dve):
        dve.wait_ge(self.s_hist, 1)
        self.nc.vector.tensor_copy(self.far_count[:], self.hist[:, 0:TILES])


PICKS = 2 * SEGMENTS + 1


def pick_round(dve, v, keys, picked, best, s_pick, j):
    picks = Steps(dve, s_pick, j * PICKS)
    for g in range(SEGMENTS):
        picks.mark(v.max(out=best[:, g, :], in_=keys[:, g * SEGMENT:(g + 1) * SEGMENT]))
    dve.wait_ge(s_pick, picks.base + picks.n)
    picks.mark(v.tensor_copy(picked[:, :, bass.ds((j - 1) * CH, CH)], best[:]))
    for g in range(SEGMENTS):
        segment = keys[:, g * SEGMENT:(g + 1) * SEGMENT]
        picks.mark(v.match_replace(out=segment, in_to_replace=best[:, g, :], in_values=segment, imm_value=0.0))
    assert picks.n == PICKS
    dve.wait_ge(s_pick, picks.base + picks.n)


def edge_keys_stage(nc, k, A, keys, lo16, hi16, iota16, iota1_16, cell, rounds_of, scratch, tally, x_sorted, y_sorted, s_empty):
    with ExitStack() as ctx:
        sp = Space(nc, ctx, "keys")
        src, dst = sp.sb("src", [P, LANE], I32), sp.sb("dst", [P, LANE], I32)
        part, tile = (scratch[:, i * LANE:(i + 1) * LANE].bitcast(I32) for i in range(2))
        real, live = sp.sb("real", [P, LANE]), sp.sb("live", [P, LANE])
        iota_i = sp.sb("iota_i", [P, P, 2], I32)
        count, most = sp.sb("count", [P, SEGMENTS]), sp.sb("most", [P, SEGMENTS])
        full, fuller = sp.sb("full", [P, 1]), sp.sb("fuller", [P, MAX_PASSES])
        levels_i, levels = sp.sb("levels_i", [P, MAX_PASSES], I32), sp.sb("levels", [P, MAX_PASSES])
        passes_f, rounds_f = sp.sb("passes_f", [P, 1]), sp.sb("rounds_f", [P, MAX_PASSES])
        blank = sp.sb("blank", [P, GT * C])
        s_load, s_iota, s_link, s_count, s_most, s_blank = (sp.sem(n) for n in ("load", "iota", "link", "count", "most", "blank"))
        edges = A["edge_index"].rearrange("a (p i) -> a p i", p=P)
        with nc.Block() as block:
            @block.sync
            def _(eng):
                eng.dma_start(src[:], edges[0]).then_inc(s_load, 16)
                eng.dma_start(dst[:], edges[1]).then_inc(s_load, 16)
                tally.start(eng)
                eng.wait_ge(s_blank, 1)
                for t, g in [(x_sorted, g) for g in range(SORTED)] + [(y_sorted, g) for g in range(2 * TALLY_TURNS, SORTED)]:
                    eng.dma_start(t[g * NODES:(g + 1) * NODES, :].rearrange("(p c) d -> p (c d)", c=GT),
                                  blank[:]).then_inc(s_empty, 16)

            @block.gpsimd
            def _(pool):
                pool.iota(iota_i[:], [[1, P], [0, 2]], base=0, channel_multiplier=0).then_inc(s_iota, 1)
                pool.iota(levels_i[:], [[TAKEN, MAX_PASSES]], base=0, channel_multiplier=0).then_inc(s_iota, 1)
                pool.wait_ge(s_count, 1)
                pool.partition_all_reduce(most[:], count[:], P, bass.bass_isa.ReduceOp.max).then_inc(s_most, 1)

            @block.vector
            def _(dve):
                v = nc.vector
                link = Steps(dve, s_link)
                v.memset(blank[:], 0.0).then_inc(s_blank, 1)
                v.memset(tally.zeros[:], 0.0).then_inc(tally.s_zero, 1)
                dve.wait_ge(s_iota, 2)
                v.tensor_copy(iota16[:], iota_i[:])
                v.tensor_copy(levels[:], levels_i[:])
                v.tensor_scalar(iota1_16[:], iota_i[:, 0:TILES, :], 1.0, None, ALU.add)
                dve.wait_ge(s_load, 32)
                link.done(v.tensor_scalar(real[:], dst[:], float(SRC_NODES), None, ALU.is_lt))
                link.done(v.scalar_tensor_tensor(live[:], src[:], float(LAST_NODE), real[:], ALU.is_lt, ALU.mult))
                link.mark(v.tensor_tensor(real[:], real[:], live[:], ALU.subtract))
                v.tensor_reduce(count[:], live[:].rearrange("p (s i) -> p s i", s=SEGMENTS), AX, ALU.add).then_inc(s_count, 1)
                keys_i = keys[:].bitcast(I32)
                link.done(v.tensor_scalar(part, dst[:], 2, P - 1, ALU.logical_shift_right, ALU.bitwise_and))
                link.mark(v.tensor_copy(lo16[:], part))
                link.mark(v.tensor_scalar(tile, dst[:], 9, 2, ALU.logical_shift_right, ALU.logical_shift_left))
                link.done(v.tensor_scalar(dst[:], dst[:], GT - 1, None, ALU.bitwise_and))
                link.done(v.tensor_tensor(tile, tile, dst[:], ALU.bitwise_or))
                link.mark(v.scalar_tensor_tensor(hi16[:], tile, 1.0, real[:], ALU.add, ALU.mult))
                link.mark(v.tensor_scalar(keys_i, tile, TILE_SHIFT, KEY_MARK, ALU.logical_shift_left, ALU.bitwise_or))
                link.done(v.tensor_scalar(part, part, NODE_BITS, None, ALU.logical_shift_left))
                link.done(v.tensor_tensor(src[:], src[:], part, ALU.bitwise_or))
                link.done(v.tensor_tensor(keys_i, keys_i, src[:], ALU.bitwise_or))
                link.mark(v.tensor_tensor(keys[:], keys[:], live[:], ALU.mult))
                dve.wait_ge(s_most, 1)
                link.done(v.tensor_reduce(full[:], most[:], AX, ALU.max))
                link.done(v.tensor_scalar(full[:], full[:], 1.0, None, ALU.max))
                link.done(v.tensor_tensor(fuller[:], levels[:], full[:].to_broadcast([P, MAX_PASSES]), ALU.is_lt))
                link.done(v.tensor_reduce(passes_f[:], fuller[:], AX, ALU.add))
                link.mark(v.tensor_copy(cell[:], passes_f[:]))
                link.done(v.memset(rounds_f[:], 2.0))
                link.done(v.tensor_scalar(rounds_f[:, 0:MAX_PASSES - 1], fuller[:, 1:], float(TAKEN // CH - 1), 2.0,
                                          ALU.mult, ALU.add))
                v.tensor_copy(rounds_of[:], rounds_f[:])


def pick_keys(nc, keys, picked, best, rounds):
    with ExitStack() as ctx:
        sp = Space(nc, ctx, "pick")
        s_pick, s_carrier, carrier = sp.sem("pick"), sp.sem("carrier"), sp.sb("carrier", [P, 1])
        with nc.Block() as block:
            @block.sync
            def _(eng):
                credit(eng, ((s_pick,), PICKS), ((s_carrier,), 1))

            @block.vector
            def _(dve):
                with dve.Fori(1, dve.value_load(rounds, min_val=2, max_val=TAKEN // CH + 1)) as j:
                    pick_round(dve, nc.vector, keys, picked, best, s_pick, j)
                    dve.wait_ge(s_carrier, j)
                    nc.vector.memset(carrier[:], 0.0).then_inc(s_carrier, 1)


def split_keys(nc, picked, split, there, count, fullest, turns_f, turns_i, turns_of):
    with ExitStack() as ctx:
        sp = Space(nc, ctx, "split")
        s_link, s_count, s_fullest = (sp.sem(n) for n in ("link", "count", "fullest"))
        with nc.Block() as block:
            @block.gpsimd
            def _(pool):
                pool.wait_ge(s_count, 1)
                pool.partition_all_reduce(fullest[:], count[:], P, bass.bass_isa.ReduceOp.max).then_inc(s_fullest, 1)

            @block.vector
            def _(dve):
                v = nc.vector
                link = Steps(dve, s_link)
                flat = picked[:].rearrange("p s i -> p (s i)")
                begins = [float(np.array(KEY_MARK + (w * WT << TILE_SHIFT), np.uint32).view(np.float32)) for w in range(WINDOWS + 1)]
                for w in range(WINDOWS):
                    link.mark(v.scalar_tensor_tensor(split[:, w, :], flat, begins[w], flat, ALU.is_ge, ALU.mult))
                for w in range(WINDOWS):
                    dve.wait_ge(s_link, w + 1)
                    link.mark(v.scalar_tensor_tensor(split[:, w, :], split[:, w, :], begins[w + 1], split[:, w, :],
                                                     ALU.is_lt, ALU.mult))
                dve.wait_ge(s_link, link.n)
                link.done(v.tensor_scalar(there[:], split[:], 0.0, None, ALU.is_gt))
                v.tensor_reduce(count[:], there[:], AX, ALU.add).then_inc(s_count, 1)
                dve.wait_ge(s_fullest, 1)
                link.done(v.tensor_scalar(turns_f[:], fullest[:], float(4 * CH - 1), float(4 * CH), ALU.add, ALU.max))
                link.done(v.tensor_copy(turns_i[:], turns_f[:]))
                v.tensor_scalar(turns_of[:], turns_i[:], 4, None, ALU.logical_shift_right)


def edge_window(nc, sp, w, B):
    (node, now, split, turns_of, bound, tile_marks, iota16, ident16, src_table) = (
        B[n] for n in ("node", "now", "split", "turns_of", "bound", "tile_marks", "iota16", "ident16", "src_table"))
    (a_dst_now, marks_now, top8, sidx, part_i, tile_i, part16, tile_f, rows) = (
        B[n] for n in ("a_dst_now", "marks_now", "top8", "sidx", "part_i", "tile_i", "part16", "tile_f", "rows"))
    (LO16, LO, LOT, HI, choice, a_dst_e, z, zd, val, spreadv, tick, sums, zeros) = (
        B[n] for n in ("LO16", "LO", "LOT", "HI", "choice", "a_dst_e", "z", "zd", "val", "spreadv", "tick", "sums", "zeros"))
    acc, psA, psT16, ones = B["acc"], B["psA"], B["psT16"], B["ones"]
    NH, W = GAT_HEADS, FEATURES
    MOST_TURNS = -(-PICKED // (2 * CH)) + 1
    s_set, s_loop, s_sum = (sp.sem(n) for n in ("set", "loop", "sum"))
    (s_idx, s_rows, s_hot, s_turned, s_lot, s_lo, s_a, s_z, s_w, s_val, s_spread, s_used, s_tick) = (sp.sems(n) for n in (
        "idx", "rows", "hot", "turned", "lot", "lo", "a", "z", "w", "val", "spread", "used", "tick"))
    STEPS = 2 * 12
    cells = turns_of[0:1, bass.ds(w, 1)]

    def after(j, u):
        return (j, 1) if u == 0 else (j + 1, 0)

    with nc.Block() as block:
        @block.sync
        def _(eng):
            credit(eng, (s_idx + s_hot + s_turned + s_lot + s_lo + s_a + s_z + s_w + s_val + s_spread + s_used + s_tick, 1),
                   ((s_loop,), STEPS))

        @block.gpsimd
        def _(pool):
            with pool.Fori(1, pool.value_load(cells, min_val=2, max_val=MOST_TURNS)) as j:
                for u in range(2):
                    pool.wait_ge(s_idx[u], j + 1)
                    pool.wait_ge(s_val[u], j)
                    pool.wait_ge(s_tick[u], j)
                    pool.tensor_tensor(tick[:, u:u + 1], ones[:, 0:1], ones[:, 0:1], ALU.mult).then_inc(s_tick[u], 1)
                    for i in range(CH):
                        pool.indirect_dma_start(out=rows[:, u, i, :], out_offset=None, in_=src_table,
                                                in_offset=bass.IndirectOffsetOnAxis(ap=sidx[:, u, i:i + 1], axis=0)
                                                ).then_inc(s_rows[u], 16)

        @block.scalar
        def _(act):
            def one_hots(nj, nu):
                act.wait_ge(s_turned[nu], nj + 1)
                act.wait_ge(s_a[nu], nj)
                nc.scalar.copy(LOT[:, nu], psT16[nu]).then_inc(s_lot[nu], 1)
                act.wait_ge(s_hot[nu], nj + 1)
                act.wait_ge(s_used[nu], nj)
                nc.scalar.copy(LO[:, nu].rearrange("p (a b) e -> p a b e", b=2),
                               LO16[:, nu].rearrange("p a e b -> p a b e")).then_inc(s_lo[nu], 1)

            one_hots(1, 0)
            turns = act.value_load(cells, min_val=2, max_val=MOST_TURNS)
            with act.Fori(1, turns) as j:
                for u in range(2):
                    act.wait_ge(s_z[u], j + 1)
                    nc.scalar.activation(val[:, u, :, HEAD_COLS:W], zd[:, u], ACT.Exp).then_inc(s_w[u], 1)
                    one_hots(*after(j, u))
            one_hots(turns, 1)

        @block.tensor
        def _(pe):
            mm = nc.tensor.matmul

            def turn_hots(nj, nu):
                pe.wait_ge(s_hot[nu], nj + 1)
                pe.wait_ge(s_lot[nu], nj)
                for i in range(CH):
                    last = nc.tensor.transpose(psT16[nu][:, i, :], LO16[:, nu, i // 2, :, i % 2], ident16[:])
                last.then_inc(s_turned[nu], 1)

            def pick_a_dst(nj, nu):
                pe.wait_ge(s_lot[nu], nj + 1)
                pe.wait_ge(s_z[nu], nj)
                for i in range(CH):
                    last = mm(psA[:, nu, i * NH * WT:(i + 1) * NH * WT], LOT[:, nu, i, :],
                              a_dst_now[:].rearrange("p h t -> p (h t)"), start=True, stop=True)
                last.then_inc(s_a[nu], 1)

            mm(acc[:, 0:W * WT], zeros[:, 0:P], zeros[:], start=True, stop=False)
            pe.wait_ge(s_set, 1)
            for u in range(2):
                turn_hots(1, u)
                pick_a_dst(1, u)
            with pe.Fori(1, pe.value_load(cells, min_val=2, max_val=MOST_TURNS)) as j:
                for u in range(2):
                    pe.wait_ge(s_lo[u], j + 1)
                    pe.wait_ge(s_spread[u], j + 1)
                    for i in range(CH):
                        if i == CH // 2:
                            turn_hots(j + 1, u)
                        last = mm(acc[:, 0:W * WT], LO[:, u, i, :], spreadv[:, u, i].rearrange("p f t -> p (f t)"),
                                  start=False, stop=False)
                    last.then_inc(s_used[u], 1)
                    pick_a_dst(j + 1, u)
            mm(acc[:, 0:W * WT], zeros[:, 0:P], zeros[:], start=False, stop=True).then_inc(s_sum, 1)

        @block.vector
        def _(dve):
            v = nc.vector

            def select(step, u):
                t8 = top8[:, u].bitcast(I32)
                step.done(v.max(out=top8[:, u], in_=now[:]))
                v.tensor_scalar(sidx[:, u], t8, SRC_NODES - 1, None, ALU.bitwise_and).then_inc(s_idx[u], 1)
                step.mark(v.tensor_scalar(part_i[:, u], t8, NODE_BITS, P - 1, ALU.logical_shift_right, ALU.bitwise_and))
                step.mark(v.tensor_scalar(tile_i[:, u], t8, TILE_SHIFT, None, ALU.logical_shift_right))
                step.done(v.match_replace(out=now[:], in_to_replace=top8[:, u], in_values=now[:], imm_value=0.0))
                step.mark(v.tensor_copy(part16[:, u], part_i[:, u]))
                step.done(v.tensor_copy(tile_f[:, u], tile_i[:, u]))

            def one_hots(u):
                v.tensor_tensor(LO16[:, u], iota16[:].unsqueeze(1).to_broadcast([P, CH // 2, P, 2]),
                                part16[:, u].rearrange("p (a b) -> p a b", b=2).unsqueeze(2)
                                .to_broadcast([P, CH // 2, P, 2]), ALU.is_equal).then_inc(s_hot[u], 1)
                return v.tensor_tensor(HI[:, u], marks_now[:].unsqueeze(1).to_broadcast([P, CH, WT]),
                                       spread(tile_f[:, u], WT), ALU.is_equal)

            link = Steps(dve, s_set)
            link.mark(v.tensor_copy(a_dst_now[:], node[:, bass.ds(w * WT, WT), W:W + NH].rearrange("p t h -> p h t")))
            link.mark(v.tensor_copy(marks_now[:], tile_marks[:, bass.ds(w * WT, WT)]))
            link.done(v.tensor_copy(now[:], split[:, bass.ds(w, 1), :].rearrange("p a i -> p (a i)")))
            select(link, 0)
            link.done(one_hots(0))
            select(link, 1)
            turns = dve.value_load(cells, min_val=2, max_val=MOST_TURNS)
            with dve.Fori(1, turns) as j:
                step = Steps(dve, s_loop, j * STEPS)
                for u in range(2):
                    nj, nu = after(j, u)
                    dve.wait_ge(s_a[u], j + 1)
                    step.done(v.tensor_tensor(choice[:, u], psA[:, u, :].rearrange("p (i h t) -> p i h t", h=NH, t=WT),
                                              HI[:, u].unsqueeze(2).to_broadcast([P, CH, NH, WT]), ALU.mult))
                    step.done(v.tensor_reduce(a_dst_e[:, u], choice[:, u], AX, ALU.add))
                    step.mark(v.tensor_tensor(z[:, u, 1], a_dst_e[:, u], bound[:].unsqueeze(1).to_broadcast([P, CH, NH]), ALU.add))
                    dve.wait_ge(s_rows[u], j * (16 * CH))
                    step.done(v.tensor_tensor(z[:, u, 0], rows[:, u, :, HEAD_COLS:W], a_dst_e[:, u], ALU.add))
                    step.done(v.scalar_tensor_tensor(z[:, u], z[:, u], 0.2, z[:, u], ALU.mult, ALU.max))
                    v.tensor_tensor(zd[:, u], z[:, u, 0], z[:, u, 1], ALU.subtract).then_inc(s_z[u], 1)
                    dve.wait_ge(s_turned[nu], nj)
                    dve.wait_ge(s_lo[nu], nj)
                    step.mark(one_hots(nu))
                    dve.wait_ge(s_w[u], j + 1)
                    v.tensor_tensor(val[:, u, :, 0:HEAD_COLS].rearrange("p i (h e) -> p i h e", h=NH),
                                    rows[:, u, :, 0:HEAD_COLS].rearrange("p i (h e) -> p i h e", h=NH),
                                    val[:, u, :, HEAD_COLS:W].unsqueeze(3).to_broadcast([P, CH, NH, GAT_EXPERTS]),
                                    ALU.mult).then_inc(s_val[u], 1)
                    dve.wait_ge(s_val[u], j + 1)
                    dve.wait_ge(s_loop, step.base + step.n)
                    dve.wait_ge(s_used[u], j)
                    v.tensor_tensor(spreadv[:, u], val[:, u].unsqueeze(3).to_broadcast([P, CH, W, WT]),
                                    HI[:, u].unsqueeze(2).to_broadcast([P, CH, W, WT]), ALU.mult).then_inc(s_spread[u], 1)
                    select(step, u)
                assert step.n == STEPS, step.n
            dve.wait_ge(s_turned[1], turns)
            dve.wait_ge(s_lo[1], turns)
            one_hots(1)
            dve.wait_ge(s_sum, 1)
            v.tensor_tensor(sums[:, bass.ds(w, 1)], sums[:, bass.ds(w, 1)],
                            acc[:, 0:W * WT].rearrange("p (o f t) -> p o f t", o=1, f=W), ALU.add)


def gat_stage(nc, k, X, xnT, A, keys, picked, best, rounds_of, far_count, cell, parts):
    NH, W = GAT_HEADS, FEATURES
    with ExitStack() as ctx:
        sp = Space(nc, ctx, "gat")
        w_node = sp.sb("w_node", [C, W + NH])
        node = sp.sb("node", [P, TILES, W + NH])
        with ExitStack() as ctx2:
            s2 = Space(nc, ctx2, "gat_set")
            WgT, att = s2.sb("WgT", [HEAD_COLS, C]), s2.sb("att", [HEAD_COLS, 2 * NH])
            psW = s2.ps("psW", [C, 512])
            s_load, s_zero, s_w = (s2.sem(n) for n in ("load", "zero", "w"))
            with nc.Block() as block:
                @block.sync
                def _(eng):
                    eng.dma_start(WgT[:], A["W_gatT"]).then_inc(s_load, 16)
                    eng.dma_start(w_node[:, 0:HEAD_COLS], A["W_gat"]).then_inc(s_load, 16)
                    eng.wait_ge(s_zero, 1)
                    for i, name in enumerate(("att_src", "att_dst")):
                        for h in range(NH):
                            eng.dma_start(att[h * NH:(h + 1) * NH, i * NH + h:i * NH + h + 1],
                                          A[name][h].unsqueeze(1)).then_inc(s_load, 16)

                @block.tensor
                def _(pe):
                    pe.wait_ge(s_load, 16 * (2 + 2 * NH))
                    nc.tensor.matmul(psW[:, 0:2 * NH], WgT[:], att[:], start=True, stop=True).then_inc(s_w, 1)

                @block.vector
                def _(dve):
                    nc.vector.memset(att[:], 0.0).then_inc(s_zero, 1)
                    dve.wait_ge(s_w, 1)
                    nc.vector.tensor_copy(w_node[:, HEAD_COLS:], psW[:, 0:2 * NH])
        normalise(nc, "gat_ln", k, X, xnT, w_node[:], node, W + NH)

        src_table = nc.dram_tensor("src_table", [SRC_NODES, W], F32, kind="Internal").ap()
        src_rows = sp.sb("src_rows", [P, TILES, W])
        most, bound = sp.sb("most", [P, NH]), sp.sb("bound", [P, NH])
        last_row = sp.sb("last_row", [P, W])
        floor = sp.sb("floor", [P, TILES, NH])
        sums = sp.sb("sums", [P, WINDOWS, W, WT])
        iota_i, window_i = sp.sb("iota_i", [P, P, 2], I32), sp.sb("window_i", [P, TILES], I32)
        iota16, tile_marks = sp.sb("iota16", [P, P, 2], BF16), sp.sb("tile_marks", [P, TILES])
        zeros = sp.sb("zeros", [P, W * WT])
        s_table, s_last = sp.sem("table"), sp.sem("last")
        with ExitStack() as ctx2:
            s2 = Space(nc, ctx2, "gat_table")
            s_packed, s_most, s_iota = (s2.sem(n) for n in ("packed", "most", "iota"))
            with nc.Block() as block:
                @block.sync
                def _(eng):
                    eng.wait_ge(s_packed, 1)
                    eng.dma_start(src_table.rearrange("(b p c) f -> p b c f", p=P, c=GT),
                                  src_rows[:].rearrange("p (b c) f -> p b c f", c=GT)).then_inc(s_table, 16)
                    eng.wait_ge(s_table, 16)
                    eng.dma_start(last_row[:], src_table[LAST_NODE:LAST_NODE + 1, :].to_broadcast([P, W])).then_inc(s_last, 16)

                @block.gpsimd
                def _(pool):
                    pool.iota(iota_i[:], [[1, P], [0, 2]], base=0, channel_multiplier=0).then_inc(s_iota, 1)
                    pool.iota(window_i[:], [[1, TILES]], base=MARKED, channel_multiplier=0).then_inc(s_iota, 1)
                    pool.wait_ge(s_most, 1)
                    pool.partition_all_reduce(bound[:], most[:], P, bass.bass_isa.ReduceOp.max)

                @block.vector
                def _(dve):
                    v = nc.vector
                    v.tensor_copy(src_rows[:], node[:, :, 0:W]).then_inc(s_packed, 1)
                    v.tensor_reduce(most[:], node[:, :, HEAD_COLS:W].rearrange("p t h -> p h t"), AX, ALU.max).then_inc(s_most, 1)
                    v.memset(zeros[:], 0.0)
                    v.memset(sums[:], 0.0)
                    dve.wait_ge(s_iota, 2)
                    v.tensor_copy(iota16[:], iota_i[:])
                    v.tensor_copy(tile_marks[:], window_i[:])

        split = sp.sb("split", [P, WINDOWS, PICKED])
        there = sp.sb("there", [P, WINDOWS, PICKED])
        count, fullest = sp.sb("count", [P, WINDOWS]), sp.sb("fullest", [P, WINDOWS])
        turns_f = sp.sb("turns_f", [P, WINDOWS])
        turns_i, turns_of = sp.sb("turns_i", [P, WINDOWS], I32), sp.sb("turns_of", [P, WINDOWS], I32)
        now = sp.sb("now", [P, PICKED])
        a_dst_now, marks_now = sp.sb("a_dst_now", [P, NH, WT]), sp.sb("marks_now", [P, WT])
        top8 = sp.sb("top8", [P, 2, CH])
        sidx, part_i, tile_i = (sp.sb(n, [P, 2, CH], I32) for n in ("sidx", "part_i", "tile_i"))
        part16, tile_f = sp.sb("part16", [P, 2, CH], BF16), sp.sb("tile_f", [P, 2, CH])
        rows = sp.sb("rows", [P, 2, CH, W])
        LO16 = sp.sb("LO16", [P, 2, CH // 2, P, 2], BF16)
        LO, LOT = sp.sb("LO", [P, 2, CH, P]), sp.sb("LOT", [P, 2, CH, P])
        HI = sp.sb("HI", [P, 2, CH, WT])
        choice = sp.sb("choice", [P, 2, CH, NH, WT])
        a_dst_e = sp.sb("a_dst_e", [P, 2, CH, NH])
        z = sp.sb("z", [P, 2, 2, CH, NH])
        zd = sp.sb("zd", [P, 2, CH, NH])
        val = sp.sb("val", [P, 2, CH, W])
        spreadv = sp.sb("spreadv", [P, 2, CH, W, WT])
        tick = sp.sb("tick", [P, 2])
        with ExitStack() as ctx2:
            s2 = Space(nc, ctx2, "gat_edges")
            acc = s2.ps("acc", [P, 512])
            psA = s2.ps("psA", [P, 2, 512])
            psT = [s2.ps(f"psT{u}", [P, 512]) for u in range(2)]
            psT16 = [p[:].bitcast(BF16).rearrange("p (i e) -> p i e", i=CH) for p in psT]
            passes = nc.values_load(cell[0:1, 0:1], min_val=1, max_val=MAX_PASSES)
            with nc.Fori(0, passes) as this:
                split_keys(nc, picked, split, there, count, fullest, turns_f, turns_i, turns_of)
                with nc.Fori(0, WINDOWS) as w:
                    with ExitStack() as ctx3:
                        edge_window(nc, Space(nc, ctx3, "gat_window"), w, {**locals(), "ident16": k["ident16"], "ones": k["ones"]})
                pick_keys(nc, keys, picked, best, rounds_of[0:1, bass.ds(this, 1)])

        def rows3(ap, n=TILES):
            return ap.unsqueeze(1).to_broadcast([P, n, ap.shape[-1]])
        own, far, lead = (sp.sb(n, [P, TILES, NH]) for n in ("own", "far", "lead"))
        eown, efar = sp.sb("eown", [P, TILES, NH]), sp.sb("efar", [P, TILES, NH])
        by_node = sp.sb("by_node", [P, TILES, W])
        agg, tmp = sp.sb("agg", [P, TILES, HEAD_COLS]), sp.sb("tmp", [P, TILES, HEAD_COLS])
        dens = sp.sb("dens", [P, TILES, NH])
        b_gat, gamma, beta = (sp.sb(n, [P, HEAD_COLS]) for n in ("b_gat", "gamma", "beta"))
        m64, v64, r64, half = (sp.sb(n, [P, TILES]) for n in ("m64", "v64", "r64", "half"))
        scores = sp.sb("scores", [P, TILES, GAT_EXPERTS])
        f_load, f_z, f_e, f_var, f_r, f_link = (sp.sem(n) for n in ("f_load", "f_z", "f_e", "f_var", "f_r", "f_link"))
        with nc.Block() as block:
            @block.sync
            def _(eng):
                eng.wait_ge(s_last, 16)
                for dst, name in ((b_gat, "b_gat"), (gamma, "ln_gamma"), (beta, "ln_beta")):
                    eng.dma_start(dst[:], A[name].unsqueeze(0).to_broadcast([P, HEAD_COLS])).then_inc(f_load, 16)

            @block.scalar
            def _(act):
                act.wait_ge(f_z, 1)
                nc.scalar.activation(eown[:], own[:], ACT.Exp)
                nc.scalar.activation(efar[:], far[:], ACT.Exp).then_inc(f_e, 1)

            @block.gpsimd
            def _(pool):
                pool.memset(half[:], -0.5).then_inc(f_r, 1)
                pool.wait_ge(f_r, 1)
                pool.wait_ge(f_var, 1)
                pool.tensor_tensor(r64[:], v64[:], half[:], ALU.pow).then_inc(f_r, 1)

            @block.vector
            def _(dve):
                v = nc.vector
                L = Steps(dve, f_link)
                do = L.done
                a_src, a_dst = node[:, :, HEAD_COLS:W], node[:, :, W:W + NH]
                dve.wait_ge(s_last, 16)
                dve.wait_ge(f_load, 48)
                do(v.tensor_copy(by_node[:].rearrange("p (w t) f -> p w t f", w=WINDOWS), sums[:].rearrange("p w f t -> p w t f")))
                do(v.tensor_tensor(lead[:], a_dst, rows3(bound[:]), ALU.add))
                do(v.scalar_tensor_tensor(floor[:], lead[:], 0.2, lead[:], ALU.mult, ALU.max))
                do(v.tensor_tensor(own[:], a_src, a_dst, ALU.add))
                do(v.scalar_tensor_tensor(lead[:], own[:], 0.2, own[:], ALU.mult, ALU.max))
                do(v.tensor_tensor(own[:], lead[:], floor[:], ALU.subtract))
                do(v.tensor_tensor(far[:], a_dst, rows3(last_row[:, HEAD_COLS:W]), ALU.add))
                do(v.scalar_tensor_tensor(lead[:], far[:], 0.2, far[:], ALU.mult, ALU.max))
                v.tensor_tensor(far[:], lead[:], floor[:], ALU.subtract).then_inc(f_z, 1)
                dve.wait_ge(f_e, 1)
                do(v.tensor_tensor(efar[:], efar[:], spread(far_count[:], NH), ALU.mult))
                do(v.tensor_tensor(dens[:], eown[:], efar[:], ALU.add))
                do(v.tensor_tensor(dens[:], dens[:], by_node[:, :, HEAD_COLS:W], ALU.add))
                do(v.tensor_scalar(dens[:], dens[:], 1e-37, None, ALU.max))
                do(v.reciprocal(dens[:], dens[:]))
                for h in range(NH):
                    c = slice(h * NH, (h + 1) * NH)
                    L.mark(v.tensor_tensor(agg[:, :, c], node[:, :, c], spread(eown[:, :, h], NH), ALU.mult))
                    L.mark(v.tensor_tensor(tmp[:, :, c], rows3(last_row[:, c]), spread(efar[:, :, h], NH), ALU.mult))
                dve.wait_ge(f_link, L.n)
                do(v.tensor_tensor(agg[:], agg[:], tmp[:], ALU.add))
                do(v.tensor_tensor(agg[:], agg[:], by_node[:, :, 0:HEAD_COLS], ALU.add))
                for h in range(NH):
                    c = slice(h * NH, (h + 1) * NH)
                    L.mark(v.tensor_tensor(tmp[:, :, c], agg[:, :, c], spread(dens[:, :, h], NH), ALU.mult))
                dve.wait_ge(f_link, L.n)
                do(v.tensor_tensor(agg[:], tmp[:], rows3(b_gat[:]), ALU.add))
                do(v.tensor_reduce(m64[:], agg[:], AX, ALU.add))
                do(v.tensor_scalar(m64[:], m64[:], 1.0 / HEAD_COLS, None, ALU.mult))
                do(v.tensor_tensor(agg[:], agg[:], spread(m64[:], HEAD_COLS), ALU.subtract))
                do(v.tensor_tensor(tmp[:], agg[:], agg[:], ALU.mult))
                do(v.tensor_reduce(m64[:], tmp[:], AX, ALU.add))
                v.tensor_scalar(v64[:], m64[:], 1.0 / HEAD_COLS, LN_EPS, ALU.mult, ALU.add).then_inc(f_var, 1)
                dve.wait_ge(f_r, 2)
                do(v.tensor_tensor(agg[:], agg[:], spread(r64[:], HEAD_COLS), ALU.mult))
                do(v.tensor_tensor(agg[:], agg[:], rows3(gamma[:]), ALU.mult))
                do(v.tensor_tensor(agg[:], agg[:], rows3(beta[:]), ALU.add))
                do(v.tensor_reduce(scores[:], agg[:].rearrange("p t (h e) -> p t e h", h=NH), AX, ALU.add))
                do(v.tensor_scalar(scores[:], scores[:], 1.0 / NH, None, ALU.mult))
        gates_of(nc, "gat_gate", scores[:], GAT_EXPERTS, 0.0, parts)


def second_ffn_stage(nc, k, X, xnT, A, parts):
    E, hid = GAT_EXPERTS, 2 * C
    cuts = [(0, P), (P, P)]
    with ExitStack() as ctx:
        sp = Space(nc, ctx, "ffn")
        w1 = sp.sb("w1", [P, E * hid])
        w2 = sp.sb("w2", [P, E * len(cuts), C])
        b1 = sp.sb("b1", [P, E * len(cuts)])
        b2, rest = sp.sb("b2", [3 * E, C]), sp.sb("rest", [3 * E, 2, C])
        b2_parts = sp.sb("b2_parts", [3 * E, 3, C], BF16)
        load_now(nc, "ffn_b2", [(b2[part * E:(part + 1) * E, :], A["b2"]) for part in range(3)])
        s_split = sp.sem("split")
        with nc.Block() as block:
            @block.vector
            def _(dve):
                v = nc.vector
                link = Steps(dve, s_split)
                link.done(v.tensor_copy(b2_parts[:, 0, :], b2[:]))
                link.done(v.tensor_tensor(rest[:, 0, :], b2[:], b2_parts[:, 0, :], ALU.subtract))
                link.done(v.tensor_copy(b2_parts[:, 1, :], rest[:, 0, :]))
                link.done(v.tensor_tensor(rest[:, 1, :], rest[:, 0, :], b2_parts[:, 1, :], ALU.subtract))
                v.tensor_copy(b2_parts[:, 2, :], rest[:, 1, :])
        pairs = [(w1[:].rearrange("c (e h) -> c e h", e=E), A["W1"].rearrange("e c h -> c e h")),
                 (w2[:], A["W2"].rearrange("e (k p) c -> p (e k) c", p=P)),
                 (b1[:], A["b1"])]
        experts(nc, "ffn_mix", k, X, xnT, parts, E, cuts, w1, w2, Loads(pairs),
                (ACT.Gelu, lambda i: b1[:, i:i + 1]), b2=b2_parts)


def program(nc, A, out):
    rows = lambda ap: ap.rearrange("(b p c) d -> p b c d", p=P, c=GT)
    with ExitStack() as ctx:
        k = constants(nc, ctx)
        sp = Space(nc, ctx, "all")
        X = sp.sb("X", [P, TILES, C])
        x4 = X[:].rearrange("p (b c) d -> p b c d", c=GT)
        s_x = sp.sem("x_in")
        edge_attention_stage(nc, k, X, A, x4, rows(A["x"]), s_x)
        xnT = sp.sb("xnT", [C, TOKENS])
        parts = sp.sb("gate_parts", [P, TILES, 3, GAT_EXPERTS], BF16)
        with ExitStack() as ctx2:
            s2 = Space(nc, ctx2, "graph")
            keys, far_count, cell = s2.sb("keys", [P, LANE]), s2.sb("far_count", [P, TILES]), s2.sb("cell", [P, 1], I32)
            rounds_of = s2.sb("rounds_of", [P, MAX_PASSES], I32)
            with ExitStack() as ctx3:
                s3 = Space(nc, ctx3, "targets")
                lo16, hi16 = s3.sb("lo16", [P, LANE], BF16), s3.sb("hi16", [P, LANE], BF16)
                iota16, iota1_16 = s3.sb("iota16", [P, P, 2], BF16), s3.sb("iota1_16", [P, TILES, 2], BF16)
                x_sorted = nc.dram_tensor("x_sorted", [SORTED * NODES, C], F32, kind="Internal").ap()
                y_sorted = nc.dram_tensor("y_sorted", [SORTED * NODES, C], F32, kind="Internal").ap()
                s_empty = s3.sem("empty")
                tally = Tally(nc, Space(nc, ctx3, "tally"), lo16, hi16, iota16, iota1_16, far_count)
                edge_keys_stage(nc, k, A, keys, lo16, hi16, iota16, iota1_16, cell, rounds_of, xnT, tally, x_sorted, y_sorted, s_empty)
                moe_stage(nc, k, X, xnT[:].rearrange("p (t c) -> p t c", c=C), A, tally, x_sorted, y_sorted, s_empty)
            picked, best = s2.sb("picked", [P, SEGMENTS, TAKEN]), s2.sb("best", [P, SEGMENTS, CH])
            dense_attention_stage(nc, k, X, xnT, A, keys, picked, best)
            gat_stage(nc, k, X, xnT, A, keys, picked, best, rounds_of, far_count, cell, parts)
        second_ffn_stage(nc, k, X, xnT, A, parts)
        load_now(nc, "x_out", [(rows(out), x4)])


def kernel(**inputs):
    import concourse.bacc as bacc
    from concourse.bass_utils import run_bass_kernel_spmd

    def plain(name):
        return np.ascontiguousarray(inputs[name])

    def turned(name, *order):
        return np.ascontiguousarray(np.transpose(inputs[name], order))

    arrays = {
        "x": plain("x").reshape(TOKENS, C), "adj": plain("adj"),
        "W_linT": turned("L0_gnn_W_lin", 1, 0), "W_valT": turned("L0_gnn_W_val", 1, 0),
        "W_outT": turned("L0_gnn_W_out", 1, 0), "a": plain("L0_gnn_a"),
        "src": plain("L0_gnn_src"), "dst": plain("L0_gnn_dst"),
        "router_wT": turned("L0_ffn_router_w", 1, 0),
        "w13T": np.concatenate([turned("L0_ffn_w1", 0, 2, 1), turned("L0_ffn_w3", 0, 2, 1)], axis=2),
        "w2T": turned("L0_ffn_w2", 0, 2, 1),
        **{n: plain("L1_gnn_" + n) for n in ("Wq", "Wk", "Wo", "bq", "bk", "bv", "bo")},
        "WvT": turned("L1_gnn_Wv", 1, 0),
        "alpha": plain("L1_gnn_alpha").reshape(1), "gamma": plain("L1_gnn_gamma").reshape(1),
        "W_gat": plain("L1_ffn_W_gat"), "W_gatT": turned("L1_ffn_W_gat", 1, 0),
        **{n: plain("L1_ffn_" + n) for n in ("att_src", "att_dst", "b_gat", "ln_gamma", "ln_beta", "W1", "W2", "b2", "edge_index")},
        "b1": np.ascontiguousarray(np.transpose(np.reshape(inputs["L1_ffn_b1"], (-1, P)))),
    }
    nc = bacc.Bacc("TRN2", target_bir_lowering=False, num_devices=1)
    A = {n: nc.dram_tensor(f"in_{n}", a.shape, mybir.dt.from_np(a.dtype), kind="ExternalInput").ap()
         for n, a in arrays.items()}
    out = nc.dram_tensor("out_x", (TOKENS, C), F32, kind="ExternalOutput").ap()
    program(nc, A, out)
    r = run_bass_kernel_spmd(nc, [{f"in_{n}": a for n, a in arrays.items()}], core_ids=[0])
    return r.results[0]["out_x"].reshape(BATCH, NODES, C)
```
